# Optimizing a Trainium2 kernel written in Bass

```python
import numpy as np
import jax
import jax.numpy as jnp

def _softmax(x, axis=-1):
    return jax.nn.softmax(x, axis=axis)

def _gelu(x):
    return jax.nn.gelu(x, approximate=True)

def _silu(x):
    return jax.nn.silu(x)

def _sigmoid(x):
    return jax.nn.sigmoid(x)

def _layernorm(x, axis=-1, eps=1e-05):
    m = jnp.mean(x, axis=axis, keepdims=True)
    v = jnp.var(x, axis=axis, keepdims=True)
    return (x - m) / jnp.sqrt(v + eps)

def _scatter_add(tgt, idx, src, axis=0):
    return tgt.at[idx].add(src)

def _segment_sum(src, seg, n):
    return jax.ops.segment_sum(src, seg, n)
kernel_name = 'mk_gnn_preln_d4_gnn_r32_403690'

def setup_inputs(seed: int=0):
    np.random.seed(seed)
    _w = jnp.asarray

    def _rec_inputs():
        import jax
        import jax.numpy as jnp
        _gk = jax.random.key(seed)
        x = -0.0007083 + 1.001 * jax.random.normal(jax.random.fold_in(_gk, 1), (3125, 48), jnp.float32)
        _s = jax.random.randint(jax.random.fold_in(_gk, 2), (25000,), 0, 3125, jnp.int32)
        _d = jax.random.randint(jax.random.fold_in(_gk, 3), (25000,), 0, 3125, jnp.int32)
        _loop = jnp.arange(3125, dtype=jnp.int32)
        src = jnp.concatenate([_s, _d, _loop])
        dst = jnp.concatenate([_d, _s, _loop])
        _o = jnp.argsort(dst, stable=True)
        src = src[_o]
        dst = dst[_o]
        edge_attr_40 = jax.random.uniform(jax.random.fold_in(_gk, 13), (53125, 40), jnp.float32, 0.0, 1)
        edge_weight = jax.random.uniform(jax.random.fold_in(_gk, 15), (53125,), jnp.float32, 0.0, 6.99999)
        node_type_119 = jax.random.randint(jax.random.fold_in(_gk, 16), (3125,), 0, 119, jnp.int32)
        node_vec = jax.random.uniform(jax.random.fold_in(_gk, 17), (3125,), jnp.float32, 0.0, 1.49999)
        return (x, src, dst, edge_attr_40, edge_weight, node_type_119, node_vec)
    x, src, dst, edge_attr_40, edge_weight, node_type_119, node_vec = _rec_inputs()

    def _L0_gnn_setup():
        import math
        import jax, jax.numpy as jnp
        import numpy as np
        N, E, C, T = (50000, 25000, 48, 128)
        C3, C9 = (C * 3, C * 9)
        EPS = 1e-05

        def sinusoidal_emb(t, dim):
            half = dim // 2
            freqs = jnp.exp(jnp.arange(half, dtype=jnp.float32) * (-math.log(10000.0) / (half - 1)))
            ang = t[:, None] * freqs[None, :]
            return jnp.concatenate([jnp.sin(ang), jnp.cos(ang)], axis=-1)

        def gcn_conv(x, W, b, src, dst, n):
            h = x @ W
            loop = jnp.arange(n, dtype=src.dtype)
            s = jnp.concatenate([src, loop])
            d = jnp.concatenate([dst, loop])
            deg = jax.ops.segment_sum(jnp.ones_like(d, dtype=h.dtype), d, num_segments=n)
            dinv = jnp.where(deg > 0, jax.lax.rsqrt(deg), 0.0)
            norm = dinv[s] * dinv[d]
            out = jax.ops.segment_sum(h[s] * norm[:, None], d, num_segments=n)
            return out + b

        def batchnorm(x, g, b):
            mean = jnp.mean(x, axis=0)
            var = jnp.mean(jnp.square(x - mean), axis=0)
            return g * (x - mean) * jax.lax.rsqrt(var + EPS) + b
        key = jax.random.key(seed)
        ks = jax.random.split(key, 12)
        rn = lambda k, sh: jax.random.normal(k, sh, jnp.float32) * 0.05
        return {'x': jax.random.normal(ks[0], (N, C), jnp.float32), 'edge_index': jax.random.randint(ks[1], (2, E), 0, N, dtype=jnp.int32), 'timestep': jax.random.randint(ks[2], (1,), 0, 1000).astype(jnp.float32), 'Wtm': rn(ks[3], (T, T)), 'btm': jnp.zeros((T,), jnp.float32), 'W_in': rn(ks[4], (C, C3)), 'b_in': jnp.zeros((C3,), jnp.float32), 'g_in': jnp.ones((C3,), jnp.float32), 'be_in': jnp.zeros((C3,), jnp.float32), 'Wt1': rn(ks[5], (T, C9)), 'bt1': jnp.zeros((C9,), jnp.float32), 'Wc1': rn(ks[6], (C3, C9)), 'bc1': jnp.zeros((C9,), jnp.float32), 'g1': jnp.ones((C9,), jnp.float32), 'be1': jnp.zeros((C9,), jnp.float32), 'Wt2': rn(ks[7], (T, C3)), 'bt2': jnp.zeros((C3,), jnp.float32), 'Wc2': rn(ks[8], (C9, C3)), 'bc2': jnp.zeros((C3,), jnp.float32), 'g2': jnp.ones((C3,), jnp.float32), 'be2': jnp.zeros((C3,), jnp.float32), 'W_out': rn(ks[9], (C3, C)), 'b_out': jnp.zeros((C,), jnp.float32), 'g_out': jnp.ones((C,), jnp.float32), 'be_out': jnp.zeros((C,), jnp.float32)}
    _L0_gnn_all = _L0_gnn_setup()
    _L0_gnn_in = {k: v for k, v in _L0_gnn_all.items() if k in ('timestep', 'Wtm', 'btm', 'W_in', 'b_in', 'g_in', 'be_in', 'Wt1', 'bt1', 'Wc1', 'bc1', 'g1', 'be1', 'Wt2', 'bt2', 'Wc2', 'bc2', 'g2', 'be2', 'W_out', 'b_out', 'g_out', 'be_out')}
    del _L0_gnn_all

    def _L1_gnn_setup():
        import jax, jax.numpy as jnp
        import numpy as np
        N_NODES = 3125
        N_EDGES = 50000
        IN_F = 48
        HID_F = 48
        OUT_F = 48

        def _sage_mean(x, src, dst, W_self, W_neigh, b, n_nodes):
            deg = jax.ops.segment_sum(jnp.ones((src.shape[0],), x.dtype), dst, num_segments=n_nodes)
            agg = jax.ops.segment_sum(x[src], dst, num_segments=n_nodes)
            h_neigh = agg / jnp.maximum(deg, 1.0)[:, None]
            return x @ W_self + h_neigh @ W_neigh + b
        key = jax.random.key(seed)
        ks = jax.random.split(key, 9)
        features = jax.random.normal(ks[0], (N_NODES, IN_F), dtype=jnp.float32)
        src = jax.random.randint(ks[1], (N_EDGES,), 0, N_NODES)
        dst = jax.random.randint(ks[2], (N_EDGES,), 0, N_NODES)
        s_in = 1.0 / np.sqrt(IN_F)
        s_hid = 1.0 / np.sqrt(HID_F)
        return {'features': features, 'src': src, 'dst': dst, 'W_self1': jax.random.normal(ks[3], (IN_F, HID_F), jnp.float32) * s_in, 'W_neigh1': jax.random.normal(ks[4], (IN_F, HID_F), jnp.float32) * s_in, 'b1': jnp.zeros((HID_F,), jnp.float32), 'W_self2': jax.random.normal(ks[5], (HID_F, OUT_F), jnp.float32) * s_hid, 'W_neigh2': jax.random.normal(ks[6], (HID_F, OUT_F), jnp.float32) * s_hid, 'b2': jnp.zeros((OUT_F,), jnp.float32)}
    _L1_gnn_all = _L1_gnn_setup()
    _L1_gnn_in = {k: v for k, v in _L1_gnn_all.items() if k in ('W_self1', 'W_neigh1', 'b1', 'W_self2', 'W_neigh2', 'b2')}
    del _L1_gnn_all

    def _L2_gnn_setup():
        import jax, jax.numpy as jnp
        import numpy as np
        N_NODES = 3125
        N_EDGES = 50000
        D_FEAT = 48
        N_LAYERS = 2
        key = jax.random.key(seed)
        k1, k2, k3 = jax.random.split(key, 3)
        row = jax.random.randint(k1, (N_EDGES,), 0, N_NODES, dtype=jnp.int32)
        col = jax.random.randint(k2, (N_EDGES,), 0, N_NODES, dtype=jnp.int32)
        x = jax.random.normal(k3, (N_NODES, D_FEAT), dtype=jnp.float32)
        return {'row': row, 'col': col, 'x': x}
    _L2_gnn_all = _L2_gnn_setup()
    _L2_gnn_in = {k: v for k, v in _L2_gnn_all.items() if k in ()}
    del _L2_gnn_all

    def _L3_gnn_setup():
        import jax, jax.numpy as jnp
        import numpy as np
        CUTOFF = 6.0
        LN_EPS = 1e-05
        key = jax.random.key(seed)
        ks = jax.random.split(key, 16)
        N, E, H, R, NEL, G = (50000, 25000, 48, 40, 119, 32)
        inp = {'h': jax.random.normal(ks[0], (N, H), jnp.float32), 'edge_index': jax.random.randint(ks[1], (2, E), 0, N, jnp.int64), 'edge_attr': jax.random.uniform(ks[2], (E, R), jnp.float32), 'distances': jax.random.uniform(ks[3], (E,), jnp.float32) * 7.0, 'atom_z': jax.random.randint(ks[4], (N,), 0, NEL, jnp.int64), 'node_mult': jax.random.uniform(ks[5], (N,), jnp.float32) + 0.5, 'batch': jnp.zeros((N,), jnp.int64), 'W1': jax.random.normal(ks[6], (H, R), jnp.float32) / np.sqrt(R), 'b1': jax.random.normal(ks[7], (H,), jnp.float32) * 0.01, 'W2': jax.random.normal(ks[8], (H, H), jnp.float32) / np.sqrt(H), 'b2': jax.random.normal(ks[9], (H,), jnp.float32) * 0.01, 'emb': jax.random.normal(ks[10], (NEL, G), jnp.float32) * 0.01, 'adaptW': jax.random.normal(ks[11], (G, G), jnp.float32) * 0.01, 'gamma': jnp.ones((H,), jnp.float32), 'beta': jnp.zeros((H,), jnp.float32)}
        return inp
    _L3_gnn_all = _L3_gnn_setup()
    _L3_gnn_in = {k: v for k, v in _L3_gnn_all.items() if k in ('W1', 'b1', 'W2', 'b2', 'emb', 'adaptW', 'gamma', 'beta')}
    del _L3_gnn_all
    return {'x': x, 'src': src, 'dst': dst, 'edge_attr_40': edge_attr_40, 'edge_weight': edge_weight, 'node_type_119': node_type_119, 'node_vec': node_vec, 'L0_gnn_timestep': _L0_gnn_in['timestep'], 'L0_gnn_Wtm': _L0_gnn_in['Wtm'], 'L0_gnn_btm': _L0_gnn_in['btm'], 'L0_gnn_W_in': _L0_gnn_in['W_in'], 'L0_gnn_b_in': _L0_gnn_in['b_in'], 'L0_gnn_g_in': _L0_gnn_in['g_in'], 'L0_gnn_be_in': _L0_gnn_in['be_in'], 'L0_gnn_Wt1': _L0_gnn_in['Wt1'], 'L0_gnn_bt1': _L0_gnn_in['bt1'], 'L0_gnn_Wc1': _L0_gnn_in['Wc1'], 'L0_gnn_bc1': _L0_gnn_in['bc1'], 'L0_gnn_g1': _L0_gnn_in['g1'], 'L0_gnn_be1': _L0_gnn_in['be1'], 'L0_gnn_Wt2': _L0_gnn_in['Wt2'], 'L0_gnn_bt2': _L0_gnn_in['bt2'], 'L0_gnn_Wc2': _L0_gnn_in['Wc2'], 'L0_gnn_bc2': _L0_gnn_in['bc2'], 'L0_gnn_g2': _L0_gnn_in['g2'], 'L0_gnn_be2': _L0_gnn_in['be2'], 'L0_gnn_W_out': _L0_gnn_in['W_out'], 'L0_gnn_b_out': _L0_gnn_in['b_out'], 'L0_gnn_g_out': _L0_gnn_in['g_out'], 'L0_gnn_be_out': _L0_gnn_in['be_out'], 'L1_gnn_W_self1': _L1_gnn_in['W_self1'], 'L1_gnn_W_neigh1': _L1_gnn_in['W_neigh1'], 'L1_gnn_b1': _L1_gnn_in['b1'], 'L1_gnn_W_self2': _L1_gnn_in['W_self2'], 'L1_gnn_W_neigh2': _L1_gnn_in['W_neigh2'], 'L1_gnn_b2': _L1_gnn_in['b2'], 'L3_gnn_W1': _L3_gnn_in['W1'], 'L3_gnn_b1': _L3_gnn_in['b1'], 'L3_gnn_W2': _L3_gnn_in['W2'], 'L3_gnn_b2': _L3_gnn_in['b2'], 'L3_gnn_emb': _L3_gnn_in['emb'], 'L3_gnn_adaptW': _L3_gnn_in['adaptW'], 'L3_gnn_gamma': _L3_gnn_in['gamma'], 'L3_gnn_beta': _L3_gnn_in['beta']}

def reference(x, src, dst, edge_attr_40, edge_weight, node_type_119, node_vec, L0_gnn_timestep, L0_gnn_Wtm, L0_gnn_btm, L0_gnn_W_in, L0_gnn_b_in, L0_gnn_g_in, L0_gnn_be_in, L0_gnn_Wt1, L0_gnn_bt1, L0_gnn_Wc1, L0_gnn_bc1, L0_gnn_g1, L0_gnn_be1, L0_gnn_Wt2, L0_gnn_bt2, L0_gnn_Wc2, L0_gnn_bc2, L0_gnn_g2, L0_gnn_be2, L0_gnn_W_out, L0_gnn_b_out, L0_gnn_g_out, L0_gnn_be_out, L1_gnn_W_self1, L1_gnn_W_neigh1, L1_gnn_b1, L1_gnn_W_self2, L1_gnn_W_neigh2, L1_gnn_b2, L3_gnn_W1, L3_gnn_b1, L3_gnn_W2, L3_gnn_b2, L3_gnn_emb, L3_gnn_adaptW, L3_gnn_gamma, L3_gnn_beta):
    import jax
    import jax.numpy as jnp

    def _L0_gnn_ref(x, edge_index, timestep, Wtm, btm, W_in, b_in, g_in, be_in, Wt1, bt1, Wc1, bc1, g1, be1, Wt2, bt2, Wc2, bc2, g2, be2, W_out, b_out, g_out, be_out):
        import math
        import jax, jax.numpy as jnp
        import numpy as np
        N, E, C, T = (50000, 25000, 48, 128)
        C3, C9 = (C * 3, C * 9)
        EPS = 1e-05

        def sinusoidal_emb(t, dim):
            half = dim // 2
            freqs = jnp.exp(jnp.arange(half, dtype=jnp.float32) * (-math.log(10000.0) / (half - 1)))
            ang = t[:, None] * freqs[None, :]
            return jnp.concatenate([jnp.sin(ang), jnp.cos(ang)], axis=-1)

        def gcn_conv(x, W, b, src, dst, n):
            h = x @ W
            loop = jnp.arange(n, dtype=src.dtype)
            s = jnp.concatenate([src, loop])
            d = jnp.concatenate([dst, loop])
            deg = jax.ops.segment_sum(jnp.ones_like(d, dtype=h.dtype), d, num_segments=n)
            dinv = jnp.where(deg > 0, jax.lax.rsqrt(deg), 0.0)
            norm = dinv[s] * dinv[d]
            out = jax.ops.segment_sum(h[s] * norm[:, None], d, num_segments=n)
            return out + b

        def batchnorm(x, g, b):
            mean = jnp.mean(x, axis=0)
            var = jnp.mean(jnp.square(x - mean), axis=0)
            return g * (x - mean) * jax.lax.rsqrt(var + EPS) + b
        src, dst = (edge_index[0], edge_index[1])
        n = x.shape[0]
        relu = jax.nn.relu
        t = relu(sinusoidal_emb(timestep, T) @ Wtm + btm)
        h = relu(batchnorm(gcn_conv(x, W_in, b_in, src, dst, n), g_in, be_in))
        te1 = relu(t @ Wt1 + bt1)
        h = batchnorm(relu(gcn_conv(h, Wc1, bc1, src, dst, n) + te1), g1, be1)
        te2 = relu(t @ Wt2 + bt2)
        h = batchnorm(relu(gcn_conv(h, Wc2, bc2, src, dst, n) + te2), g2, be2)
        return relu(batchnorm(gcn_conv(h, W_out, b_out, src, dst, n), g_out, be_out))

    def _L1_gnn_ref(features, src, dst, W_self1, W_neigh1, b1, W_self2, W_neigh2, b2):
        import jax, jax.numpy as jnp
        import numpy as np
        N_NODES = 3125
        N_EDGES = 50000
        IN_F = 48
        HID_F = 48
        OUT_F = 48

        def _sage_mean(x, src, dst, W_self, W_neigh, b, n_nodes):
            deg = jax.ops.segment_sum(jnp.ones((src.shape[0],), x.dtype), dst, num_segments=n_nodes)
            agg = jax.ops.segment_sum(x[src], dst, num_segments=n_nodes)
            h_neigh = agg / jnp.maximum(deg, 1.0)[:, None]
            return x @ W_self + h_neigh @ W_neigh + b
        n = features.shape[0]
        h = jax.nn.relu(_sage_mean(features, src, dst, W_self1, W_neigh1, b1, n))
        out = _sage_mean(h, src, dst, W_self2, W_neigh2, b2, n)
        return out

    def _L2_gnn_ref(row, col, x):
        import jax, jax.numpy as jnp
        import numpy as np
        N_NODES = 3125
        N_EDGES = 50000
        D_FEAT = 48
        N_LAYERS = 2
        n = x.shape[0]
        loop = jnp.arange(n, dtype=row.dtype)
        r = jnp.concatenate([row, loop])
        c = jnp.concatenate([col, loop])
        deg = jax.ops.segment_sum(jnp.ones(r.shape, dtype=x.dtype), r, num_segments=n)
        dinv = jnp.where(deg > 0, jax.lax.rsqrt(deg), 0.0)
        w = dinv[r] * dinv[c]
        for _ in range(N_LAYERS):
            x = jax.ops.segment_sum(w[:, None] * x[c], r, num_segments=n)
        return x

    def _L3_gnn_ref(h, edge_index, edge_attr, distances, atom_z, node_mult, batch, W1, b1, W2, b2, emb, adaptW, gamma, beta):
        import jax, jax.numpy as jnp
        import numpy as np
        CUTOFF = 6.0
        LN_EPS = 1e-05
        src, dst = (edge_index[0], edge_index[1])
        N = h.shape[0]
        gate = jax.nn.silu(edge_attr @ W1.T + b1) @ W2.T + b2
        ei = emb[atom_z[src]]
        ej = emb[atom_z[dst]]
        adapt_logit = jnp.sum(ei * (ej @ adaptW.T), axis=-1, keepdims=True)
        gate = gate + adapt_logit
        cw = jnp.where(distances < CUTOFF, 0.5 * (jnp.cos(jnp.pi * distances / CUTOFF) + 1.0), 0.0)
        mj = node_mult[dst]
        msg = gate * h[dst] * (cw * mj)[:, None]
        agg = jax.ops.segment_sum(msg, src, num_segments=N)
        tot = jax.ops.segment_sum(mj, src, num_segments=N)
        agg = agg / jnp.clip(tot, 1e-08, None)[:, None]
        x = h + agg
        mu = jnp.mean(x, axis=-1, keepdims=True)
        var = jnp.mean(jnp.square(x - mu), axis=-1, keepdims=True)
        return (x - mu) / jnp.sqrt(var + LN_EPS) * gamma + beta
    edge_index = jnp.stack([src, dst])
    batch0 = jnp.zeros((3125,), jnp.int32)
    h = jnp.maximum(_layernorm(x, axis=-1), 0.0)
    x = x + _L0_gnn_ref(h, edge_index, L0_gnn_timestep, L0_gnn_Wtm, L0_gnn_btm, L0_gnn_W_in, L0_gnn_b_in, L0_gnn_g_in, L0_gnn_be_in, L0_gnn_Wt1, L0_gnn_bt1, L0_gnn_Wc1, L0_gnn_bc1, L0_gnn_g1, L0_gnn_be1, L0_gnn_Wt2, L0_gnn_bt2, L0_gnn_Wc2, L0_gnn_bc2, L0_gnn_g2, L0_gnn_be2, L0_gnn_W_out, L0_gnn_b_out, L0_gnn_g_out, L0_gnn_be_out)
    h = jnp.maximum(_layernorm(x, axis=-1), 0.0)
    x = x + _L1_gnn_ref(h, src, dst, L1_gnn_W_self1, L1_gnn_W_neigh1, L1_gnn_b1, L1_gnn_W_self2, L1_gnn_W_neigh2, L1_gnn_b2)
    h = jnp.maximum(_layernorm(x, axis=-1), 0.0)
    x = x + _L2_gnn_ref(src, dst, h)
    h = jnp.maximum(_layernorm(x, axis=-1), 0.0)
    x = x + _L3_gnn_ref(h, edge_index, edge_attr_40, edge_weight, node_type_119, node_vec, batch0, L3_gnn_W1, L3_gnn_b1, L3_gnn_W2, L3_gnn_b2, L3_gnn_emb, L3_gnn_adaptW, L3_gnn_gamma, L3_gnn_beta)
    return x

_drawn_inputs = setup_inputs


def setup_inputs(seed=0):
    import zlib

    import numpy as np

    out = dict(_drawn_inputs(seed))
    spreads = {'L0_gnn_btm': (0.0, 0.1),
     'L0_gnn_b_in': (0.0, 2.0),
     'L0_gnn_g_in': (1.0, 0.2),
     'L0_gnn_be_in': (0.0, 0.1),
     'L0_gnn_bt1': (0.0, 0.1),
     'L0_gnn_bc1': (0.0, 0.1),
     'L0_gnn_g1': (1.0, 0.2),
     'L0_gnn_be1': (0.0, 0.1),
     'L0_gnn_bt2': (0.0, 0.1),
     'L0_gnn_bc2': (0.0, 0.1),
     'L0_gnn_g2': (1.0, 0.2),
     'L0_gnn_be2': (0.0, 0.514),
     'L0_gnn_b_out': (0.0, 2.0),
     'L0_gnn_g_out': (1.0, 0.2),
     'L0_gnn_be_out': (0.0, 0.1),
     'L1_gnn_b1': (0.0, 0.1),
     'L1_gnn_b2': (0.0, 0.1),
     'L3_gnn_gamma': (1.0, 0.2),
     'L3_gnn_beta': (0.0, 0.297)}
    factors = {'edge_attr_40': 4.142,
     'edge_weight': 3.66,
     'node_vec': 5.332,
     'L3_gnn_b1': 64.0,
     'L3_gnn_b2': 64.0,
     'L3_gnn_emb': 64.0,
     'L3_gnn_adaptW': 64.0}
    for name, (base, spread) in spreads.items():
        noise = np.random.default_rng([zlib.crc32(name.encode()), seed]).standard_normal(out[name].shape)
        drawn = base * np.exp(spread * noise) if base else spread * noise
        out[name] = jnp.asarray(drawn.astype(out[name].dtype))
    for name, factor in factors.items():
        out[name] = (out[name] * factor).astype(out[name].dtype)
    return out
```

```python
from contextlib import ExitStack

import numpy as np

import concourse.bass as bass
from concourse import mybir

F32 = mybir.dt.float32
F16 = mybir.dt.float16
I32 = mybir.dt.int32
ALU = mybir.AluOpType
ACT = mybir.ActivationFunctionType
AX = mybir.AxisListType.X

N, E, C, RBF, NEL, GD = 3125, 53125, 48, 40, 119, 32
P = 128
NT = -(-N // P)
NP = NT * P
TAIL = N - (NT - 1) * P
C3, C9 = 3 * C, 9 * C
C2P = 2 * C
EPS = 1e-5
LOW = 4096.0

WIN = 16
NWIN = -(-N // WIN)
NC = NWIN * WIN
CODE = 64
WCH = 4
NCHUNK = 4 * (-(-E // 512))
EP = NCHUNK * P
NB = NCHUNK // 4

QT = [6, 6, 6, 7]
QCOL = [0, 768, 1536, 2304]
QW = [768, 768, 768, NC - 2304]
QMAX = max(QW)
SW = 7 * P
M2, M3 = 4, 2
R2, R3 = C9 // M2, C3 // M3
HALF = NC // 2
SC = 7
SCW = NC // SC
HROW = 80


def two_pi_parts():
    a = 6.28125
    b = float(np.float32(2 * np.pi - a))
    return a, b, float(2 * np.pi - a - b)


def build(nc, d, out):
    with ExitStack() as ctx:
        def sb(name, shape, dt):
            return ctx.enter_context(nc.sbuf_tensor(name, shape, dt))

        def sem(name):
            return ctx.enter_context(nc.semaphore(name))

        adj = sb("adj", [P, NT, NC], F16)
        big = sb("big", [P, 3600], F32)
        H = sb("H", [P, 7200], F16)
        S = sb("S", [P, 3, SW], F32)
        X = sb("X", [P, NT, C], F32)
        dinv_q = sb("dinv_q", [P, QMAX], F32)
        wreg = sb("wreg", [P, 1296], F32)
        bnst = sb("bnst", [P, M2, 8, 6], F32)
        mv = sb("mv", [P, M2, 2], F32)
        dinv = sb("dinv", [P, NT], F32)
        rdeg = sb("rdeg", [P, NT], F32)
        nvec = sb("nvec", [P, NT], F32)
        rtot = sb("rtot", [P, NT], F32)
        stat = sb("stat", [P, 2, NT], F32)
        sq = sb("sq", [P, C3], F32)
        comb = sb("comb", [P, C], F32)
        pidx = sb("pidx", [P, 1], F32)
        half = sb("half", [P, 1], F32)
        cols = sb("cols", [P, 31], F32)
        bias2 = sb("bias2", [P, M2], F32)
        bias3 = sb("bias3", [P, M3], F32)
        e1st = sb("e1st", [P, 2, 2, GD], F32)
        e1ix = sb("e1ix", [P, 2, 4], I32)
        ps = ctx.enter_context(nc.psum_tensor("ps", [P, 8, 512], F32))

        G_d = nc.dram_tensor("gate_edges", [NB, P, 4 * C], F32, kind="Internal").ap()
        E1_d = nc.dram_tensor("emb_src_edges", [NB, P, 4 * GD], F32, kind="Internal").ap()
        TN1_d = nc.dram_tensor("emb_nodes", [NP, GD], F32, kind="Internal").ap()
        HV_d = nc.dram_tensor("hv_nodes", [NP, HROW], F32, kind="Internal").ap()
        DI_d = nc.dram_tensor("dinv_row", [NP], F32, kind="Internal").ap()
        R2_d = nc.dram_tensor("relu2", [R2, M2, NC], F32, kind="Internal").ap()
        R3_d = nc.dram_tensor("relu3", [R3, M3, NC], F32, kind="Internal").ap()

        ID_d = nc.dram_tensor("identity", [P, P], F16, kind="Internal").ap()

        bigC3 = big[:, :].rearrange("p (t f) -> p t f", f=C3)
        hA = big[:, 0:1200].rearrange("p (t f) -> p t f", f=C)
        hT = big[:, 1200:2400].rearrange("p (t f) -> p t f", f=C)
        hY = big[:, 2400:3600].rearrange("p (t f) -> p t f", f=C)
        H1 = H[:, 0:2400].rearrange("p (t g h f) -> p t g h f", g=1, h=2, f=C)
        H3 = H[:, :].rearrange("p (t g h f) -> p t g h f", g=3, h=2, f=C)
        Hf = H[:, :].bitcast(F32)
        HfC3 = Hf.rearrange("p (t f) -> p t f", f=C3)
        Hf1 = Hf[:, 0:1200].rearrange("p (t f) -> p t f", f=C)
        rst = big[:, 0:M2 * QMAX].rearrange("p (m w) -> p m w", w=QMAX)
        Sflat = S[:, :, :].rearrange("p a b -> p (a b)")
        early = adj[:, :, :].rearrange("p a b -> p (a b)").bitcast(F32)
        typ = early[:, 0:NP].bitcast(I32)
        onehot_t = early[:, NP:2 * NP]
        tn = early[:, 2 * NP:2 * NP + NT * 64].rearrange("p (t f) -> p t f", f=64)
        wtm = wreg[:, 0:128]
        wt1 = wreg[:, 128:560]
        wt2 = wreg[:, 560:704]
        embT = wreg[0:GD, 704:704 + NEL]
        adaT = wreg[0:GD, 824:824 + GD]
        tt12 = wreg[0:NEL, 856:856 + 64]
        w1t = wreg[0:RBF, 1168:1296]
        w2b = wreg[0:C + 1, 968:1016]
        b1c = wreg[0:C, 1016:1017]
        tw = wreg[:, 1020:1040]
        ident16 = wreg[:, 1040:1104].bitcast(F16)
        iota16 = wreg[:, 1104:1168].bitcast(F16)
        dst_i = big[:, 0:NCHUNK].bitcast(I32)
        src_i = big[:, NCHUNK:2 * NCHUNK].bitcast(I32)
        dst_f = big[:, 2 * NCHUNK:3 * NCHUNK]
        hi_f = big[:, 3 * NCHUNK:4 * NCHUNK]
        lo_f = big[:, 4 * NCHUNK:5 * NCHUNK]
        cw = big[:, 5 * NCHUNK:6 * NCHUNK]
        wtab = big[:, 2496:2496 + NWIN]
        c0i = big[0:1, 2716:2716 + NWIN].bitcast(I32)
        c0f = big[0:1, 2912:2912 + NWIN]
        key = big[:, 3520:3520 + 48].rearrange("p (b t w k) -> p b t w k", b=2, t=3, w=2)
        gst = big[:, 3108:3108 + 384].rearrange("p (b f) -> p b f", b=2)
        last_i = big[0:104, 3492:3496].bitcast(I32)
        last_f = big[0:104, 3496:3500]
        ones1 = big[:, 3500:3501]
        mov = H[:, 0:3200].rearrange("p (b k n) -> p b k n", b=2, k=WCH)
        sta = H[:, 3200:4224].rearrange("p (b k n) -> p b k n", b=2, k=WCH)
        iota_w = H[:, 4224:4624]
        cmp_w = Hf[0:104, 2320:2320 + NWIN * 4].rearrange("p (g w) -> p g w", g=4)
        attr = Sflat[0:RBF, 0:1024].rearrange("p (b e) -> p b e", b=2)
        silu = Sflat[0:C + 1, 1024:2048].rearrange("p (b e) -> p b e", b=2)
        ones16 = H[:, 4624:4626]
        degrow = big[0:1, 0:NC]
        af = adj[:, :, :].rearrange("p a b -> p (a b)").bitcast(F32)
        iota_n = adj[:, 0, :]
        ohn = adj[:, 1:9, :].rearrange("p (b k) n -> p b k n", b=2)
        o0 = 9 * NC // 2
        ldst = af[:, o0:o0 + NCHUNK].bitcast(I32)
        lsrc_i = af[:, o0 + NCHUNK:o0 + 2 * NCHUNK].bitcast(I32)
        lsrc = af[:, o0 + 2 * NCHUNK:o0 + 3 * NCHUNK]
        lcw = af[:, o0 + 3 * NCHUNK:o0 + 4 * NCHUNK]
        o1 = o0 + 4 * NCHUNK
        lg = af[:, o1:o1 + 384].rearrange("p (b k f) -> p b k f", b=2, k=4)
        le = af[:, o1 + 384:o1 + 640].rearrange("p (b k f) -> p b k f", b=2, k=4)
        lh = af[:, o1 + 640:o1 + 1280].rearrange("p (b k f) -> p b k f", b=2, k=4)
        ldot = af[:, o1 + 1280:o1 + 1536].rearrange("p (b k f) -> p b k f", b=2, k=4)
        la = af[:, o1 + 1536:o1 + 1544].rearrange("p (b k) -> p b k", b=2)
        lm = af[:, o1 + 1544:o1 + 1928].rearrange("p (b k f) -> p b k f", b=2, k=4)
        lmh = af[:, o1 + 1928:o1 + 2312].bitcast(F16).rearrange("p (b k h f) -> p b k h f", b=2, k=4, h=2)
        lix = af[:, o1 + 2320:o1 + 2328].bitcast(I32).rearrange("p (b k) -> p b k", b=2)
        aggS = af[:, o1 + 2400:o1 + 2400 + NP]
        o2 = o1 + 2400 + NP
        iota_i = af[:, o2:o2 + NC].bitcast(I32)
        cw_t = af[:, o2 + NC:o2 + NC + 3 * NCHUNK].rearrange("p (k n) -> p k n", k=3)

        CB = {}
        at = 0
        for nm, w in (("btm", 1), ("freq", 1), ("bc1", M2), ("bt1", M2), ("g1", M2), ("be1", M2),
                      ("bc2", M3), ("bt2", M3), ("g2", M3), ("be2", M3), ("tstep", 1)):
            CB[nm] = (at, w)
            at += w

        def col(nm, rows=P):
            a, w = CB[nm]
            return cols[0:rows, a:a + w]

        names = """in_small in_edges in_types in_x in_cw tables_tt tables_T t_onehot t_mm t_evac tn_stored
            consts ones_row c0_cmp c0_sum c0_ready keys_prep dve_step act_step pool_step
            t_emb t_mm1 t_rel t_mm2 bias_ready t_r
            key_ready onehots_built win_done win_evac
            attr_in0 attr_in1 z_done silu_done gate_done g_evac gstored0 gstored1 cw_ready
            pool_passed deg_h deg_mm deg_row deg_tr deg_col dinv_stored dinv_in
            var_ready std_ready h_scaled h_hi h_res h_ready spmm_done spmm_evac
            n1_done n1_evac nq_done nq_evac fe_done fe_evac r_stored bn_read
            bn_in bn_mm bn_cent bn_sq bn_aff
            w0_in w1_in w1_ready w2_in w3_in w4_in w5_in w6_in w7_in fold_t fold_mm fold_w ring0 ring1 ring2 ring3
            cv_done cv_evac tr_done tr_evac self_done self_evac
            ident_ready ident_kept flip_done flip_evac flip_cols adj_i adj_noi adj_t e1_in0 e1_in1 e1_got0 e1_got1 e1_st0 e1_st1
            hv_ready hv_stored late_in lcw_ready l_in0 l_in1 l_got0 l_got1 l_msg l_hi l_res l_lo l_oh l_mm
            agg_evac agg_mm tot_in tot_mm out_ready out_done relu_in relu_out padz ln_x""".split()
        s = {n: sem(n) for n in names}

        class Chain:

            def __init__(self, eng, semaphore):
                self.eng, self.sem, self.n = eng, semaphore, 0

            def __call__(self, instruction):
                self.n += 1
                instruction.then_inc(self.sem, 1)
                self.eng.wait_ge(self.sem, self.n)

        block = ctx.enter_context(nc.Block())
        GCN_FEATURE = (1, 2)
        GROUPS = [1, 3, 3, 1, 1, 1, 1, 1]
        UNIT0 = [4 * sum(GROUPS[:i]) for i in range(9)]
        NODE_ORDER = {3: 0, 4: 1, 5: 2, 6: 3, 7: 4}
        FLIPS = [(x, list(range(y, min(y + 4, x + 1)))) for x in range(NT) for y in range(0, x + 1, 4)]
        FLIP_COLS = [sum(any(y != x for y in ys) for x, ys in FLIPS[:k + 1]) for k in range(len(FLIPS))]
        FE0 = {1: 0, 2: 4 * 2 * M2}

        def quarter_used(eng, i, q):
            if i == 0:
                eng.wait_ge(s["n1_done"], sum(QT[:q + 1]))
            elif i in GCN_FEATURE:
                eng.wait_ge(s["fe_done"], FE0[i] + 2 * (M2 if i == 1 else M3) * (q + 1))
            else:
                eng.wait_ge(s["nq_done"], 4 * NODE_ORDER[i] + q + 1)

        def bc(ap, n):
            return ap.broadcast_to(n)

        @block.sync
        def _(sp):
            def pb(name, n=P):
                return d[name][None, :].broadcast_to([n, d[name].shape[0]])

            small = [(wtm, d["Wtm"]), (wt1, d["Wt1"]), (wt2, d["Wt2"]), (embT, d["embT"]), (adaT, d["adaT"]),
                     (tt12[:, 0:GD], d["emb"]), (w1t[:, 0:C], d["W1T"]), (w2b[0:C, :], d["W2T"]),
                     (w2b[C:C + 1, :], d["b2"][None, :]), (b1c, d["b1"][:, None]),
                     (col("btm"), d["btm"][:, None]), (col("freq"), d["freq"][:, None]),
                     (col("tstep"), d["timestep"][None, :].broadcast_to([P, 1])), (nvec[:, :], d["node_vec"])]
            for nm, r in (("bc1", R2), ("bt1", R2), ("g1", R2), ("be1", R2),
                          ("bc2", R3), ("bt2", R3), ("g2", R3), ("be2", R3)):
                small.append((col(nm, r), d[nm]))
            sp.dma_start(dst_i, d["dst"]).then_inc(s["in_edges"], 16)
            sp.dma_start(src_i, d["src"]).then_inc(s["in_edges"], 16)
            sp.dma_start(last_i, d["dst"][P - 1:P, :].rearrange("o (p g) -> (o p) g", g=4)).then_inc(s["in_edges"], 16)
            sp.dma_start(cw, d["edge_weight"]).then_inc(s["in_cw"], 16)
            for o, i in small:
                sp.dma_start(o, i).then_inc(s["in_small"], 16)
            sp.dma_start(typ[0:NEL, :], d["node_type"][None, :].broadcast_to([NEL, NP])).then_inc(s["in_types"], 16)
            sp.dma_start(X[:, :, :], d["x"].rearrange("(t p) f -> p t f", p=P)).then_inc(s["in_x"], 16)
            sp.wait_ge(s["ident_ready"], 1)
            sp.dma_start(ID_d, ident16).then_inc(s["ident_kept"], 16)
            sp.wait_ge(s["t_evac"], 4)
            sp.dma_start(TN1_d.rearrange("(t p) f -> p t f", p=P), tn[:, :, 0:GD]).then_inc(s["tn_stored"], 16)
            sp.dma_start(HV_d[:, C:HROW].rearrange("(t p) f -> p t f", p=P), tn[:, :, GD:2 * GD]).then_inc(s["tn_stored"], 16)
            sp.wait_ge(s["padz"], 1)

            def load_attr(b, par):
                sp.wait_ge(s["silu_done"], b + 1)
                sp.dma_start(attr[:, par, :], d["edge_attr"][:, bass.ds(b * 512, 512)]).then_inc(s[f"attr_in{par}"], 16)

            def store_gate(b, par):
                sp.wait_ge(s["g_evac"], b + 3)
                sp.dma_start(G_d[bass.ds(b, 1), :, :].rearrange("o p f -> (o p) f"), gst[:, par, :]).then_inc(s[f"gstored{par}"], 16)

            load_attr(0, 0)
            load_attr(1, 1)
            with sp.Fori(0, NB // 2 - 1) as i:
                load_attr(i * 2 + 2, 0)
                load_attr(i * 2 + 3, 1)
                store_gate(i * 2, 0)
                store_gate(i * 2 + 1, 1)
            store_gate(NB - 2, 0)
            store_gate(NB - 1, 1)
            sp.wait_ge(s["deg_tr"], 1)
            sp.wait_ge(s["gstored0"], 16 * (NB // 2))
            sp.wait_ge(s["gstored1"], 16 * (NB // 2))
            w = wreg
            for o, i in ((w[0:C, 0:C3], d["W_in"]), (w[C:C2P, 0:C3], d["W_in"]), (w[:, C3:2 * C3], pb("b_in")),
                         (w[:, 2 * C3:3 * C3], pb("g_in")), (w[:, 3 * C3:4 * C3], pb("be_in"))):
                sp.dma_start(o, i).then_inc(s["w0_in"], 16)
            sp.wait_ge(s["deg_col"], 1)
            sp.dma_start(DI_d.rearrange("(t p) -> p t", p=P), dinv[:, :], allow_slow_non_contiguous=True).then_inc(s["dinv_stored"], 16)
            sp.wait_ge(s["dinv_stored"], 16)

            def dinv_quarter(i, q):
                k = 4 * (i - 1) + q
                if k:
                    sp.wait_ge(s["spmm_evac"], UNIT0[i] + 3 * q)
                sp.dma_start(dinv_q[:, 0:QW[q]], DI_d[None, QCOL[q]:QCOL[q] + QW[q]].broadcast_to([P, QW[q]])).then_inc(s["dinv_in"], 16)

            def store_relu(i, q, dram, rows, m):
                k0 = FE0[i] + 2 * m * (q + 1)
                sp.wait_ge(s["fe_evac"], k0)
                sp.dma_start(dram[:, :, QCOL[q]:QCOL[q] + QW[q]], rst[0:rows, 0:m, 0:QW[q]]).then_inc(s["r_stored"], 16)

            def ring_tiles(i, dram, rows, m):
                for t in range(NT):
                    k = NT * (i - 1) + t
                    if t >= 4:
                        sp.wait_ge(s["cv_done"], NT * (i - 1) + t - 3)
                    wd = min(P, NC - P * t)
                    slot = Sflat[0:rows, (t % 4) * 512:(t % 4) * 512 + m * P].rearrange("p (m n) -> p m n", m=m)
                    sp.dma_start(slot[:, :, 0:wd], dram[:, :, P * t:P * t + wd]).then_inc(s[f"ring{t % 4}"], 16)

            sp.wait_ge(s["bn_aff"], 1)
            for o, i in ((w[0:C, :], 0), (w[C:C2P, :], 0)):
                sp.dma_start(o.rearrange("p (g f) -> p g f", g=3), d["Wc1"].rearrange("(g p) f -> p g f", g=3)).then_inc(s["w1_in"], 16)
            for q in range(4):
                dinv_quarter(1, q)
                if q:
                    store_relu(1, q - 1, R2_d, R2, M2)
            store_relu(1, 3, R2_d, R2, M2)
            quarter_used(sp, 1, 3)
            sp.dma_start(w[0:R2, 0:M2 * C3].rearrange("p (m f) -> p m f", m=M2), d["Wc2"].rearrange("(m p) f -> p m f", m=M2)).then_inc(s["w2_in"], 16)
            sp.wait_ge(s["r_stored"], 64)
            ring_tiles(1, R2_d, R2, M2)
            for q in range(4):
                dinv_quarter(2, q)
                if q:
                    store_relu(2, q - 1, R3_d, R3, M3)
            store_relu(2, 3, R3_d, R3, M3)
            quarter_used(sp, 2, 3)
            sp.dma_start(w[0:R3, 0:M3 * C].rearrange("p (m f) -> p m f", m=M3), d["W_out"].rearrange("(m p) f -> p m f", m=M3)).then_inc(s["w3_in"], 16)
            for k, nm in enumerate(("b_out", "g_out", "be_out")):
                sp.dma_start(w[:, C3 + C * k:C3 + C * k + C], pb(nm)).then_inc(s["w3_in"], 16)
            sp.wait_ge(s["r_stored"], 128)
            ring_tiles(2, R3_d, R3, M3)
            sp.wait_ge(s["bn_aff"], 2)
            for k, nm in enumerate(("W_self1", "W_neigh1", "sb1", "W_self2", "W_neigh2", "sb2")):
                if nm[0] == "s":
                    sp.dma_start(w[:, C * k:C * k + C], pb(nm)).then_inc(s["w4_in"], 16)
                else:
                    sp.dma_start(w[0:C, C * k:C * k + C], d[nm]).then_inc(s["w4_in"], 16)
                    if "neigh" in nm:
                        sp.dma_start(w[C:C2P, C * k:C * k + C], d[nm]).then_inc(s["w4_in"], 16)
            sp.wait_ge(s["ident_kept"], 16)
            sp.dma_start(ident16, ID_d).then_inc(s["w4_in"], 16)
            sp.wait_ge(s["nq_evac"], 20)
            for k, nm in enumerate(("gamma", "beta")):
                sp.dma_start(w[:, 512 + C * k:512 + C * k + C], pb(nm)).then_inc(s["w6_in"], 16)
            sp.dma_start(ldst, d["dst"]).then_inc(s["late_in"], 16)
            sp.dma_start(lsrc_i, d["src"]).then_inc(s["late_in"], 16)
            sp.dma_start(lcw, d["edge_weight"]).then_inc(s["late_in"], 16)
            sp.wait_ge(s["hv_ready"], 1)
            sp.dma_start(HV_d[:, 0:C].rearrange("(t p) f -> p t f", p=P), hT).then_inc(s["hv_stored"], 16)
            sp.wait_ge(s["e1_st0"], 16 * NB)
            sp.wait_ge(s["e1_st1"], 16 * NB)

            def load_late(b, par):
                sp.wait_ge(s["l_msg"], b + 1)
                sp.dma_start(lg[:, par, :, :].rearrange("p k f -> p (k f)"), G_d[bass.ds(b, 1), :, :].rearrange("o p f -> (o p) f")).then_inc(s[f"l_in{par}"], 16)
                sp.dma_start(le[:, par, :, :].rearrange("p k f -> p (k f)"), E1_d[bass.ds(b, 1), :, :].rearrange("o p f -> (o p) f")).then_inc(s[f"l_in{par}"], 16)

            with sp.Fori(0, NB // 2) as i:
                load_late(i * 2, 0)
                load_late(i * 2 + 1, 1)
            sp.wait_ge(s["out_ready"], 1)
            full = (NT - 1) * P
            sp.dma_start(out[0:full, :].rearrange("(t p) f -> p t f", p=P), X[:, 0:NT - 1, :]).then_inc(s["out_done"], 16)
            sp.dma_start(out[full:N, :], X[0:TAIL, NT - 1, :]).then_inc(s["out_done"], 16)
            sp.wait_ge(s["out_done"], 32)

        @block.gpsimd
        def _(pool):
            g = nc.gpsimd
            step = Chain(pool, s["pool_step"])
            g.iota(pidx[:, :], [[0, 1]], base=0, channel_multiplier=1, allow_small_or_imprecise_dtypes=True).then_inc(s["consts"], 1)
            g.iota(iota16, [[1, P]], base=0, channel_multiplier=0, allow_small_or_imprecise_dtypes=True).then_inc(s["consts"], 1)
            g.iota(iota_w, [[CODE, NT], [1, WIN]], base=0, channel_multiplier=0, allow_small_or_imprecise_dtypes=True).then_inc(s["consts"], 1)
            g.iota(wtab, [[WIN, NWIN]], base=0, channel_multiplier=0, allow_small_or_imprecise_dtypes=True).then_inc(s["consts"], 1)
            pool.wait_ge(s["consts"], 4)
            pool.wait_ge(s["keys_prep"], 1)
            pool.wait_ge(s["c0_ready"], 1)

            def pair_keys(pair, slot):
                w = pair * 2
                pool.wait_ge(s["onehots_built"], w + 1)
                c0 = [pool.value_load(c0i[0:1, bass.ds(w + j, 1)], min_val=0, max_val=NCHUNK - WCH) for j in range(2)]
                for j in range(2):
                    g.tensor_copy(key[:, slot, 2, j, :], lo_f[:, bass.ds(c0[j], WCH)])
                    ins = g.tensor_tensor(key[:, slot, 1, j, :], dst_f[:, bass.ds(c0[j], WCH)],
                                          bc(wtab[:, bass.ds(w + j, 1)], [P, WCH]), ALU.subtract)
                ins.then_inc(s["pool_step"], 1)
                pool.wait_ge(s["pool_step"], w + 1)
                pool.sem_inc(s["pool_passed"], 1)
                g.tensor_scalar(key[:, slot, 1, :, :], key[:, slot, 1, :, :], float(WIN), -1.0, ALU.min, ALU.max).then_inc(s["pool_step"], 1)
                pool.wait_ge(s["pool_step"], w + 2)
                for j in range(2):
                    ins = g.tensor_tensor(key[:, slot, 0, j, :], key[:, slot, 1, j, :], hi_f[:, bass.ds(c0[j], WCH)], ALU.add)
                ins.then_inc(s["key_ready"], 1)

            with pool.Fori(0, NWIN // 4) as i:
                pair_keys(i * 2, 0)
                pair_keys(i * 2 + 1, 1)

            def load_sources(b, par):
                pool.dma_start(e1ix[:, par, :], d["src"][:, bass.ds(b * 4, 4)]).then_inc(s[f"e1_in{par}"], 16)

            def gather_half(b, par, h, turn):
                if turn is not None:
                    pool.wait_ge(s[f"e1_st{h}"], turn)
                    pool.sem_inc(s["pool_passed"], 1)
                for k in range(2):
                    g.indirect_dma_start(out=e1st[:, h, k, :], out_offset=None, in_=TN1_d,
                                         in_offset=bass.IndirectOffsetOnAxis(ap=e1ix[:, par, 2 * h + k:2 * h + k + 1], axis=0)).then_inc(s[f"e1_got{h}"], 16)

            def store_half(b, h, turn):
                pool.wait_ge(s[f"e1_got{h}"], turn)
                pool.dma_start(E1_d[bass.ds(b, 1), :, 2 * GD * h:2 * GD * h + 2 * GD].rearrange("o p f -> (o p) f"),
                               e1st[:, h, :, :].rearrange("p k f -> p (k f)")).then_inc(s[f"e1_st{h}"], 16)

            def gather_batch(i, par, more=True):
                b = i * 2 + par
                pool.wait_ge(s[f"e1_in{par}"], i * 16 + 16)
                pool.sem_inc(s["pool_passed"], 1)
                first = isinstance(b, int) and b == 0
                gather_half(b, par, 0, None if first else b * 16)
                gather_half(b, par, 1, None if first else b * 16)
                store_half(b, 0, b * 32 + 32)
                store_half(b, 1, b * 32 + 32)
                if more:
                    load_sources(b + 2, par)

            pool.wait_ge(s["tn_stored"], 32)
            load_sources(0, 0)
            load_sources(1, 1)
            gather_batch(0, 0)
            gather_batch(0, 1)
            with pool.Fori(1, NB // 2 - 1) as i:
                gather_batch(i, 0)
                gather_batch(i, 1)
            gather_batch(NB // 2 - 1, 0, more=False)
            gather_batch(NB // 2 - 1, 1, more=False)
            pool.wait_ge(s["nq_evac"], 20)
            g.iota(iota_n, [[1, NC]], base=-(NC // 2), channel_multiplier=0, allow_small_or_imprecise_dtypes=True).then_inc(s["consts"], 1)
            pool.wait_ge(s["hv_stored"], 16)
            pool.wait_ge(s["late_in"], 48)

            def gather_dst(b, par):
                pool.wait_ge(s["l_msg"], b + 1)
                g.tensor_copy(lix[:, par, :], ldst[:, bass.ds(b * 4, 4)]).then_inc(s["pool_step"], 1)
                pool.wait_ge(s["pool_step"], b + (NWIN + 1))
                pool.sem_inc(s["pool_passed"], 1)
                for k in range(4):
                    g.indirect_dma_start(out=lh[:, par, k, :], out_offset=None, in_=HV_d,
                                         in_offset=bass.IndirectOffsetOnAxis(ap=lix[:, par, k:k + 1], axis=0)).then_inc(s[f"l_got{par}"], 16)

            with pool.Fori(0, NB // 2) as i:
                gather_dst(i * 2, 0)
                gather_dst(i * 2 + 1, 1)

        @block.vector
        def _(dve):
            v = nc.vector
            step = Chain(dve, s["dve_step"])
            dve.sem_inc(s["onehots_built"], 3)
            dve.sem_inc(s["g_evac"], 2)
            step(v.memset(w1t[:, C:P], 0.0))
            dve.wait_ge(s["consts"], 2)
            step(v.tensor_scalar(half[:, :], pidx[:, :], float(C), 1.0 / LOW - 1.0, ALU.is_ge, ALU.mult))
            step(v.tensor_scalar(half[:, :], half[:, :], 1.0, None, ALU.add))
            step(v.tensor_scalar(sq[:, 0:C], iota16[:, 0:C], pidx[:, 0:1], None, ALU.is_equal))
            step(v.tensor_scalar(sq[:, C:C + 1], pidx[:, :], -float(C), None, ALU.add))
            step(v.tensor_scalar(comb[:, :], iota16[:, 0:C], sq[:, C:C + 1], None, ALU.is_equal))
            step(v.tensor_tensor(comb[:, :], comb[:, :], sq[:, 0:C], ALU.add))
            step(v.tensor_scalar(comb[:, :], comb[:, :], half[:, 0:1], None, ALU.mult))
            v.tensor_scalar(ident16, iota16, pidx[:, 0:1], None, ALU.is_equal).then_inc(s["ident_ready"], 1)
            dve.wait_ge(s["in_small"], 16 * 22)
            A, B, D = two_pi_parts()
            ang, kk, r, ph = tw[:, 0:1], tw[:, 1:2], tw[:, 2:3], tw[:, 3:4]
            step(v.tensor_tensor(ang, col("tstep"), col("freq"), ALU.mult))
            step(v.tensor_scalar(ph, pidx[:, :], 64.0, float(np.pi / 2), ALU.is_ge, ALU.mult))
            step(v.tensor_tensor(kk, ang, ph, ALU.add))
            step(v.tensor_scalar(kk, kk, float(1 / (2 * np.pi)), 12582912.0, ALU.mult, ALU.add))
            step(v.tensor_scalar(kk, kk, -12582912.0, None, ALU.add))
            step(v.scalar_tensor_tensor(r, kk, -A, ang, ALU.mult, ALU.add))
            step(v.scalar_tensor_tensor(r, kk, -B, r, ALU.mult, ALU.add))
            step(v.tensor_tensor(r, r, ph, ALU.add))
            step(v.scalar_tensor_tensor(r, kk, -D, r, ALU.mult, ALU.add))
            v.tensor_scalar(r, r, 3.1415925, -3.1415925, ALU.min, ALU.max).then_inc(s["t_r"], 1)
            dve.wait_ge(s["t_mm1"], 1)
            step(v.tensor_tensor(tw[:, 5:6], ps[:, 0, 0:1], col("btm"), ALU.add))
            v.tensor_scalar(tw[:, 5:6], tw[:, 5:6], 0.0, None, ALU.max).then_inc(s["t_rel"], 1)
            dve.wait_ge(s["t_mm2"], 1)
            step(v.tensor_tensor(bias2[0:R2, :], ps[0:R2, 1, 0:M2], col("bt1", R2), ALU.add))
            step(v.tensor_scalar(bias2[0:R2, :], bias2[0:R2, :], 0.0, None, ALU.max))
            step(v.tensor_tensor(bias2[0:R2, :], bias2[0:R2, :], col("bc1", R2), ALU.add))
            step(v.tensor_tensor(bias3[0:R3, :], ps[0:R3, 1, M2:M2 + M3], col("bt2", R3), ALU.add))
            step(v.tensor_scalar(bias3[0:R3, :], bias3[0:R3, :], 0.0, None, ALU.max))
            v.tensor_tensor(bias3[0:R3, :], bias3[0:R3, :], col("bc2", R3), ALU.add).then_inc(s["bias_ready"], 1)
            dve.wait_ge(s["tables_T"], 1)
            v.tensor_copy(tt12[:, GD:2 * GD], ps[0:NEL, 2, 0:GD]).then_inc(s["tables_tt"], 1)
            dve.wait_ge(s["in_types"], 16)
            v.tensor_scalar(onehot_t[0:NEL, :], typ[0:NEL, :], pidx[0:NEL, 0:1], None, ALU.is_equal).then_inc(s["t_onehot"], 1)
            for j in range(4):
                n = min(8, NT - 8 * j)
                dve.wait_ge(s["t_mm"], j + 1)
                v.tensor_copy(tn[:, 8 * j:8 * j + n, :], ps[:, 4 + j, 0:64 * n].rearrange("p (t f) -> p t f", f=64)).then_inc(s["t_evac"], 1)
            dve.wait_ge(s["in_edges"], 48)
            step(v.tensor_copy(last_f, last_i))
            v.memset(ones1, 1.0).then_inc(s["ones_row"], 1)
            dve.wait_ge(s["consts"], 4)
            for k in range(4):
                v.tensor_scalar(cmp_w[:, k, :], wtab[0:104, :], last_f[:, k:k + 1], None, ALU.is_gt).then_inc(s["c0_cmp"], 1)
            dve.wait_ge(s["c0_sum"], 1)
            step(v.tensor_scalar(c0f, ps[0:1, 3, 0:NWIN], float(NCHUNK - WCH), None, ALU.min))
            v.tensor_copy(c0i, c0f).then_inc(s["c0_ready"], 1)
            step(v.tensor_copy(dst_f, dst_i))
            step(v.tensor_scalar(dst_i, src_i, 7, 6, ALU.arith_shift_right, ALU.logical_shift_left))
            step(v.tensor_copy(hi_f, dst_i))
            step(v.tensor_scalar(dst_i, src_i, P - 1, None, ALU.bitwise_and))
            v.tensor_copy(lo_f, dst_i).then_inc(s["keys_prep"], 1)
            dve.wait_ge(s["in_cw"], 16)

            def cutoff(wd, k, r, m, act_at):
                step(v.tensor_scalar(k, wd, 1.0 / 12.0, 12582912.0, ALU.mult, ALU.add))
                step(v.tensor_scalar(k, k, -12582912.0, None, ALU.add))
                step(v.scalar_tensor_tensor(r, k, -12.0, wd, ALU.mult, ALU.add))
                step(v.tensor_scalar(k, r, -1.0, None, ALU.mult))
                step(v.tensor_tensor(r, r, k, ALU.max))
                step(v.tensor_scalar(r, r, float(-np.pi / 6), float(np.pi / 2), ALU.mult, ALU.add))
                v.tensor_scalar(m, wd, 6.0, 0.5, ALU.is_lt, ALU.mult).then_inc(s["cw_ready"], 1)
                dve.wait_ge(s["t_emb"], act_at)
                dve.wait_ge(s["cw_ready"], 1 if act_at == 2 else 2)
                step(v.tensor_scalar(r, r, 1.0, None, ALU.add))
                step(v.tensor_tensor(wd, r, m, ALU.mult))

            dve.wait_ge(s["keys_prep"], 1)
            dve.wait_ge(s["tn_stored"], 32)
            cutoff(cw, Sflat[:, 0:NCHUNK], Sflat[:, NCHUNK:2 * NCHUNK], Sflat[:, 2 * NCHUNK:3 * NCHUNK], 2)
            v.memset(silu[:, :, :], 1.0).then_inc(s["padz"], 1)

            def window_onehots(pair, slot, half_):
                w, par = pair * 2 + half_, half_
                if half_ == 0:
                    dve.wait_ge(s["key_ready"], pair + 1)
                dve.wait_ge(s["win_done"], w + 1)
                for k in range(WCH):
                    v.tensor_scalar(mov[:, par, k, :], iota_w, key[:, slot, 0, half_, k:k + 1], None, ALU.is_equal)
                    last = v.tensor_scalar(sta[:, par, k, :], iota16, key[:, slot, 2, half_, k:k + 1], None, ALU.is_equal)
                last.then_inc(s["onehots_built"], 1)

            def gate_out(b, par, turn):
                dve.wait_ge(s["gate_done"], b + 3)
                if not (isinstance(turn, int) and turn == 0):
                    dve.wait_ge(s[f"gstored{par}"], turn * 16)
                v.tensor_tensor(gst[:, par, :].rearrange("p (k f) -> p k f", k=4), ps[:, 4 + par, 0:4 * C].rearrange("p (k f) -> p k f", k=4),
                                bc(cw[:, bass.ds(b * 4, 4)].unsqueeze(2), [P, 4, C]), ALU.mult).then_inc(s["g_evac"], 1)

            def windows_and_gates(i):
                window_onehots(i * 2, 0, 0)
                window_onehots(i * 2, 0, 1)
                if not isinstance(i, int):
                    gate_out(i * 2 - 1, 1, i - 1)
                window_onehots(i * 2 + 1, 1, 0)
                window_onehots(i * 2 + 1, 1, 1)
                gate_out(i * 2, 0, i)

            windows_and_gates(0)
            with dve.Fori(1, NWIN // 4) as i:
                windows_and_gates(i)
            gate_out(2 * (NWIN // 4) - 1, 1, NWIN // 4 - 1)
            with dve.Fori(NWIN // 4, NB // 2) as i:
                gate_out(i * 2, 0, i)
                gate_out(i * 2 + 1, 1, i)
            dve.wait_ge(s["win_evac"], NWIN + 2)

            def diagonal(op):
                last = NC - P * (NT - 1)
                for t in range(NT):
                    wd = min(P, NC - P * t)
                    i = v.tensor_tensor(adj[0:wd, t, P * t:P * t + wd], adj[0:wd, t, P * t:P * t + wd], ident16[0:wd, 0:wd], op)
                return i

            diagonal(ALU.add).then_inc(s["adj_i"], 1)
            v.memset(ones16, 1.0).then_inc(s["deg_h"], 1)
            dve.wait_ge(s["deg_mm"], 1)
            dve.wait_ge(s["gstored0"], 16 * (NB // 2))
            dve.wait_ge(s["gstored1"], 16 * (NB // 2))
            for c in range(SC):
                i = v.tensor_copy(degrow[:, c * SCW:(c + 1) * SCW], ps[0:1, c, 0:SCW])
            i.then_inc(s["deg_row"], 1)
            dve.wait_ge(s["deg_tr"], 1)
            step(v.memset(stat[:, 1, :], 1.0))
            step(v.tensor_copy(stat[:, 1, 0:NT - 1], ps[:, 7, 0:NT - 1]))
            step(v.tensor_copy(stat[0:64, 1, NT - 1:NT], ps[0:64, 7, NT - 1:NT]))
            step(v.tensor_scalar(rdeg[:, :], stat[:, 1, :], -1.0, 1.0, ALU.add, ALU.max))
            step(v.reciprocal(rdeg[:, :], rdeg[:, :]))
            nsq = [0]

            def sqrt_of(a, n, rows=P):
                nsq[0] += 1
                v.tensor_copy(sq[0:rows, 0:n], a).then_inc(s["var_ready"], 1)
                dve.wait_ge(s["std_ready"], nsq[0])

            sqrt_of(stat[:, 1, :], NT)
            v.reciprocal(dinv[:, :], sq[:, 0:NT]).then_inc(s["deg_col"], 1)
            dve.wait_ge(s["deg_col"], 1)
            step(v.memset(Sflat[:, :], 0.0))

            def layernorm(out_h, tmp, gamma=None, beta=None, src=None):
                src = X[:, :, :] if src is None else src
                step(v.tensor_reduce(stat[:, 0, :], src, AX, ALU.add))
                step(v.tensor_scalar(stat[:, 0, :], stat[:, 0, :], 1.0 / C, None, ALU.mult))
                step(v.tensor_tensor(out_h, src, bc(stat[:, 0, :].unsqueeze(2), [P, NT, C]), ALU.subtract))
                step(v.tensor_tensor(tmp, out_h, out_h, ALU.mult))
                step(v.tensor_reduce(stat[:, 1, :], tmp, AX, ALU.add))
                step(v.tensor_scalar(stat[:, 1, :], stat[:, 1, :], 1.0 / C, EPS, ALU.mult, ALU.add))
                sqrt_of(stat[:, 1, :], NT)
                step(v.reciprocal(stat[:, 1, :], sq[:, 0:NT]))
                step(v.tensor_tensor(out_h, out_h, bc(stat[:, 1, :].unsqueeze(2), [P, NT, C]), ALU.mult))
                if gamma is None:
                    step(v.tensor_scalar(out_h, out_h, 0.0, None, ALU.max))

            nsplit = [0]

            def split(val, hview, scale=None):
                k = nsplit[0] = nsplit[0] + 1
                shape = list(val.shape)
                if scale is None:
                    dve.sem_inc(s["h_scaled"], 1)
                else:
                    v.tensor_tensor(val, val, bc(scale[:, :].unsqueeze(2), shape), ALU.mult).then_inc(s["h_scaled"], 1)
                    dve.wait_ge(s["h_scaled"], k)
                dve.wait_ge(s["h_hi"], k)
                if hview.shape[2] == 1:
                    v.tensor_tensor(val, val, hview[:, :, 0, 0, :], ALU.subtract).then_inc(s["h_res"], 1)
                else:
                    for gi in range(3):
                        i = v.tensor_tensor(val[:, :, C * gi:C * gi + C], val[:, :, C * gi:C * gi + C], hview[:, :, gi, 0, :], ALU.subtract)
                    i.then_inc(s["h_res"], 1)

            def rows_of(region, k, w):
                return region[:, k * w:(k + 1) * w]

            def bn_nodes(k, val, F, gB, bB):
                dve.wait_ge(s["bn_mm"], 2 * k + 1)
                step(v.tensor_scalar(sq[:, 0:F], ps[:, 4, 0:F], 1.0 / N, None, ALU.mult))
                v.tensor_tensor(val, val, bc(sq[:, 0:F].unsqueeze(1), [P, NT, F]), ALU.subtract).then_inc(s["bn_cent"], 1)
                dve.wait_ge(s["bn_cent"], k + 1)
                dve.wait_ge(s["bn_mm"], 2 * k + 2)
                step(v.tensor_scalar(sq[:, 0:F], ps[:, 5, 0:F], 1.0 / N, EPS, ALU.mult, ALU.add))
                nsq[0] += 1
                dve.sem_inc(s["var_ready"], 1)
                dve.wait_ge(s["std_ready"], nsq[0])
                step(v.reciprocal(sq[:, 0:F], sq[:, 0:F]))
                step(v.tensor_tensor(sq[:, 0:F], sq[:, 0:F], gB, ALU.mult))
                step(v.tensor_tensor(val, val, bc(sq[:, 0:F].unsqueeze(1), [P, NT, F]), ALU.mult))
                step(v.tensor_tensor(val, val, bc(bB.unsqueeze(1), [P, NT, F]), ALU.add))
                step(v.tensor_scalar(val, val, 0.0, None, ALU.max))
                dve.sem_inc(s["bn_aff"], 1)

            dve.wait_ge(s["in_x"], 16)
            layernorm(hA, hT)
            split(hA, H1, dinv)
            dve.wait_ge(s["w0_in"], 80)
            step(v.memset(wreg[:, 576:704], 1.0))
            v.tensor_scalar(wreg[0:C2P, 0:C3], wreg[0:C2P, 0:C3], half[0:C2P, 0:1], None, ALU.mult).then_inc(s["w1_ready"], 1)
            for t in range(NT):
                dve.wait_ge(s["n1_done"], t + 1)
                i = v.scalar_tensor_tensor(bigC3[:, t, :], ps[:, 4 + t % 4, 0:C3], dinv[:, t:t + 1], wreg[:, C3:2 * C3],
                                           ALU.mult, ALU.add).then_inc(s["n1_evac"], 1)
            dve.wait_ge(s["n1_evac"], NT)
            bn_nodes(0, bigC3, C3, wreg[:, 2 * C3:3 * C3], wreg[:, 3 * C3:4 * C3])
            split(bigC3, H3, dinv)
            dve.wait_ge(s["w1_in"], 32)
            v.tensor_scalar(wreg[0:C2P, :], wreg[0:C2P, :], half[0:C2P, 0:1], None, ALU.mult).then_inc(s["w1_ready"], 1)

            def feature_conv(i, rows, m):
                for q in range(4):
                    for gi in range(3):
                        u = UNIT0[i] + 3 * q + gi
                        dve.wait_ge(s["spmm_done"], u + 1)
                        if gi == 0:
                            dve.wait_ge(s["dinv_in"], 16 * (4 * (i - 1) + q + 1))
                            if q:
                                quarter_used(dve, i, q - 1)
                        bank = 2 * (u % 2)
                        hw = QW[q] // 2
                        v.tensor_tensor(S[0:C2P, gi, 0:QW[q]].rearrange("p (c w) -> p c w", c=2), ps[0:C2P, bank:bank + 2, 0:hw],
                                        dinv_q[0:C2P, 0:QW[q]].rearrange("p (c w) -> p c w", c=2), ALU.mult).then_inc(s["spmm_evac"], 1)
                    if q:
                        stats_of(i, q - 1, rows, m)
                stats_of(i, 3, rows, m)

            def stats_of(i, q, rows, m):
                hw = QW[q] // 2
                for c in range(2):
                    for mi in range(m):
                        k = FE0[i] + (2 * q + c) * m + mi
                        dve.wait_ge(s["fe_evac"], k + 1)
                        n = min(hw, N - QCOL[q] - c * hw)
                        v.bn_stats(bnst[0:rows, mi, 2 * q + c, :], rst[0:rows, mi, c * hw:c * hw + n]).then_inc(s["bn_read"], 1)

            def fold(i, rows, m, F, gc, bc_, win):
                dve.wait_ge(s["bn_read"], FE0[i] + 8 * m)
                for mi in range(m):
                    ins = v.bn_aggr(mv[0:rows, mi, :], bnst[0:rows, mi, :, :].rearrange("p a b -> p (a b)"))
                step(ins)
                step(v.tensor_scalar(mv[0:rows, 0:m, 1], mv[0:rows, 0:m, 1], EPS, None, ALU.add))
                sqrt_of(mv[0:rows, 0:m, 1], m, rows)
                step(v.reciprocal(sq[0:rows, 0:m], sq[0:rows, 0:m]))
                step(v.tensor_tensor(sq[0:rows, 0:m], sq[0:rows, 0:m], gc, ALU.mult))
                step(v.tensor_tensor(sq[0:rows, m:2 * m], sq[0:rows, 0:m], mv[0:rows, 0:m, 0], ALU.mult))
                step(v.tensor_tensor(sq[0:rows, 2 * m:3 * m], bc_, sq[0:rows, m:2 * m], ALU.subtract))
                step(v.memset(Hf[0:rows, 0:m * P], 1.0))
                for mi in range(m):
                    ins = v.tensor_scalar(Hf[0:rows, mi * P:(mi + 1) * P], Hf[0:rows, mi * P:(mi + 1) * P], sq[0:rows, 2 * m + mi:2 * m + mi + 1], None, ALU.mult)
                dve.wait_ge(s[win], 16 if i == 1 else 64)
                ins.then_inc(s["fold_t"], 1)
                dve.wait_ge(s["fold_mm"], i)
                v.tensor_copy(wreg[:, m * F:(m + 1) * F], ps[:, 4, 0:F])
                for mi in range(m):
                    ins = v.tensor_scalar(wreg[0:rows, mi * F:(mi + 1) * F], wreg[0:rows, mi * F:(mi + 1) * F], sq[0:rows, mi:mi + 1], None, ALU.mult)
                ins.then_inc(s["fold_w"], 1)
                dve.wait_ge(s["fold_w"], i)
                dve.wait_ge(s["r_stored"], 64 * i)
                dst = bigC3 if F == C3 else hA
                for t in range(NT):
                    dve.wait_ge(s["cv_done"], NT * (i - 1) + t + 1)
                    v.tensor_tensor(dst[:, t, :], ps[:, 4 + t % 4, 0:F], wreg[:, m * F:(m + 1) * F], ALU.add).then_inc(s["cv_evac"], 1)
                dve.wait_ge(s["cv_evac"], NT * i)

            feature_conv(1, R2, M2)
            fold(1, R2, M2, C3, col("g1", R2), col("be1", R2), "w2_in")
            split(bigC3, H3, dinv)
            step(v.memset(wreg[:, 720:720 + 432], 0.0))
            for gi in range(3):
                ins = v.tensor_copy(wreg[:, 720 + 192 * gi:720 + 192 * gi + C], comb[:, :])
            ins.then_inc(s["w1_ready"], 1)
            step(v.memset(Sflat[:, :], 0.0))
            feature_conv(2, R3, M3)
            fold(2, R3, M3, C, col("g2", R3), col("be2", R3), "w3_in")
            split(hA, H1, dinv)
            step(v.memset(wreg[:, 288:416], 1.0))
            v.memset(Sflat[:, :], 0.0).then_inc(s["w1_ready"], 1)

            def node_quarters(i, fn):
                for q in range(4):
                    k = 4 * NODE_ORDER[i] + q
                    dve.wait_ge(s["nq_done"], k + 1)
                    n, t0 = QT[q], 6 * q
                    fn(ps[:, 4 + q % 2, 0:n * C].rearrange("p (t f) -> p t f", f=C), t0, n)
                    dve.sem_inc(s["nq_evac"], 1)

            def out_conv(p_, t0, n):
                step(v.tensor_tensor(hY[:, t0:t0 + n, :], p_, bc(dinv[:, t0:t0 + n].unsqueeze(2), [P, n, C]), ALU.mult))
                step(v.tensor_tensor(hY[:, t0:t0 + n, :], hY[:, t0:t0 + n, :], bc(wreg[:, C3:C3 + C].unsqueeze(1), [P, n, C]), ALU.add))

            node_quarters(3, out_conv)
            bn_nodes(1, hY, C, wreg[:, C3 + C:C3 + 2 * C], wreg[:, C3 + 2 * C:C3 + 3 * C])
            step(v.tensor_tensor(X[:, :, :], X[:, :, :], hY, ALU.add))
            dve.wait_ge(s["w4_in"], 144)
            step(diagonal(ALU.subtract))
            dve.sem_inc(s["adj_noi"], 1)
            step(v.tensor_scalar(wreg[0:C2P, C:2 * C], wreg[0:C2P, C:2 * C], half[0:C2P, 0:1], None, ALU.mult))
            step(v.tensor_scalar(wreg[0:C2P, 4 * C:5 * C], wreg[0:C2P, 4 * C:5 * C], half[0:C2P, 0:1], None, ALU.mult))
            step(v.tensor_copy(wreg[:, 288:416], ident16))
            dve.sem_inc(s["w1_ready"], 1)

            def self_term(layer, bB):
                for j in range(7):
                    k = 7 * layer + j
                    n = min(4, NT - 4 * j)
                    dve.wait_ge(s["tr_done"], k + 1)
                    v.tensor_copy(Sflat[0:C, (k % 2) * 512:(k % 2) * 512 + n * P], ps[0:C, 4 + k % 2, 0:n * P]).then_inc(s["tr_evac"], 1)
                    dve.wait_ge(s["self_done"], k + 1)
                    v.tensor_tensor(hY[:, 4 * j:4 * j + n, :], ps[:, 6 + k % 2, 0:n * C].rearrange("p (t f) -> p t f", f=C),
                                    bc(bB.unsqueeze(1), [P, n, C]), ALU.add).then_inc(s["self_evac"], 1)
                dve.wait_ge(s["self_evac"], 7 * layer + 7)

            def sage(dst, relu):
                def fn(p_, t0, n):
                    a = hT[:, t0:t0 + n, :]
                    step(v.tensor_tensor(a, p_, bc(rdeg[:, t0:t0 + n].unsqueeze(2), [P, n, C]), ALU.mult))
                    step(v.tensor_tensor(a, a, hY[:, t0:t0 + n, :], ALU.add))
                    if relu:
                        step(v.tensor_scalar(dst[:, t0:t0 + n, :], a, 0.0, None, ALU.max))
                    else:
                        step(v.tensor_tensor(dst[:, t0:t0 + n, :], dst[:, t0:t0 + n, :], a, ALU.add))
                return fn

            layernorm(hA, hT)
            dve.sem_inc(s["ln_x"], 1)
            self_term(0, wreg[:, 2 * C:3 * C])
            split(hA, H1)
            step(v.memset(Sflat[:, :], 0.0))
            dve.sem_inc(s["padz"], 1)
            node_quarters(4, sage(hA, True))
            dve.sem_inc(s["ln_x"], 1)
            self_term(1, wreg[:, 5 * C:6 * C])
            split(hA, H1)
            step(v.memset(Sflat[:, :], 0.0))
            dve.sem_inc(s["padz"], 1)
            node_quarters(5, sage(X, False))
            layernorm(hA, hT)
            for k, (x, ys) in enumerate(FLIPS):
                dve.wait_ge(s["flip_done"], k + 1)
                ys = [y for y in ys if y != x]
                if not ys:
                    continue
                n, wx = len(ys), min(P, NC - P * x)
                src_ = ps[:, 4 + k % 4, 0:n * 64].bitcast(F16).rearrange("p (j c) -> p j c", j=n)[:, :, 0:wx]
                v.tensor_copy(adj[:, ys[0]:ys[0] + n, P * x:P * x + wx], src_).then_inc(s["flip_cols"], 1)
            dve.wait_ge(s["flip_cols"], FLIP_COLS[-1])
            step(v.memset(H[:, 0:4], 1.0))
            nv = H[:, 8:8 + 4 * NT].rearrange("p (t k) -> p t k", k=4)
            step(v.memset(H[:, 8:8 + 4 * NT], 1.0))
            step(v.tensor_copy(nv[:, :, 1], nvec[:, :]))
            step(v.tensor_tensor(stat[:, 0, :], nvec[:, :], nv[:, :, 1], ALU.subtract))
            step(v.tensor_scalar(nv[:, :, 2], stat[:, 0, :], LOW, None, ALU.mult))
            dve.sem_inc(s["tot_in"], 1)
            dve.wait_ge(s["tot_mm"], 1)
            tr3 = big[0:4, 1200:1200 + NC] if False else Sflat[0:4, 0:SC * 384]
            for c in range(6):
                ins = v.tensor_copy(Sflat[0:4, c * SCW:(c + 1) * SCW], ps[0:4, c, 0:SCW])
            v.tensor_copy(dinv_q[0:4, 0:SCW], ps[0:4, 6, 0:SCW]).then_inc(s["tot_in"], 1)
            dve.wait_ge(s["tot_mm"], 2)
            totp = ps[:, 7, 0:4 * NT].rearrange("p (t k) -> p t k", k=4)
            step(v.memset(stat[:, 1, :], 1.0))
            step(v.memset(rtot[:, :], 1.0))
            for r, a in ((P, slice(0, NT - 1)), (64, slice(NT - 1, NT))):
                step(v.tensor_scalar(stat[0:r, 1, a], totp[0:r, a, 0], 1.0, None, ALU.add))
                step(v.tensor_copy(stat[0:r, 0, a], totp[0:r, a, 1]))
                step(v.scalar_tensor_tensor(rtot[0:r, a], totp[0:r, a, 2], 1.0 / LOW, stat[0:r, 0, a], ALU.mult, ALU.add))
            step(v.tensor_scalar(rtot[:, :], rtot[:, :], 1e-8, None, ALU.max))
            step(v.reciprocal(rtot[:, :], rtot[:, :]))
            sqrt_of(stat[:, 1, :], NT)
            step(v.reciprocal(dinv[:, :], sq[:, 0:NT]))
            diagonal(ALU.add).then_inc(s["adj_t"], 1)
            step(v.memset(Sflat[:, :], 0.0))
            dve.sem_inc(s["padz"], 1)
            split(hA, H1, dinv)

            def light(dst, add):
                def fn(p_, t0, n):
                    a = hT[:, t0:t0 + n, :]
                    step(v.tensor_tensor(a, p_, bc(dinv[:, t0:t0 + n].unsqueeze(2), [P, n, C]), ALU.mult))
                    if add:
                        step(v.tensor_tensor(dst[:, t0:t0 + n, :], dst[:, t0:t0 + n, :], a, ALU.add))
                    else:
                        step(v.tensor_copy(dst[:, t0:t0 + n, :], a))
                return fn

            node_quarters(6, light(hA, False))
            split(hA, H1, dinv)
            node_quarters(7, light(X, True))
            layernorm(hA, hT)
            v.tensor_tensor(hT, hA, bc(nvec[:, :].unsqueeze(2), [P, NT, C]), ALU.mult).then_inc(s["hv_ready"], 1)
            dve.wait_ge(s["late_in"], 48)
            cutoff(lcw, cw_t[:, 0, :], cw_t[:, 1, :], cw_t[:, 2, :], 3)
            step(v.tensor_copy(lsrc, lsrc_i))
            step(v.tensor_scalar(lsrc, lsrc, float(-(NC // 2)), None, ALU.add))
            dve.wait_ge(s["consts"], 5)
            dve.sem_inc(s["l_msg"], 2)
            dve.sem_inc(s["l_res"], 2)

            base = step.n

            def message(b, par, first):
                dve.wait_ge(s[f"l_in{par}"], (b - par) * 16 + 32)
                dve.wait_ge(s[f"l_got{par}"], (b - par) * 32 + 64)
                n0 = b * 4 + base
                dve.wait_ge(s["l_mm"], b + 1)
                v.tensor_tensor(ldot[:, par, :, :], le[:, par, :, :], lh[:, par, :, C:HROW], ALU.mult).then_inc(s["dve_step"], 1)
                for k in range(2):
                    v.tensor_scalar(ohn[:, par, k, :], iota_n, lsrc[:, bass.ds(b * 4 + k, 1)], None, ALU.is_equal)
                dve.wait_ge(s["dve_step"], n0 + 1)
                v.tensor_reduce(la[:, par, :], ldot[:, par, :, :], AX, ALU.add).then_inc(s["dve_step"], 1)
                dve.wait_ge(s["dve_step"], n0 + 2)
                v.tensor_tensor(la[:, par, :], la[:, par, :], lcw[:, bass.ds(b * 4, 4)], ALU.mult).then_inc(s["dve_step"], 1)
                dve.wait_ge(s["dve_step"], n0 + 3)
                v.tensor_tensor(lm[:, par, :, :], lg[:, par, :, :], bc(la[:, par, :].unsqueeze(2), [P, 4, C]), ALU.add).then_inc(s["dve_step"], 1)
                dve.wait_ge(s["dve_step"], n0 + 4)
                v.tensor_tensor(lm[:, par, :, :], lm[:, par, :, :], lh[:, par, :, 0:C], ALU.mult).then_inc(s["l_msg"], 1)
                for k in range(2, 4):
                    ins = v.tensor_scalar(ohn[:, par, k, :], iota_n, lsrc[:, bass.ds(b * 4 + k, 1)], None, ALU.is_equal)
                dve.wait_ge(s["l_hi"], b + 1)
                v.tensor_tensor(lm[:, par, :, :], lm[:, par, :, :], lmh[:, par, :, 0, :], ALU.subtract).then_inc(s["l_res"], 1)

            with dve.Fori(0, NB // 2) as i:
                message(i * 2, 0, False)
                message(i * 2 + 1, 1, False)
            step.n = base + 4 * NB
            dve.wait_ge(s["agg_mm"], 4)
            step(v.tensor_copy(hT, Hf1)) if False else None
            for j in range(3):
                n = min(10, NT - 10 * j)
                step(v.tensor_tensor(hT[:, 10 * j:10 * j + n, :], ps[:, 4 + j, 0:n * C].rearrange("p (t f) -> p t f", f=C),
                                     bc(rtot[:, 10 * j:10 * j + n].unsqueeze(2), [P, n, C]), ALU.mult)) if False else None
            for j in range(3):
                n = min(10, NT - 10 * j)
                step(v.tensor_tensor(hT[:, 10 * j:10 * j + n, :], ps[:, j, 0:n * C].rearrange("p (t f) -> p t f", f=C),
                                     bc(rtot[:, 10 * j:10 * j + n].unsqueeze(2), [P, n, C]), ALU.mult))
            step(v.tensor_tensor(hT, hT, hA, ALU.add))
            layernorm(hY, hA, gamma=1, src=hT)
            dve.wait_ge(s["w6_in"], 32)
            step(v.tensor_tensor(hY, hY, bc(wreg[:, 512:512 + C].unsqueeze(1), [P, NT, C]), ALU.mult))
            step(v.tensor_tensor(hY, hY, bc(wreg[:, 512 + C:512 + 2 * C].unsqueeze(1), [P, NT, C]), ALU.add))
            v.tensor_tensor(X[:, :, :], X[:, :, :], hY, ALU.add).then_inc(s["out_ready"], 1)

        @block.scalar
        def _(act):
            a = nc.scalar
            act.sem_inc(s["silu_done"], 2)
            act.sem_inc(s["win_evac"], 2)
            act.wait_ge(s["t_r"], 1)
            a.activation(tw[:, 4:5], tw[:, 2:3], ACT.Sin).then_inc(s["t_emb"], 1)
            act.wait_ge(s["cw_ready"], 1)
            a.activation(Sflat[:, NCHUNK:2 * NCHUNK], Sflat[:, NCHUNK:2 * NCHUNK], ACT.Sin).then_inc(s["t_emb"], 1)
            act.wait_ge(s["padz"], 1)

            def evac_window(w, par):
                act.wait_ge(s["win_done"], w + 3)
                a.activation(adj[:, :, bass.ds(w * WIN, WIN)], ps[:, par, 0:NT * WIN].rearrange("p (s x) -> p s x", x=WIN),
                             ACT.Copy).then_inc(s["win_evac"], 1)

            def gate_silu(b, par):
                act.wait_ge(s["z_done"], b + 1)
                act.wait_ge(s["gate_done"], b + 1)
                a.activation(silu[0:C, par, :], ps[0:C, 2 + par, :], ACT.Silu, bias=b1c).then_inc(s["silu_done"], 1)

            with act.Fori(0, NWIN // 4) as i:
                gate_silu(i * 2, 0)
                evac_window(i * 4, 0)
                evac_window(i * 4 + 1, 1)
                gate_silu(i * 2 + 1, 1)
                evac_window(i * 4 + 2, 0)
                evac_window(i * 4 + 3, 1)
            with act.Fori(NWIN // 4, NB // 2) as i:
                gate_silu(i * 2, 0)
                gate_silu(i * 2 + 1, 1)
            nsq = [0]

            def sqrt_served(n, rows=P):
                nsq[0] += 1
                act.wait_ge(s["var_ready"], nsq[0])
                a.activation(sq[0:rows, 0:n], sq[0:rows, 0:n], ACT.Sqrt).then_inc(s["std_ready"], 1)

            nsplit = [0]

            def split(val, hview):
                k = nsplit[0] = nsplit[0] + 1
                act.wait_ge(s["h_scaled"], k)
                gs = hview.shape[2]
                for gi in range(gs):
                    ins = a.activation(hview[:, :, gi, 0, :], val[:, :, C * gi:C * gi + C], ACT.Copy)
                ins.then_inc(s["h_hi"], 1)
                act.wait_ge(s["h_res"], k)
                for gi in range(gs):
                    ins = a.activation(hview[:, :, gi, 1, :], val[:, :, C * gi:C * gi + C], ACT.Copy, scale=LOW)
                ins.then_inc(s["h_ready"], 1)

            def evac_quarters(i):
                for q in range(4):
                    u = UNIT0[i] + q
                    act.wait_ge(s["spmm_done"], u + 1)
                    if q >= 2:
                        quarter_used(act, i, q - 2)
                    bank, hw = 2 * (u % 2), QW[q] // 2
                    a.activation(S[0:C2P, q % 2, 0:QW[q]].rearrange("p (c w) -> p c w", c=2), ps[0:C2P, bank:bank + 2, 0:hw],
                                 ACT.Copy).then_inc(s["spmm_evac"], 1)

            def bn_square(k, val, out_sq):
                act.wait_ge(s["bn_cent"], k + 1)
                a.activation(out_sq, val, ACT.Square).then_inc(s["bn_sq"], 1)
                sqrt_served(val.shape[2])

            def relu_blocks(i, rows, m, bias):
                for q in range(4):
                    hw = QW[q] // 2
                    if q or i > 1:
                        act.wait_ge(s["r_stored"], 16 * (4 * (i - 1) + q))
                        act.wait_ge(s["bn_read"], FE0[i] + 2 * m * q)
                    for c in range(2):
                        for mi in range(m):
                            k = FE0[i] + (2 * q + c) * m + mi
                            act.wait_ge(s["fe_done"], k + 1)
                            a.activation(rst[0:rows, mi, c * hw:(c + 1) * hw], ps[0:rows, 4 + k % 4, 0:hw], ACT.Relu,
                                         bias=bias[0:rows, mi:mi + 1]).then_inc(s["fe_evac"], 1)

            sqrt_served(NT)
            sqrt_served(NT)
            split(hA, H1)
            act.wait_ge(s["padz"], 1)
            evac_quarters(0)
            bn_square(0, bigC3, HfC3)
            split(bigC3, H3)
            act.wait_ge(s["bias_ready"], 1)
            relu_blocks(1, R2, M2, bias2)
            sqrt_served(M2, R2)
            split(bigC3, H3)
            relu_blocks(2, R3, M3, bias3)
            sqrt_served(M3, R3)
            split(hA, H1)
            act.wait_ge(s["w1_ready"], 4)
            evac_quarters(3)
            bn_square(1, hY, Hf1)
            sqrt_served(NT)
            split(hA, H1)
            act.wait_ge(s["padz"], 2)
            evac_quarters(4)
            split(hA, H1)
            act.wait_ge(s["padz"], 3)
            evac_quarters(5)
            sqrt_served(NT)
            for k, (x, ys) in enumerate(FLIPS):
                act.wait_ge(s["flip_done"], k + 1)
                wx = min(P, NC - P * x)
                w = min(P * len(ys), NC - P * ys[0])
                a.activation(adj[0:wx, x, P * ys[0]:P * ys[0] + w], ps[0:wx, k % 4, 0:256].bitcast(F16)[:, 0:w],
                             ACT.Copy).then_inc(s["flip_evac"], 1)
            sqrt_served(NT)
            split(hA, H1)
            act.wait_ge(s["padz"], 4)
            evac_quarters(6)
            split(hA, H1)
            evac_quarters(7)
            sqrt_served(NT)
            act.wait_ge(s["cw_ready"], 2)
            a.activation(cw_t[:, 1, :], cw_t[:, 1, :], ACT.Sin).then_inc(s["t_emb"], 1)

            def parts(b, par):
                act.wait_ge(s["l_msg"], b + 3)
                act.wait_ge(s["l_mm"], b + 1)
                a.activation(lmh[:, par, :, 0, :], lm[:, par, :, :], ACT.Copy).then_inc(s["l_hi"], 1)
                act.wait_ge(s["l_res"], b + 3)
                a.activation(lmh[:, par, :, 1, :], lm[:, par, :, :], ACT.Copy, scale=LOW).then_inc(s["l_lo"], 1)

            with act.Fori(0, NB // 2) as i:
                parts(i * 2, 0)
                parts(i * 2 + 1, 1)
            act.wait_ge(s["l_mm"], NB + 2)
            for c in range(SC):
                ins = a.activation(aggS[0:C2P, c * SCW:(c + 1) * SCW], ps[0:C2P, c, 0:SCW], ACT.Copy)
            ins = a.activation(aggS[0:C2P, NC:NP], ps[0:C2P, 0, 0:NP - NC], ACT.Copy, scale=0.0).then_inc(s["agg_evac"], 1)
            sqrt_served(NT)

        @block.tensor
        def _(pe):
            mm = nc.tensor.matmul
            for nm, n in (("win_done", 2), ("gate_done", 2), ("l_mm", 2)):
                pe.sem_inc(s[nm], n)
            pe.wait_ge(s["in_small"], 16 * 22)
            pe.wait_ge(s["t_emb"], 1)
            mm(ps[:, 0, 0:1], wtm, tw[:, 4:5], start=True, stop=True).then_inc(s["t_mm1"], 1)
            pe.wait_ge(s["t_rel"], 1)
            for m in range(M2):
                mm(ps[0:R2, 1, m:m + 1], wt1[:, m * R2:(m + 1) * R2], tw[:, 5:6], start=True, stop=True)
            for m in range(M3):
                ins = mm(ps[0:R3, 1, M2 + m:M2 + m + 1], wt2[:, m * R3:(m + 1) * R3], tw[:, 5:6], start=True, stop=True)
            ins.then_inc(s["t_mm2"], 1)
            mm(ps[0:NEL, 2, 0:GD], embT, adaT, start=True, stop=True).then_inc(s["tables_T"], 1)
            pe.wait_ge(s["tables_tt"], 1)
            pe.wait_ge(s["t_onehot"], 1)
            for j in range(4):
                n = min(8, NT - 8 * j)
                for t in range(8 * j, 8 * j + n):
                    ins = mm(ps[:, 4 + j, 64 * (t % 8):64 * (t % 8) + 64], onehot_t[0:NEL, P * t:P * t + P], tt12, start=True, stop=True)
                ins.then_inc(s["t_mm"], 1)
            pe.wait_ge(s["c0_cmp"], 4)
            pe.wait_ge(s["ones_row"], 1)
            for k in range(4):
                ins = mm(ps[0:1, 3, 0:NWIN], ones1[0:104, :], cmp_w[:, k, :], start=(k == 0), stop=(k == 3))
            ins.then_inc(s["c0_sum"], 1)
            pe.wait_ge(s["c0_ready"], 1)
            pe.wait_ge(s["bias_ready"], 1)
            pe.wait_ge(s["t_evac"], 4)

            def window(w, par):
                pe.wait_ge(s["onehots_built"], w + 4)
                pe.wait_ge(s["win_evac"], w + 1)
                for k in range(WCH):
                    ins = mm(ps[:, par, 0:NT * WIN], sta[:, par, k, :], mov[:, par, k, :], start=(k == 0), stop=(k == WCH - 1))
                ins.then_inc(s["win_done"], 1)

            def gate_hidden(b, par):
                pe.wait_ge(s[f"attr_in{par}"], (b - par) * 8 + 16)
                pe.wait_ge(s["silu_done"], b + 1)
                mm(ps[:, 2 + par, :], w1t, attr[:, par, :], start=True, stop=True).then_inc(s["z_done"], 1)

            def gate_product(b, par):
                pe.wait_ge(s["silu_done"], b + 3)
                pe.wait_ge(s["g_evac"], b + 1)
                for k in range(4):
                    ins = mm(ps[:, 4 + par, C * k:C * k + C], silu[:, par, P * k:P * k + P], w2b, start=True, stop=True)
                ins.then_inc(s["gate_done"], 1)

            with pe.Fori(0, NWIN // 4) as i:
                gate_hidden(i * 2, 0)
                window(i * 4, 0)
                window(i * 4 + 1, 1)
                gate_product(i * 2, 0)
                gate_hidden(i * 2 + 1, 1)
                window(i * 4 + 2, 0)
                window(i * 4 + 3, 1)
                gate_product(i * 2 + 1, 1)
            with pe.Fori(NWIN // 4, NB // 2) as i:
                gate_hidden(i * 2, 0)
                gate_hidden(i * 2 + 1, 1)
                gate_product(i * 2, 0)
                gate_product(i * 2 + 1, 1)
            pe.wait_ge(s["g_evac"], NB + 2)
            pe.wait_ge(s["adj_i"], 1)
            pe.wait_ge(s["deg_h"], 1)
            for t in range(NT):
                for c in range(SC):
                    ins = mm(ps[0:1, c, 0:SCW], ones16[:, 0:1], adj[:, t, c * SCW:(c + 1) * SCW], start=(t == 0), stop=(t == NT - 1))
            ins.then_inc(s["deg_mm"], 1)
            pe.wait_ge(s["deg_row"], 1)
            for t in range(NT):
                wd = min(P, NC - P * t)
                ins = mm(ps[0:wd, 7, t:t + 1], degrow[:, P * t:P * t + wd], ones1[0:1, 0:1], start=True, stop=True)
            ins.then_inc(s["deg_tr"], 1)

            def spmm(i, q, gi, hview):
                u = UNIT0[i] + (3 * q + gi if GROUPS[i] == 3 else q)
                if q == 0 and gi == 0:
                    pe.wait_ge(s["h_ready"], i + 1)
                if u >= 2:
                    pe.wait_ge(s["spmm_evac"], u - 1)
                bank, hw = 2 * (u % 2), QW[q] // 2
                for t in range(NT):
                    for c in range(2):
                        ins = mm(ps[0:C2P, bank + c, 0:hw], hview[:, t, gi, :, :].rearrange("p h f -> p (h f)"),
                                 adj[:, t, QCOL[q] + c * hw:QCOL[q] + (c + 1) * hw], start=(t == 0), stop=(t == NT - 1))
                ins.then_inc(s["spmm_done"], 1)
                return u

            pe.wait_ge(s["n1_evac"], 0) if False else None

            def conv1_tiles(q):
                pe.wait_ge(s["spmm_evac"], q + 1)
                for j in range(QT[q]):
                    t = 6 * q + j
                    if t == 0:
                        pe.wait_ge(s["w1_ready"], 1)
                    if t >= 4:
                        pe.wait_ge(s["n1_evac"], t - 3)
                    ins = mm(ps[:, 4 + t % 4, 0:C3], S[0:C2P, q % 2, P * j:P * j + P], wreg[0:C2P, 0:C3], start=True, stop=True)
                    ins.then_inc(s["n1_done"], 1)

            def bn_sums(k, val, sqv, F, evac_sem, evac_n):
                pe.wait_ge(evac_sem, evac_n)
                on = wreg[:, 576:704] if k == 0 else wreg[:, 288:416]
                for part, bank in ((0, 4), (1, 5)):
                    if part:
                        pe.wait_ge(s["bn_sq"], k + 1)
                    x_ = sqv if part else val
                    for t in range(NT):
                        r = P if t < NT - 1 else TAIL
                        ins = mm(ps[:, bank, 0:F], on[0:r, :], x_[0:r, t, :], start=(t == 0), stop=(t == NT - 1))
                    ins.then_inc(s["bn_mm"], 1)

            for q in range(4):
                spmm(0, q, 0, H1)
                if q:
                    conv1_tiles(q - 1)
            conv1_tiles(3)
            bn_sums(0, bigC3, HfC3, C3, s["n1_evac"], NT)

            def feature_blocks(i, q, rows, m, wv):
                pe.wait_ge(s["spmm_evac"], UNIT0[i] + 3 * q + 3)
                if q == 0:
                    pe.wait_ge(s["w1_ready"], i + 1)
                hw = QW[q] // 2
                for c in range(2):
                    for mi in range(m):
                        k = FE0[i] + (2 * q + c) * m + mi
                        if k >= 4:
                            pe.wait_ge(s["fe_evac"], k - 3)
                        for gi in range(3):
                            ins = mm(ps[0:rows, 4 + k % 4, 0:hw], wv[0:C2P, gi, mi * rows:(mi + 1) * rows], S[0:C2P, gi, c * hw:(c + 1) * hw],
                                     start=(gi == 0), stop=(gi == 2))
                        ins.then_inc(s["fe_done"], 1)

            def feature_conv(i, rows, m, wv):
                for q in range(4):
                    spmm(i, q, 0, H3)
                    if q:
                        feature_blocks(i, q - 1, rows, m, wv)
                    spmm(i, q, 1, H3)
                    spmm(i, q, 2, H3)
                feature_blocks(i, 3, rows, m, wv)

            def folded(i, rows, m, F):
                pe.wait_ge(s["fold_t"], i)
                pe.wait_ge(*((s["w2_in"], 16) if i == 1 else (s["w3_in"], 64)))
                pe.wait_ge(s["fe_evac"], FE0[i] + 8 * m)
                for mi in range(m):
                    ins = mm(ps[:, 4, 0:F], Hf[0:rows, mi * P:(mi + 1) * P], wreg[0:rows, mi * F:(mi + 1) * F], start=(mi == 0), stop=(mi == m - 1))
                ins.then_inc(s["fold_mm"], 1)
                pe.wait_ge(s["fold_w"], i)
                for t in range(NT):
                    k = NT * (i - 1) + t
                    uses = 16 * ((i - 1) * len(range(t % 4, NT, 4)) + t // 4 + 1)
                    pe.wait_ge(s[f"ring{t % 4}"], uses)
                    if t >= 4:
                        pe.wait_ge(s["cv_evac"], k - 3)
                    for mi in range(m):
                        lhs = Sflat[0:rows, (t % 4) * 512 + mi * P:(t % 4) * 512 + (mi + 1) * P]
                        ins = mm(ps[:, 4 + t % 4, 0:F], lhs, wreg[0:rows, mi * F:(mi + 1) * F], start=(mi == 0), stop=(mi == m - 1))
                    ins.then_inc(s["cv_done"], 1)

            feature_conv(1, R2, M2, wreg[:, :].rearrange("p (g f) -> p g f", g=3))
            folded(1, R2, M2, C3)
            feature_conv(2, R3, M3, wreg[:, 720:1152].rearrange("p (g f) -> p g f", g=3))
            folded(2, R3, M3, C)

            def node_tiles(i, q, wv):
                k = 4 * NODE_ORDER[i] + q
                pe.wait_ge(s["spmm_evac"], UNIT0[i] + q + 1)
                if k >= 2:
                    pe.wait_ge(s["nq_evac"], k - 1)
                for j in range(QT[q]):
                    ins = mm(ps[:, 4 + q % 2, C * j:C * j + C], S[0:C2P, q % 2, P * j:P * j + P], wv, start=True, stop=True)
                ins.then_inc(s["nq_done"], 1)

            def node_conv(i, wv):
                for q in range(4):
                    spmm(i, q, 0, H1)
                    if q:
                        node_tiles(i, q - 1, wv)
                node_tiles(i, 3, wv)

            node_conv(3, comb[0:C2P, :])
            bn_sums(1, hY, Hf1, C, s["nq_evac"], 4)

            def self_product(layer, wv):
                pe.wait_ge(s["ln_x"], layer + 1)
                if layer == 0:
                    pe.wait_ge(s["w1_ready"], 5)
                idf = wreg[:, 288:416]
                for j in range(7):
                    k = 7 * layer + j
                    n = min(4, NT - 4 * j)
                    if k >= 2:
                        pe.wait_ge(s["self_evac"], k - 1)
                    for t in range(n):
                        ins = nc.tensor.transpose(ps[0:C, 4 + k % 2, P * t:P * t + P], hA[:, 4 * j + t, :], idf)
                    ins.then_inc(s["tr_done"], 1)
                    pe.wait_ge(s["tr_evac"], k + 1)
                    for t in range(n):
                        ins = mm(ps[:, 6 + k % 2, C * t:C * t + C], Sflat[0:C, (k % 2) * 512 + t * P:(k % 2) * 512 + t * P + P], wv, start=True, stop=True)
                    ins.then_inc(s["self_done"], 1)

            pe.wait_ge(s["adj_noi"], 1)
            self_product(0, wreg[0:C, 0:C])
            node_conv(4, wreg[0:C2P, C:2 * C])
            self_product(1, wreg[0:C, 3 * C:4 * C])
            node_conv(5, wreg[0:C2P, 4 * C:5 * C])
            pe.wait_ge(s["nq_evac"], 12)
            id16 = ident16
            for k, (x, ys) in enumerate(FLIPS):
                if k >= 4:
                    pe.wait_ge(s["flip_evac"], k - 3)
                    if FLIP_COLS[k - 4]:
                        pe.wait_ge(s["flip_cols"], FLIP_COLS[k - 4])
                wx = min(P, NC - P * x)
                rows_ = ps[:, k % 4, 0:256].bitcast(F16)
                cols_ = ps[:, 4 + k % 4, 0:256].bitcast(F16)
                for j, y in enumerate(ys):
                    if y != x:
                        nc.tensor.transpose(cols_[:, P * j:P * j + P], adj[:, x, P * y:P * y + P], id16)
                    ins = nc.tensor.transpose(rows_[0:wx, P * j:P * j + P], adj[:, y, P * x:P * x + wx], id16)
                ins.then_inc(s["flip_done"], 1)
            pe.wait_ge(s["flip_evac"], len(FLIPS))
            pe.wait_ge(s["tot_in"], 1)
            nv = H[:, 8:8 + 4 * NT].rearrange("p (t k) -> p t k", k=4)
            for t in range(NT):
                for c in range(SC):
                    ins = mm(ps[0:4, c, 0:SCW], nv[:, t, :], adj[:, t, c * SCW:(c + 1) * SCW], start=(t == 0), stop=(t == NT - 1))
            ins.then_inc(s["tot_mm"], 1)
            pe.wait_ge(s["tot_in"], 2)
            for t in range(NT):
                wd = min(P, NC - P * t)
                at, done = P * t, 0
                srcs = Sflat[0:4, at:at + wd] if at + wd <= 6 * SCW else dinv_q[0:4, at - 6 * SCW:at - 6 * SCW + wd]
                ins = mm(ps[0:wd, 7, 4 * t:4 * t + 4], srcs, wreg[0:4, 288:292], start=True, stop=True)
            ins.then_inc(s["tot_mm"], 1)
            pe.wait_ge(s["adj_t"], 1)
            node_conv(6, comb[0:C2P, :])
            node_conv(7, comb[0:C2P, :])

            def scatter(b, par, first, last):
                pe.wait_ge(s["l_res"], b + 3)
                pe.wait_ge(s["l_lo"], b + 1)
                for k in range(4):
                    for c in range(SC):
                        ins = mm(ps[0:C2P, c, 0:SCW], lmh[:, par, k, :, :].rearrange("p h f -> p (h f)"), ohn[:, par, k, c * SCW:(c + 1) * SCW],
                                 start=(first and k == 0), stop=(last and k == 3))
                ins.then_inc(s["l_mm"], 1)

            pe.wait_ge(s["nq_evac"], 20)
            scatter(0, 0, True, False)
            scatter(1, 1, False, False)
            with pe.Fori(1, NB // 2 - 1) as i:
                scatter(i * 2, 0, False, False)
                scatter(i * 2 + 1, 1, False, False)
            scatter(NB - 2, 0, False, False)
            scatter(NB - 1, 1, False, True)
            pe.wait_ge(s["agg_evac"], 1)
            for t in range(NT):
                ins = mm(ps[:, t // 10, C * (t % 10):C * (t % 10) + C], aggS[0:C2P, P * t:P * t + P], comb[0:C2P, :], start=True, stop=True)
            ins.then_inc(s["agg_mm"], 4)


def kernel(**x):
    import concourse.bacc as _bacc
    from concourse.bass_utils import run_bass_kernel_spmd as _run

    def arr(name):
        return np.asarray(x[name])

    def by_chunk(a, fill):
        full = np.full(EP, fill, a.dtype)
        full[:E] = a
        return np.ascontiguousarray(full.reshape(NCHUNK, P).T)

    def by_tile(a):
        full = np.zeros(NP, a.dtype)
        full[:N] = a
        return np.ascontiguousarray(full.reshape(NT, P).T)

    def by_block(a, m):
        return np.ascontiguousarray(a.reshape(m, -1).T)

    xp = np.zeros((NP, C), np.float32)
    xp[:N] = arr("x")
    types = np.zeros(NP, np.int32)
    types[:N] = arr("node_type_119")
    attr = np.zeros((RBF, EP), np.float32)
    attr[:, :E] = arr("edge_attr_40").T
    freqs = np.exp(np.arange(64, dtype=np.float32) * np.float32(-np.log(10000.0) / 63)).astype(np.float32)
    L0, L1, L3 = "L0_gnn_", "L1_gnn_", "L3_gnn_"
    ins = {
        "x": xp, "src": by_chunk(arr("src"), NP - 1), "dst": by_chunk(arr("dst"), NP - 1),
        "edge_attr": attr, "edge_weight": by_chunk(arr("edge_weight"), 0.0),
        "node_type": types, "node_vec": by_tile(arr("node_vec")),
        "freq": np.concatenate([freqs, freqs]), "timestep": arr(L0 + "timestep"),
        "Wtm": arr(L0 + "Wtm"), "btm": arr(L0 + "btm"), "W_in": arr(L0 + "W_in"), "b_in": arr(L0 + "b_in"),
        "g_in": arr(L0 + "g_in"), "be_in": arr(L0 + "be_in"), "Wt1": arr(L0 + "Wt1"), "Wt2": arr(L0 + "Wt2"),
        "Wc1": arr(L0 + "Wc1"), "Wc2": arr(L0 + "Wc2"), "W_out": arr(L0 + "W_out"), "b_out": arr(L0 + "b_out"),
        "g_out": arr(L0 + "g_out"), "be_out": arr(L0 + "be_out"),
        "W_self1": arr(L1 + "W_self1"), "W_neigh1": arr(L1 + "W_neigh1"), "sb1": arr(L1 + "b1"),
        "W_self2": arr(L1 + "W_self2"), "W_neigh2": arr(L1 + "W_neigh2"), "sb2": arr(L1 + "b2"),
        "W1T": arr(L3 + "W1").T, "b1": arr(L3 + "b1"), "W2T": arr(L3 + "W2").T, "b2": arr(L3 + "b2"),
        "emb": arr(L3 + "emb"), "embT": arr(L3 + "emb").T, "adaT": arr(L3 + "adaptW").T,
        "gamma": arr(L3 + "gamma"), "beta": arr(L3 + "beta"),
    }
    for nm in ("bc1", "bt1", "g1", "be1"):
        ins[nm] = by_block(arr(L0 + nm), M2)
    for nm in ("bc2", "bt2", "g2", "be2"):
        ins[nm] = by_block(arr(L0 + nm), M3)

    nc = _bacc.Bacc("TRN2", target_bir_lowering=False, num_devices=1)
    arrays, aps = {}, {}
    for name, a in ins.items():
        a = np.ascontiguousarray(a)
        arrays["in_" + name] = a
        aps[name] = nc.dram_tensor("in_" + name, a.shape, mybir.dt.from_np(a.dtype), kind="ExternalInput").ap()
    out = nc.dram_tensor("out_0", [N, C], F32, kind="ExternalOutput").ap()
    build(nc, aps, out)
    r = _run(nc, [arrays], core_ids=[0])
    return r.results[0]["out_0"]
```

```python
from contextlib import ExitStack

import numpy as np

import concourse.bass as bass
from concourse import mybir

F32 = mybir.dt.float32
F16 = mybir.dt.float16
I32 = mybir.dt.int32
ALU = mybir.AluOpType
ACT = mybir.ActivationFunctionType
AX = mybir.AxisListType.X

N, E, C, RBF, NEL, GD = 3125, 53125, 48, 40, 119, 32
P = 128
NT = -(-N // P)
NP = NT * P
TAIL = N - (NT - 1) * P
C3, C9 = 3 * C, 9 * C
C2P = 2 * C
EPS = 1e-5
LOW = 4096.0

WIN = 16
NWIN = -(-N // WIN)
NC = NWIN * WIN
CODE = 64
WCH = 4
NCHUNK = 4 * (-(-E // 512))
EP = NCHUNK * P
NB = NCHUNK // 4

QT = [6, 6, 6, 7]
QCOL = [0, 768, 1536, 2304]
QW = [768, 768, 768, NC - 2304]
QMAX = max(QW)
SW = 7 * P
M2, M3 = 4, 2
R2, R3 = C9 // M2, C3 // M3
HALF = NC // 2
SC = 7
SCW = NC // SC
HROW = C + GD + 2
CA = C + 1


def two_pi_parts():
    a = 6.28125
    b = float(np.float32(2 * np.pi - a))
    return a, b, float(2 * np.pi - a - b)


def build(nc, d, out):
    with ExitStack() as ctx:
        def sb(name, shape, dt):
            return ctx.enter_context(nc.sbuf_tensor(name, shape, dt))

        def sem(name):
            return ctx.enter_context(nc.semaphore(name))

        adj = sb("adj", [P, NT, NC], F16)
        big = sb("big", [P, 3600], F32)
        H = sb("H", [P, 7200], F16)
        S = sb("S", [P, 3, SW], F32)
        X = sb("X", [P, NT, C], F32)
        dinv_q = sb("dinv_q", [P, QMAX], F32)
        wreg = sb("wreg", [P, 1296], F32)
        bnst = sb("bnst", [P, M2, 8, 6], F32)
        mv = sb("mv", [P, M2, 2], F32)
        dinv = sb("dinv", [P, NT], F32)
        rdeg = sb("rdeg", [P, NT], F32)
        nvec = sb("nvec", [P, NT], F32)
        rtot = sb("rtot", [P, NT], F32)
        stat = sb("stat", [P, 2, NT], F32)
        sq = sb("sq", [P, C3], F32)
        comb = sb("comb", [P, C], F32)
        pidx = sb("pidx", [P, 1], F32)
        half = sb("half", [P, 1], F32)
        cols = sb("cols", [P, 31], F32)
        bias2 = sb("bias2", [P, M2], F32)
        bias3 = sb("bias3", [P, M3], F32)
        e1st = sb("e1st", [P, 2, 2, GD], F32)
        e1ix = sb("e1ix", [P, 2, 4], I32)
        ps = ctx.enter_context(nc.psum_tensor("ps", [P, 8, 512], F32))

        G_d = nc.dram_tensor("gate_edges", [NB, P, 4 * C], F32, kind="Internal").ap()
        E1_d = nc.dram_tensor("emb_src_edges", [NB, P, 4 * GD], F32, kind="Internal").ap()
        TN1_d = nc.dram_tensor("emb_nodes", [NP, GD], F32, kind="Internal").ap()
        HV_d = nc.dram_tensor("hv_nodes", [NP, HROW], F32, kind="Internal").ap()
        DI_d = nc.dram_tensor("dinv_row", [NP], F32, kind="Internal").ap()
        R2_d = nc.dram_tensor("relu2", [R2, M2, NC], F32, kind="Internal").ap()
        R3_d = nc.dram_tensor("relu3", [R3, M3, NC], F32, kind="Internal").ap()

        ID_d = nc.dram_tensor("identity", [P, P], F16, kind="Internal").ap()

        bigC3 = big[:, :].rearrange("p (t f) -> p t f", f=C3)
        hA = big[:, 0:1200].rearrange("p (t f) -> p t f", f=C)
        hT = big[:, 1200:2400].rearrange("p (t f) -> p t f", f=C)
        hY = big[:, 2400:3600].rearrange("p (t f) -> p t f", f=C)
        H1 = H[:, 0:2400].rearrange("p (t g h f) -> p t g h f", g=1, h=2, f=C)
        H3 = H[:, :].rearrange("p (t g h f) -> p t g h f", g=3, h=2, f=C)
        Hf = H[:, :].bitcast(F32)
        HfC3 = Hf.rearrange("p (t f) -> p t f", f=C3)
        Hf1 = Hf[:, 0:1200].rearrange("p (t f) -> p t f", f=C)
        rst = big[:, 0:M2 * QMAX].rearrange("p (m w) -> p m w", w=QMAX)
        Sflat = S[:, :, :].rearrange("p a b -> p (a b)")
        early = adj[:, :, :].rearrange("p a b -> p (a b)").bitcast(F32)
        typ = early[:, 0:NP].bitcast(I32)
        onehot_t = early[:, NP:2 * NP]
        tn = early[:, 2 * NP:2 * NP + NT * 66].rearrange("p (t f) -> p t f", f=66)
        nv_hi = early[:, 2 * NP + NT * 66:2 * NP + NT * 67].bitcast(F16)[:, 0:NT]
        nv_lo = early[:, 2 * NP + NT * 67:2 * NP + NT * 68].bitcast(F16)[:, 0:NT]
        wtm = wreg[:, 0:128]
        wt1 = wreg[:, 128:560]
        wt2 = wreg[:, 560:704]
        embT = wreg[0:GD, 704:704 + NEL]
        adaT = wreg[0:GD, 824:824 + GD]
        tt12 = wreg[0:NEL, 856:856 + 64]
        w1t = wreg[0:RBF, 1168:1296]
        w2b = wreg[0:C + 1, 968:1016]
        b1c = wreg[0:C, 1016:1017]
        tw = wreg[:, 1020:1040]
        ident16 = wreg[:, 1040:1104].bitcast(F16)
        iota16 = wreg[:, 1104:1168].bitcast(F16)
        dst_i = big[:, 0:NCHUNK].bitcast(I32)
        src_i = big[:, NCHUNK:2 * NCHUNK].bitcast(I32)
        c0i = big[0:1, 2 * NCHUNK:2 * NCHUNK + NWIN].bitcast(I32)
        dst_f = big[:, 1200:1200 + NCHUNK]
        hi_f = big[:, 1200 + NCHUNK:1200 + 2 * NCHUNK]
        lo_f = big[:, 1200 + 2 * NCHUNK:1200 + 3 * NCHUNK]
        cw = big[:, 1200 + 3 * NCHUNK:1200 + 4 * NCHUNK]
        wtab = big[:, 2864:2864 + NWIN]
        key = big[:, 3060:3060 + 48].rearrange("p (b t w k) -> p b t w k", b=2, t=3, w=2)
        last_i = big[0:104, 3108:3112].bitcast(I32)
        last_f = big[0:104, 3112:3116]
        ones1 = big[:, 3116:3117]
        rowsum = big[:, 3117:3118]
        flag_f = big[0:1, 3118:3119]
        flag_i = big[0:1, 3119:3120].bitcast(I32)
        gst = big[:, 3216:3600].rearrange("p (b f) -> p b f", b=2)
        mov = H[:, 0:3200].rearrange("p (b k n) -> p b k n", b=2, k=WCH)
        sta = H[:, 3200:4224].rearrange("p (b k n) -> p b k n", b=2, k=WCH)
        iota_w = dinv_q[:, 0:200].bitcast(F16)
        c0f = Hf[0:1, 3200:3200 + NWIN]
        degrow = H[0:1, 4224:4224 + 6 * SCW]
        degrow_end = dinv_q[0:1, 400:400 + SCW // 2].bitcast(F16)
        all_keys = Hf[:, 2400:2400 + NCHUNK]
        cmp_w = Hf[0:104, 2320:2320 + NWIN * 4].rearrange("p (g w) -> p g w", g=4)
        attr = Sflat[0:RBF, 0:1024].rearrange("p (b e) -> p b e", b=2)
        silu = Sflat[0:C + 1, 1024:2048].rearrange("p (b e) -> p b e", b=2)
        ones16 = dinv_q[:, 200:201].bitcast(F16)
        af = adj[:, :, :].rearrange("p a b -> p (a b)").bitcast(F32)
        iota_n = adj[:, 0, :]
        ohn = adj[:, 1:9, :].rearrange("p (b k) n -> p b k n", b=2)
        o0 = 9 * NC // 2
        ldst = af[:, o0:o0 + NCHUNK].bitcast(I32)
        lsrc_i = af[:, o0 + NCHUNK:o0 + 2 * NCHUNK].bitcast(I32)
        lsrc = af[:, o0 + 2 * NCHUNK:o0 + 3 * NCHUNK]
        lcw = af[:, o0 + 3 * NCHUNK:o0 + 4 * NCHUNK]
        o1 = o0 + 4 * NCHUNK

        def late(words):
            nonlocal o1
            o1 += words
            return af[:, o1 - words:o1]

        lg = late(8 * C).rearrange("p (b k f) -> p b k f", b=2, k=4)
        le = late(8 * GD).rearrange("p (b k f) -> p b k f", b=2, k=4)
        lh = late(8 * HROW).rearrange("p (b k f) -> p b k f", b=2, k=4)
        ldot = late(8 * GD).rearrange("p (b k f) -> p b k f", b=2, k=4)
        la = late(8).rearrange("p (b k) -> p b k", b=2)
        lm = late(8 * C).rearrange("p (b k f) -> p b k f", b=2, k=4)
        lmh = late(8 * CA).bitcast(F16).rearrange("p (b k h f) -> p b k h f", b=2, k=4, h=2)
        lix = late(8).bitcast(I32).rearrange("p (b k) -> p b k", b=2)
        aggS = late(NP)
        cw_t = late(3 * NCHUNK).rearrange("p (k n) -> p k n", k=3)
        combA = wreg[0:2 * CA, 0:CA]

        CB = {}
        at = 0
        for nm, w in (("btm", 1), ("freq", 1), ("bc1", M2), ("bt1", M2), ("g1", M2), ("be1", M2),
                      ("bc2", M3), ("bt2", M3), ("g2", M3), ("be2", M3), ("tstep", 1)):
            CB[nm] = (at, w)
            at += w

        def col(nm, rows=P):
            a, w = CB[nm]
            return cols[0:rows, a:a + w]

        names = """in_small in_edges in_types in_x in_cw tables_tt tables_T t_onehot t_mm t_evac tn_stored
            consts ones_row c0_cmp c0_sum c0_ready keys_prep dve_step act_step pool_step
            t_emb t_mm1 t_rel t_mm2 bias_ready t_r
            key_ready onehots_built win_done win_evac
            attr_in0 attr_in1 z_done silu_done gate_done g_evac gstored0 gstored1 cw_ready
            pool_passed ones_ready deg_mm deg_row deg_tr rows_summed total_mm total_ready all_keys_ready all_onehots0 all_onehots1 all_used0 all_used1 all_step all_step_passed
            all_evac all_deg deg_col dinv_stored dinv_in
            var_ready std_ready h_scaled h_hi h_res h_ready spmm_done spmm_evac
            n1_done n1_evac nq_done nq_evac fe_done fe_evac r_stored bn_read
            bn_in bn_mm bn_cent bn_sq bn_aff
            w0_in w1_in w1_ready w2_in w3_in w4_in w5_in w6_in w7_in fold_t fold_mm fold_w ring0 ring1 ring2 ring3
            cv_done cv_evac tr_done tr_evac self_done self_evac
            ident_ready ident_kept flip_done flip_evac flip_cols adj_i adj_noi adj_t e1_in0 e1_in1 e1_got0 e1_got1 e1_st0 e1_st1
            hv_ready hv_stored late_in lcw_ready l_in0 l_in1 l_got0 l_got1 l_msg l_hi l_res l_lo l_oh l_mm
            agg_evac agg_mm out_ready out_done relu_in relu_out padz ln_x""".split()
        s = {n: sem(n) for n in names}

        class Chain:

            def __init__(self, eng, semaphore):
                self.eng, self.sem, self.n = eng, semaphore, 0

            def __call__(self, instruction):
                self.n += 1
                instruction.then_inc(self.sem, 1)
                self.eng.wait_ge(self.sem, self.n)

        block = ctx.enter_context(nc.Block())
        GCN_FEATURE = (1, 2)
        GROUPS = [1, 3, 3, 1, 1, 1, 1, 1]
        UNIT0 = [4 * sum(GROUPS[:i]) for i in range(9)]
        NODE_ORDER = {3: 0, 4: 1, 5: 2, 6: 3, 7: 4}
        FLIPS = [(x, list(range(y, min(y + 4, x + 1)))) for x in range(NT) for y in range(0, x + 1, 4)]
        FLIP_COLS = [sum(any(y != x for y in ys) for x, ys in FLIPS[:k + 1]) for k in range(len(FLIPS))]
        FE0 = {1: 0, 2: 4 * 2 * M2}

        def quarter_used(eng, i, q):
            if i == 0:
                eng.wait_ge(s["n1_done"], sum(QT[:q + 1]))
            elif i in GCN_FEATURE:
                eng.wait_ge(s["fe_done"], FE0[i] + 2 * (M2 if i == 1 else M3) * (q + 1))
            else:
                eng.wait_ge(s["nq_done"], 4 * NODE_ORDER[i] + q + 1)

        def bc(ap, n):
            return ap.broadcast_to(n)

        @block.sync
        def _(sp):
            def pb(name, n=P):
                return d[name][None, :].broadcast_to([n, d[name].shape[0]])

            small = [(wtm, d["Wtm"]), (wt1, d["Wt1"]), (wt2, d["Wt2"]), (embT, d["embT"]), (adaT, d["adaT"]),
                     (tt12[:, 0:GD], d["emb"]), (w1t[:, 0:C], d["W1T"]), (w2b[0:C, :], d["W2T"]),
                     (w2b[C:C + 1, :], d["b2"][None, :]), (b1c, d["b1"][:, None]),
                     (col("btm"), d["btm"][:, None]), (col("freq"), d["freq"][:, None]),
                     (col("tstep"), d["timestep"][None, :].broadcast_to([P, 1])), (nvec[:, :], d["node_vec"])]
            for nm, r in (("bc1", R2), ("bt1", R2), ("g1", R2), ("be1", R2),
                          ("bc2", R3), ("bt2", R3), ("g2", R3), ("be2", R3)):
                small.append((col(nm, r), d[nm]))
            sp.dma_start(dst_i, d["dst"]).then_inc(s["in_edges"], 16)
            sp.dma_start(src_i, d["src"]).then_inc(s["in_edges"], 16)
            sp.dma_start(last_i, d["dst"][P - 1:P, :].rearrange("o (p g) -> (o p) g", g=4)).then_inc(s["in_edges"], 16)
            sp.dma_start(cw, d["edge_weight"]).then_inc(s["in_cw"], 16)
            for o, i in small:
                sp.dma_start(o, i).then_inc(s["in_small"], 16)
            sp.dma_start(typ[0:NEL, :], d["node_type"][None, :].broadcast_to([NEL, NP])).then_inc(s["in_types"], 16)
            sp.dma_start(X[:, :, :], d["x"].rearrange("(t p) f -> p t f", p=P)).then_inc(s["in_x"], 16)
            sp.wait_ge(s["ident_ready"], 1)
            sp.dma_start(ID_d, ident16).then_inc(s["ident_kept"], 16)
            sp.wait_ge(s["t_evac"], 4)
            sp.dma_start(TN1_d.rearrange("(t p) f -> p t f", p=P), tn[:, :, 0:GD]).then_inc(s["tn_stored"], 16)
            sp.dma_start(HV_d[:, C:HROW].rearrange("(t p) f -> p t f", p=P), tn[:, :, GD:2 * GD + 2]).then_inc(s["tn_stored"], 16)
            sp.wait_ge(s["padz"], 1)

            def load_attr(b, par):
                sp.wait_ge(s["silu_done"], b + 1)
                sp.dma_start(attr[:, par, :], d["edge_attr"][:, bass.ds(b * 512, 512)]).then_inc(s[f"attr_in{par}"], 16)

            def store_gate(b, par):
                sp.wait_ge(s["g_evac"], b + 3)
                sp.dma_start(G_d[bass.ds(b, 1), :, :].rearrange("o p f -> (o p) f"), gst[:, par, :]).then_inc(s[f"gstored{par}"], 16)

            w = wreg
            for o, i in ((w[0:C, 0:C3], d["W_in"]), (w[C:C2P, 0:C3], d["W_in"]), (w[:, C3:2 * C3], pb("b_in")),
                         (w[:, 2 * C3:3 * C3], pb("g_in")), (w[:, 3 * C3:4 * C3], pb("be_in"))):
                sp.dma_start(o, i).then_inc(s["w0_in"], 16)
            load_attr(0, 0)
            load_attr(1, 1)
            with sp.Fori(0, NB // 2 - 1) as i:
                load_attr(i * 2 + 2, 0)
                load_attr(i * 2 + 3, 1)
                store_gate(i * 2, 0)
                store_gate(i * 2 + 1, 1)
            store_gate(NB - 2, 0)
            store_gate(NB - 1, 1)
            sp.wait_ge(s["deg_col"], 1)
            sp.dma_start(DI_d.rearrange("(t p) -> p t", p=P), dinv[:, :], allow_slow_non_contiguous=True).then_inc(s["dinv_stored"], 16)
            sp.wait_ge(s["dinv_stored"], 16)

            def dinv_quarter(i, q):
                k = 4 * (i - 1) + q
                if k:
                    sp.wait_ge(s["spmm_evac"], UNIT0[i] + 3 * q)
                sp.dma_start(dinv_q[:, 0:QW[q]], DI_d[None, QCOL[q]:QCOL[q] + QW[q]].broadcast_to([P, QW[q]])).then_inc(s["dinv_in"], 16)

            def store_relu(i, q, dram, rows, m):
                k0 = FE0[i] + 2 * m * (q + 1)
                sp.wait_ge(s["fe_evac"], k0)
                sp.dma_start(dram[:, :, QCOL[q]:QCOL[q] + QW[q]], rst[0:rows, 0:m, 0:QW[q]]).then_inc(s["r_stored"], 16)

            def ring_tiles(i, dram, rows, m):
                for t in range(NT):
                    k = NT * (i - 1) + t
                    if t >= 4:
                        sp.wait_ge(s["cv_done"], NT * (i - 1) + t - 3)
                    wd = min(P, NC - P * t)
                    slot = Sflat[0:rows, (t % 4) * 512:(t % 4) * 512 + m * P].rearrange("p (m n) -> p m n", m=m)
                    sp.dma_start(slot[:, :, 0:wd], dram[:, :, P * t:P * t + wd]).then_inc(s[f"ring{t % 4}"], 16)

            sp.wait_ge(s["bn_aff"], 1)
            for o, i in ((w[0:C, :], 0), (w[C:C2P, :], 0)):
                sp.dma_start(o.rearrange("p (g f) -> p g f", g=3), d["Wc1"].rearrange("(g p) f -> p g f", g=3)).then_inc(s["w1_in"], 16)
            for q in range(4):
                dinv_quarter(1, q)
                if q:
                    store_relu(1, q - 1, R2_d, R2, M2)
            store_relu(1, 3, R2_d, R2, M2)
            quarter_used(sp, 1, 3)
            sp.dma_start(w[0:R2, 0:M2 * C3].rearrange("p (m f) -> p m f", m=M2), d["Wc2"].rearrange("(m p) f -> p m f", m=M2)).then_inc(s["w2_in"], 16)
            sp.wait_ge(s["r_stored"], 64)
            ring_tiles(1, R2_d, R2, M2)
            for q in range(4):
                dinv_quarter(2, q)
                if q:
                    store_relu(2, q - 1, R3_d, R3, M3)
            store_relu(2, 3, R3_d, R3, M3)
            quarter_used(sp, 2, 3)
            sp.dma_start(w[0:R3, 0:M3 * C].rearrange("p (m f) -> p m f", m=M3), d["W_out"].rearrange("(m p) f -> p m f", m=M3)).then_inc(s["w3_in"], 16)
            for k, nm in enumerate(("b_out", "g_out", "be_out")):
                sp.dma_start(w[:, C3 + C * k:C3 + C * k + C], pb(nm)).then_inc(s["w3_in"], 16)
            sp.wait_ge(s["r_stored"], 128)
            ring_tiles(2, R3_d, R3, M3)
            sp.wait_ge(s["bn_aff"], 2)
            for k, nm in enumerate(("W_self1", "W_neigh1", "sb1", "W_self2", "W_neigh2", "sb2")):
                if nm[0] == "s":
                    sp.dma_start(w[:, C * k:C * k + C], pb(nm)).then_inc(s["w4_in"], 16)
                else:
                    sp.dma_start(w[0:C, C * k:C * k + C], d[nm]).then_inc(s["w4_in"], 16)
                    if "neigh" in nm:
                        sp.dma_start(w[C:C2P, C * k:C * k + C], d[nm]).then_inc(s["w4_in"], 16)
            sp.wait_ge(s["ident_kept"], 16)
            sp.dma_start(ident16, ID_d).then_inc(s["w4_in"], 16)
            sp.wait_ge(s["nq_evac"], 20)
            for k, nm in enumerate(("gamma", "beta")):
                sp.dma_start(w[:, 512 + C * k:512 + C * k + C], pb(nm)).then_inc(s["w6_in"], 16)
            sp.dma_start(ldst, d["dst"]).then_inc(s["late_in"], 16)
            sp.dma_start(lsrc_i, d["src"]).then_inc(s["late_in"], 16)
            sp.dma_start(lcw, d["edge_weight"]).then_inc(s["late_in"], 16)
            sp.wait_ge(s["hv_ready"], 1)
            sp.dma_start(HV_d[:, 0:C].rearrange("(t p) f -> p t f", p=P), hT).then_inc(s["hv_stored"], 16)
            sp.wait_ge(s["e1_st0"], 16 * NB)
            sp.wait_ge(s["e1_st1"], 16 * NB)

            def load_late(b, par):
                sp.wait_ge(s["l_msg"], b + 1)
                sp.dma_start(lg[:, par, :, :].rearrange("p k f -> p (k f)"), G_d[bass.ds(b, 1), :, :].rearrange("o p f -> (o p) f")).then_inc(s[f"l_in{par}"], 16)
                sp.dma_start(le[:, par, :, :].rearrange("p k f -> p (k f)"), E1_d[bass.ds(b, 1), :, :].rearrange("o p f -> (o p) f")).then_inc(s[f"l_in{par}"], 16)

            with sp.Fori(0, NB // 2) as i:
                load_late(i * 2, 0)
                load_late(i * 2 + 1, 1)
            sp.wait_ge(s["out_ready"], 1)
            full = (NT - 1) * P
            sp.dma_start(out[0:full, :].rearrange("(t p) f -> p t f", p=P), X[:, 0:NT - 1, :]).then_inc(s["out_done"], 16)
            sp.dma_start(out[full:N, :], X[0:TAIL, NT - 1, :]).then_inc(s["out_done"], 16)
            sp.wait_ge(s["out_done"], 32)

        @block.gpsimd
        def _(pool):
            g = nc.gpsimd
            step = Chain(pool, s["pool_step"])
            g.iota(pidx[:, :], [[0, 1]], base=0, channel_multiplier=1, allow_small_or_imprecise_dtypes=True).then_inc(s["consts"], 1)
            g.iota(iota16, [[1, P]], base=0, channel_multiplier=0, allow_small_or_imprecise_dtypes=True).then_inc(s["consts"], 1)
            g.iota(iota_w, [[CODE, NT], [1, WIN]], base=0, channel_multiplier=0, allow_small_or_imprecise_dtypes=True).then_inc(s["consts"], 1)
            g.memset(ones16, 1.0).then_inc(s["ones_ready"], 1)
            g.iota(wtab, [[WIN, NWIN]], base=0, channel_multiplier=0, allow_small_or_imprecise_dtypes=True).then_inc(s["consts"], 1)
            pool.wait_ge(s["consts"], 4)
            pool.wait_ge(s["keys_prep"], 1)
            pool.wait_ge(s["c0_ready"], 1)

            def pair_keys(pair, slot):
                w = pair * 2
                pool.wait_ge(s["onehots_built"], w + 1)
                c0 = [pool.value_load(c0i[0:1, bass.ds(w + j, 1)], min_val=0, max_val=NCHUNK - WCH) for j in range(2)]
                for j in range(2):
                    g.tensor_copy(key[:, slot, 2, j, :], lo_f[:, bass.ds(c0[j], WCH)])
                    ins = g.tensor_tensor(key[:, slot, 1, j, :], dst_f[:, bass.ds(c0[j], WCH)],
                                          bc(wtab[:, bass.ds(w + j, 1)], [P, WCH]), ALU.subtract)
                ins.then_inc(s["pool_step"], 1)
                pool.wait_ge(s["pool_step"], w + 1)
                pool.sem_inc(s["pool_passed"], 1)
                g.tensor_scalar(key[:, slot, 1, :, :], key[:, slot, 1, :, :], float(WIN), -1.0, ALU.min, ALU.max).then_inc(s["pool_step"], 1)
                pool.wait_ge(s["pool_step"], w + 2)
                for j in range(2):
                    ins = g.tensor_tensor(key[:, slot, 0, j, :], key[:, slot, 1, j, :], hi_f[:, bass.ds(c0[j], WCH)], ALU.add)
                ins.then_inc(s["key_ready"], 1)

            with pool.Fori(0, NWIN // 4) as i:
                pair_keys(i * 2, 0)
                pair_keys(i * 2 + 1, 1)

            def load_sources(b, par):
                pool.dma_start(e1ix[:, par, :], d["src"][:, bass.ds(b * 4, 4)]).then_inc(s[f"e1_in{par}"], 16)

            def gather_half(b, par, h, turn):
                if turn is not None:
                    pool.wait_ge(s[f"e1_st{h}"], turn)
                    pool.sem_inc(s["pool_passed"], 1)
                for k in range(2):
                    g.indirect_dma_start(out=e1st[:, h, k, :], out_offset=None, in_=TN1_d,
                                         in_offset=bass.IndirectOffsetOnAxis(ap=e1ix[:, par, 2 * h + k:2 * h + k + 1], axis=0)).then_inc(s[f"e1_got{h}"], 16)

            def store_half(b, h, turn):
                pool.wait_ge(s[f"e1_got{h}"], turn)
                pool.dma_start(E1_d[bass.ds(b, 1), :, 2 * GD * h:2 * GD * h + 2 * GD].rearrange("o p f -> (o p) f"),
                               e1st[:, h, :, :].rearrange("p k f -> p (k f)")).then_inc(s[f"e1_st{h}"], 16)

            def gather_batch(i, par, more=True):
                b = i * 2 + par
                pool.wait_ge(s[f"e1_in{par}"], i * 16 + 16)
                pool.sem_inc(s["pool_passed"], 1)
                first = isinstance(b, int) and b == 0
                gather_half(b, par, 0, None if first else b * 16)
                gather_half(b, par, 1, None if first else b * 16)
                store_half(b, 0, b * 32 + 32)
                store_half(b, 1, b * 32 + 32)
                if more:
                    load_sources(b + 2, par)

            pool.wait_ge(s["tn_stored"], 32)
            load_sources(0, 0)
            load_sources(1, 1)
            gather_batch(0, 0)
            gather_batch(0, 1)
            with pool.Fori(1, NB // 2 - 1) as i:
                gather_batch(i, 0)
                gather_batch(i, 1)
            gather_batch(NB // 2 - 1, 0, more=False)
            gather_batch(NB // 2 - 1, 1, more=False)
            pool.wait_ge(s["nq_evac"], 20)
            g.iota(iota_n, [[1, NC]], base=-(NC // 2), channel_multiplier=0, allow_small_or_imprecise_dtypes=True).then_inc(s["consts"], 1)
            pool.wait_ge(s["hv_stored"], 16)
            pool.wait_ge(s["late_in"], 48)

            def gather_dst(b, par):
                pool.wait_ge(s["l_hi"], b + 1)
                g.tensor_copy(lix[:, par, :], ldst[:, bass.ds(b * 4, 4)]).then_inc(s["pool_step"], 1)
                pool.wait_ge(s["pool_step"], b + (NWIN + 1))
                pool.sem_inc(s["pool_passed"], 1)
                for k in range(4):
                    g.indirect_dma_start(out=lh[:, par, k, :], out_offset=None, in_=HV_d,
                                         in_offset=bass.IndirectOffsetOnAxis(ap=lix[:, par, k:k + 1], axis=0)).then_inc(s[f"l_got{par}"], 16)

            with pool.Fori(0, NB // 2) as i:
                gather_dst(i * 2, 0)
                gather_dst(i * 2 + 1, 1)

        @block.vector
        def _(dve):
            v = nc.vector
            step = Chain(dve, s["dve_step"])
            dve.sem_inc(s["onehots_built"], 3)
            dve.sem_inc(s["g_evac"], 2)
            step(v.memset(w1t[:, C:P], 0.0))
            dve.wait_ge(s["consts"], 2)
            step(v.tensor_scalar(half[:, :], pidx[:, :], float(C), 1.0 / LOW - 1.0, ALU.is_ge, ALU.mult))
            step(v.tensor_scalar(half[:, :], half[:, :], 1.0, None, ALU.add))
            step(v.tensor_scalar(sq[:, 0:C], iota16[:, 0:C], pidx[:, 0:1], None, ALU.is_equal))
            step(v.tensor_scalar(sq[:, C:C + 1], pidx[:, :], -float(C), None, ALU.add))
            step(v.tensor_scalar(comb[:, :], iota16[:, 0:C], sq[:, C:C + 1], None, ALU.is_equal))
            step(v.tensor_tensor(comb[:, :], comb[:, :], sq[:, 0:C], ALU.add))
            step(v.tensor_scalar(comb[:, :], comb[:, :], half[:, 0:1], None, ALU.mult))
            v.tensor_scalar(ident16, iota16, pidx[:, 0:1], None, ALU.is_equal).then_inc(s["ident_ready"], 1)
            dve.wait_ge(s["in_small"], 16 * 22)
            A, B, D = two_pi_parts()
            ang, kk, r, ph = tw[:, 0:1], tw[:, 1:2], tw[:, 2:3], tw[:, 3:4]
            step(v.tensor_tensor(ang, col("tstep"), col("freq"), ALU.mult))
            step(v.tensor_scalar(ph, pidx[:, :], 64.0, float(np.pi / 2), ALU.is_ge, ALU.mult))
            step(v.tensor_tensor(kk, ang, ph, ALU.add))
            step(v.tensor_scalar(kk, kk, float(1 / (2 * np.pi)), 12582912.0, ALU.mult, ALU.add))
            step(v.tensor_scalar(kk, kk, -12582912.0, None, ALU.add))
            step(v.scalar_tensor_tensor(r, kk, -A, ang, ALU.mult, ALU.add))
            step(v.scalar_tensor_tensor(r, kk, -B, r, ALU.mult, ALU.add))
            step(v.tensor_tensor(r, r, ph, ALU.add))
            step(v.scalar_tensor_tensor(r, kk, -D, r, ALU.mult, ALU.add))
            v.tensor_scalar(r, r, 3.1415925, -3.1415925, ALU.min, ALU.max).then_inc(s["t_r"], 1)
            dve.wait_ge(s["t_mm1"], 1)
            step(v.tensor_tensor(tw[:, 5:6], ps[:, 0, 0:1], col("btm"), ALU.add))
            v.tensor_scalar(tw[:, 5:6], tw[:, 5:6], 0.0, None, ALU.max).then_inc(s["t_rel"], 1)
            dve.wait_ge(s["t_mm2"], 1)
            step(v.tensor_tensor(bias2[0:R2, :], ps[0:R2, 1, 0:M2], col("bt1", R2), ALU.add))
            step(v.tensor_scalar(bias2[0:R2, :], bias2[0:R2, :], 0.0, None, ALU.max))
            step(v.tensor_tensor(bias2[0:R2, :], bias2[0:R2, :], col("bc1", R2), ALU.add))
            step(v.tensor_tensor(bias3[0:R3, :], ps[0:R3, 1, M2:M2 + M3], col("bt2", R3), ALU.add))
            step(v.tensor_scalar(bias3[0:R3, :], bias3[0:R3, :], 0.0, None, ALU.max))
            v.tensor_tensor(bias3[0:R3, :], bias3[0:R3, :], col("bc2", R3), ALU.add).then_inc(s["bias_ready"], 1)
            dve.wait_ge(s["tables_T"], 1)
            v.tensor_copy(tt12[:, GD:2 * GD], ps[0:NEL, 2, 0:GD]).then_inc(s["tables_tt"], 1)
            dve.wait_ge(s["in_types"], 16)
            v.tensor_scalar(onehot_t[0:NEL, :], typ[0:NEL, :], pidx[0:NEL, 0:1], None, ALU.is_equal).then_inc(s["t_onehot"], 1)
            step(v.tensor_copy(nv_hi, nvec[:, :]))
            step(v.tensor_tensor(tn[:, :, 2 * GD + 1], nvec[:, :], nv_hi, ALU.subtract))
            step(v.tensor_scalar(tn[:, :, 2 * GD + 1], tn[:, :, 2 * GD + 1], LOW, None, ALU.mult))
            v.tensor_copy(nv_lo, tn[:, :, 2 * GD + 1])
            step(v.tensor_copy(tn[:, :, 2 * GD], nv_hi))
            step(v.tensor_copy(tn[:, :, 2 * GD + 1], nv_lo))
            for j in range(4):
                n = min(8, NT - 8 * j)
                dve.wait_ge(s["t_mm"], j + 1)
                v.tensor_copy(tn[:, 8 * j:8 * j + n, 0:2 * GD], ps[:, 4 + j, 0:64 * n].rearrange("p (t f) -> p t f", f=64)).then_inc(s["t_evac"], 1)
            dve.wait_ge(s["in_edges"], 48)
            step(v.tensor_copy(last_f, last_i))
            v.memset(ones1, 1.0).then_inc(s["ones_row"], 1)
            dve.wait_ge(s["consts"], 4)
            for k in range(4):
                v.tensor_scalar(cmp_w[:, k, :], wtab[0:104, :], last_f[:, k:k + 1], None, ALU.is_gt).then_inc(s["c0_cmp"], 1)
            dve.wait_ge(s["c0_sum"], 1)
            step(v.tensor_scalar(c0f, ps[0:1, 3, 0:NWIN], float(NCHUNK - WCH), None, ALU.min))
            v.tensor_copy(c0i, c0f).then_inc(s["c0_ready"], 1)
            step(v.tensor_copy(dst_f, dst_i))
            step(v.tensor_scalar(dst_i, src_i, 7, 6, ALU.arith_shift_right, ALU.logical_shift_left))
            step(v.tensor_copy(hi_f, dst_i))
            step(v.tensor_scalar(dst_i, src_i, P - 1, None, ALU.bitwise_and))
            v.tensor_copy(lo_f, dst_i).then_inc(s["keys_prep"], 1)
            dve.wait_ge(s["in_cw"], 16)

            def cutoff(wd, k, r, m, act_at):
                step(v.tensor_scalar(k, wd, 1.0 / 12.0, 12582912.0, ALU.mult, ALU.add))
                step(v.tensor_scalar(k, k, -12582912.0, None, ALU.add))
                step(v.scalar_tensor_tensor(r, k, -12.0, wd, ALU.mult, ALU.add))
                step(v.tensor_scalar(k, r, -1.0, None, ALU.mult))
                step(v.tensor_tensor(r, r, k, ALU.max))
                step(v.tensor_scalar(r, r, float(-np.pi / 6), float(np.pi / 2), ALU.mult, ALU.add))
                v.tensor_scalar(m, wd, 6.0, 0.5, ALU.is_lt, ALU.mult).then_inc(s["cw_ready"], 1)
                dve.wait_ge(s["t_emb"], act_at)
                dve.wait_ge(s["cw_ready"], 1 if act_at == 2 else 2)
                step(v.tensor_scalar(r, r, 1.0, None, ALU.add))
                step(v.tensor_tensor(wd, r, m, ALU.mult))

            dve.wait_ge(s["keys_prep"], 1)
            dve.wait_ge(s["tn_stored"], 32)
            cutoff(cw, Sflat[:, 0:NCHUNK], Sflat[:, NCHUNK:2 * NCHUNK], Sflat[:, 2 * NCHUNK:3 * NCHUNK], 2)
            v.memset(silu[:, :, :], 1.0).then_inc(s["padz"], 1)

            def window_onehots(pair, slot, half_):
                w, par = pair * 2 + half_, half_
                if half_ == 0:
                    dve.wait_ge(s["key_ready"], pair + 1)
                dve.wait_ge(s["win_done"], w + 1)
                for k in range(WCH):
                    v.tensor_scalar(mov[:, par, k, :], iota_w, key[:, slot, 0, half_, k:k + 1], None, ALU.is_equal)
                    last = v.tensor_scalar(sta[:, par, k, :], iota16, key[:, slot, 2, half_, k:k + 1], None, ALU.is_equal)
                last.then_inc(s["onehots_built"], 1)

            def gate_out(b, par, turn):
                dve.wait_ge(s["gate_done"], b + 3)
                if not (isinstance(turn, int) and turn == 0):
                    dve.wait_ge(s[f"gstored{par}"], turn * 16)
                v.tensor_tensor(gst[:, par, :].rearrange("p (k f) -> p k f", k=4), ps[:, 4 + par, 0:4 * C].rearrange("p (k f) -> p k f", k=4),
                                bc(cw[:, bass.ds(b * 4, 4)].unsqueeze(2), [P, 4, C]), ALU.mult).then_inc(s["g_evac"], 1)

            def windows_and_gates(i):
                window_onehots(i * 2, 0, 0)
                window_onehots(i * 2, 0, 1)
                if not isinstance(i, int):
                    gate_out(i * 2 - 1, 1, i - 1)
                window_onehots(i * 2 + 1, 1, 0)
                window_onehots(i * 2 + 1, 1, 1)
                gate_out(i * 2, 0, i)

            windows_and_gates(0)
            with dve.Fori(1, NWIN // 4) as i:
                windows_and_gates(i)
            gate_out(2 * (NWIN // 4) - 1, 1, NWIN // 4 - 1)
            nsq = [0]

            def sqrt_of(a, n, rows=P, meanwhile=()):
                nsq[0] += 1
                v.tensor_copy(sq[0:rows, 0:n], a).then_inc(s["var_ready"], 1)
                for b in meanwhile:
                    gate_out(b, b % 2, b // 2)
                dve.wait_ge(s["std_ready"], nsq[0])

            def layernorm(out_h, tmp, positive=True, src=None, meanwhile=()):
                src = X[:, :, :] if src is None else src
                step(v.tensor_reduce(stat[:, 0, :], src, AX, ALU.add))
                step(v.tensor_scalar(stat[:, 0, :], stat[:, 0, :], 1.0 / C, None, ALU.mult))
                step(v.tensor_tensor(out_h, src, bc(stat[:, 0, :].unsqueeze(2), [P, NT, C]), ALU.subtract))
                step(v.tensor_tensor(tmp, out_h, out_h, ALU.mult))
                step(v.tensor_reduce(stat[:, 1, :], tmp, AX, ALU.add))
                step(v.tensor_scalar(stat[:, 1, :], stat[:, 1, :], 1.0 / C, EPS, ALU.mult, ALU.add))
                sqrt_of(stat[:, 1, :], NT, meanwhile=meanwhile)
                step(v.reciprocal(stat[:, 1, :], sq[:, 0:NT]))
                step(v.tensor_tensor(out_h, out_h, bc(stat[:, 1, :].unsqueeze(2), [P, NT, C]), ALU.mult))
                if positive:
                    step(v.tensor_scalar(out_h, out_h, 0.0, None, ALU.max))

            dve.wait_ge(s["in_x"], 16)
            dve.wait_ge(s["win_done"], NWIN + 2)
            layernorm(hA, Hf1, meanwhile=(NB - 6, NB - 5))

            def read_degrees(step):
                step(v.memset(stat[:, 0, :], 0.0))
                step(v.tensor_copy(stat[:, 0, 0:NT - 1], ps[:, 7, 0:NT - 1]))
                step(v.tensor_copy(stat[0:NC - P * (NT - 1), 0, NT - 1:NT], ps[0:NC - P * (NT - 1), 7, NT - 1:NT]))

            dve.wait_ge(s["deg_tr"], 1)
            read_degrees(step)
            v.tensor_reduce(rowsum, stat[:, 0, :], AX, ALU.add).then_inc(s["rows_summed"], 1)
            for b in (NB - 4, NB - 3):
                gate_out(b, b % 2, b // 2)
            dve.wait_ge(s["total_mm"], 1)
            step(v.tensor_scalar(flag_f, ps[0:1, 6, 0:1], float(E), None, ALU.not_equal))
            step(v.tensor_copy(flag_i, flag_f))
            dve.sem_inc(s["total_ready"], 1)
            missed = dve.value_load(flag_i, min_val=0, max_val=1)
            with dve.If(missed > 0):
                dve.sem_inc(s["all_evac"], 1)
                with dve.Fori(0, NWIN) as w:
                    v.tensor_tensor(all_keys, dst_f, bc(wtab[:, bass.ds(w, 1)], [P, NCHUNK]), ALU.subtract).then_inc(s["all_keys_ready"], 1)
                    dve.wait_ge(s["all_keys_ready"], w * 3 + 1)
                    v.tensor_scalar(all_keys, all_keys, float(WIN), -1.0, ALU.min, ALU.max).then_inc(s["all_keys_ready"], 1)
                    dve.wait_ge(s["all_keys_ready"], w * 3 + 2)
                    v.tensor_tensor(all_keys, all_keys, hi_f, ALU.add).then_inc(s["all_keys_ready"], 1)
                    dve.wait_ge(s["all_keys_ready"], w * 3 + 3)
                    dve.sem_inc(s["all_step_passed"], 1)
                    with dve.Fori(0, NB // 2) as g:
                        for slot in range(2):
                            dve.wait_ge(s[f"all_used{slot}"], w * (NB // 2) + g + 1)
                            for k in range(WCH):
                                c = g * (2 * WCH) + (WCH * slot + k)
                                v.tensor_scalar(mov[:, slot, k, :], iota_w, all_keys[:, bass.ds(c, 1)], None, ALU.is_equal)
                                ins = v.tensor_scalar(sta[:, slot, k, :], iota16, lo_f[:, bass.ds(c, 1)], None, ALU.is_equal)
                            ins.then_inc(s[f"all_onehots{slot}"], 1)
                    dve.wait_ge(s["all_used1"], w * (NB // 2) + (NB // 2 + 1))
                    v.tensor_copy(adj[:, :, bass.ds(w * WIN, WIN)], ps[:, 0, 0:NT * WIN].rearrange("p (s x) -> p s x", x=WIN)).then_inc(s["all_evac"], 1)
                dve.wait_ge(s["all_deg"], 1)
                read_degrees(Chain(dve, s["all_step"]))

            def diagonal(op):
                for t in range(NT):
                    wd = min(P, NC - P * t)
                    i = v.tensor_tensor(adj[0:wd, t, P * t:P * t + wd], adj[0:wd, t, P * t:P * t + wd], ident16[0:wd, 0:wd], op)
                return i

            diagonal(ALU.add).then_inc(s["adj_i"], 1)
            step(v.tensor_scalar(stat[:, 1, :], stat[:, 0, :], 1.0, None, ALU.add))
            step(v.tensor_scalar(rdeg[:, :], stat[:, 0, :], 1.0, None, ALU.max))
            step(v.reciprocal(rdeg[:, :], rdeg[:, :]))
            sqrt_of(stat[:, 1, :], NT, meanwhile=(NB - 2, NB - 1))
            v.reciprocal(dinv[:, :], sq[:, 0:NT]).then_inc(s["deg_col"], 1)
            dve.wait_ge(s["deg_col"], 1)
            step(v.memset(Sflat[:, :], 0.0))

            nsplit = [0]

            def split(val, hview, scale=None):
                k = nsplit[0] = nsplit[0] + 1
                shape = list(val.shape)
                if scale is None:
                    dve.sem_inc(s["h_scaled"], 1)
                else:
                    v.tensor_tensor(val, val, bc(scale[:, :].unsqueeze(2), shape), ALU.mult).then_inc(s["h_scaled"], 1)
                    dve.wait_ge(s["h_scaled"], k)
                dve.wait_ge(s["h_hi"], k)
                if hview.shape[2] == 1:
                    v.tensor_tensor(val, val, hview[:, :, 0, 0, :], ALU.subtract).then_inc(s["h_res"], 1)
                else:
                    for gi in range(3):
                        i = v.tensor_tensor(val[:, :, C * gi:C * gi + C], val[:, :, C * gi:C * gi + C], hview[:, :, gi, 0, :], ALU.subtract)
                    i.then_inc(s["h_res"], 1)

            def rows_of(region, k, w):
                return region[:, k * w:(k + 1) * w]

            def bn_nodes(k, val, F, gB, bB):
                dve.wait_ge(s["bn_mm"], 2 * k + 1)
                step(v.tensor_scalar(sq[:, 0:F], ps[:, 4, 0:F], 1.0 / N, None, ALU.mult))
                v.tensor_tensor(val, val, bc(sq[:, 0:F].unsqueeze(1), [P, NT, F]), ALU.subtract).then_inc(s["bn_cent"], 1)
                dve.wait_ge(s["bn_cent"], k + 1)
                dve.wait_ge(s["bn_mm"], 2 * k + 2)
                step(v.tensor_scalar(sq[:, 0:F], ps[:, 5, 0:F], 1.0 / N, EPS, ALU.mult, ALU.add))
                nsq[0] += 1
                dve.sem_inc(s["var_ready"], 1)
                dve.wait_ge(s["std_ready"], nsq[0])
                step(v.reciprocal(sq[:, 0:F], sq[:, 0:F]))
                step(v.tensor_tensor(sq[:, 0:F], sq[:, 0:F], gB, ALU.mult))
                step(v.tensor_tensor(val, val, bc(sq[:, 0:F].unsqueeze(1), [P, NT, F]), ALU.mult))
                step(v.tensor_tensor(val, val, bc(bB.unsqueeze(1), [P, NT, F]), ALU.add))
                step(v.tensor_scalar(val, val, 0.0, None, ALU.max))
                dve.sem_inc(s["bn_aff"], 1)

            split(hA, H1, dinv)
            dve.wait_ge(s["w0_in"], 80)
            step(v.memset(wreg[:, 576:704], 1.0))
            v.tensor_scalar(wreg[0:C2P, 0:C3], wreg[0:C2P, 0:C3], half[0:C2P, 0:1], None, ALU.mult).then_inc(s["w1_ready"], 1)
            for par in range(2):
                dve.wait_ge(s[f"gstored{par}"], 16 * (NB // 2))
            for t in range(NT):
                dve.wait_ge(s["n1_done"], t + 1)
                i = v.scalar_tensor_tensor(bigC3[:, t, :], ps[:, 4 + t % 4, 0:C3], dinv[:, t:t + 1], wreg[:, C3:2 * C3],
                                           ALU.mult, ALU.add).then_inc(s["n1_evac"], 1)
            dve.wait_ge(s["n1_evac"], NT)
            bn_nodes(0, bigC3, C3, wreg[:, 2 * C3:3 * C3], wreg[:, 3 * C3:4 * C3])
            split(bigC3, H3, dinv)
            dve.wait_ge(s["w1_in"], 32)
            v.tensor_scalar(wreg[0:C2P, :], wreg[0:C2P, :], half[0:C2P, 0:1], None, ALU.mult).then_inc(s["w1_ready"], 1)

            def out_degree(t):
                v.tensor_reduce(rtot[:, t:t + 1], adj[:, t, :], AX, ALU.add)

            def feature_conv(i, rows, m):
                for q in range(4):
                    for gi in range(3):
                        u = UNIT0[i] + 3 * q + gi
                        dve.wait_ge(s["spmm_done"], u + 1)
                        if gi == 0:
                            dve.wait_ge(s["dinv_in"], 16 * (4 * (i - 1) + q + 1))
                            if q:
                                quarter_used(dve, i, q - 1)
                        bank = 2 * (u % 2)
                        hw = QW[q] // 2
                        v.tensor_tensor(S[0:C2P, gi, 0:QW[q]].rearrange("p (c w) -> p c w", c=2), ps[0:C2P, bank:bank + 2, 0:hw],
                                        dinv_q[0:C2P, 0:QW[q]].rearrange("p (c w) -> p c w", c=2), ALU.mult).then_inc(s["spmm_evac"], 1)
                        out_degree(12 * (i - 1) + 3 * q + gi)
                    if q:
                        stats_of(i, q - 1, rows, m)
                stats_of(i, 3, rows, m)

            def stats_of(i, q, rows, m):
                hw = QW[q] // 2
                for c in range(2):
                    for mi in range(m):
                        k = FE0[i] + (2 * q + c) * m + mi
                        dve.wait_ge(s["fe_evac"], k + 1)
                        n = min(hw, N - QCOL[q] - c * hw)
                        v.bn_stats(bnst[0:rows, mi, 2 * q + c, :], rst[0:rows, mi, c * hw:c * hw + n]).then_inc(s["bn_read"], 1)

            def fold(i, rows, m, F, gc, bc_, win):
                dve.wait_ge(s["bn_read"], FE0[i] + 8 * m)
                for mi in range(m):
                    ins = v.bn_aggr(mv[0:rows, mi, :], bnst[0:rows, mi, :, :].rearrange("p a b -> p (a b)"))
                step(ins)
                step(v.tensor_scalar(mv[0:rows, 0:m, 1], mv[0:rows, 0:m, 1], EPS, None, ALU.add))
                sqrt_of(mv[0:rows, 0:m, 1], m, rows)
                step(v.reciprocal(sq[0:rows, 0:m], sq[0:rows, 0:m]))
                step(v.tensor_tensor(sq[0:rows, 0:m], sq[0:rows, 0:m], gc, ALU.mult))
                step(v.tensor_tensor(sq[0:rows, m:2 * m], sq[0:rows, 0:m], mv[0:rows, 0:m, 0], ALU.mult))
                step(v.tensor_tensor(sq[0:rows, 2 * m:3 * m], bc_, sq[0:rows, m:2 * m], ALU.subtract))
                step(v.memset(Hf[0:rows, 0:m * P], 1.0))
                for mi in range(m):
                    ins = v.tensor_scalar(Hf[0:rows, mi * P:(mi + 1) * P], Hf[0:rows, mi * P:(mi + 1) * P], sq[0:rows, 2 * m + mi:2 * m + mi + 1], None, ALU.mult)
                dve.wait_ge(s[win], 16 if i == 1 else 64)
                ins.then_inc(s["fold_t"], 1)
                dve.wait_ge(s["fold_mm"], i)
                v.tensor_copy(wreg[:, m * F:(m + 1) * F], ps[:, 4, 0:F])
                for mi in range(m):
                    ins = v.tensor_scalar(wreg[0:rows, mi * F:(mi + 1) * F], wreg[0:rows, mi * F:(mi + 1) * F], sq[0:rows, mi:mi + 1], None, ALU.mult)
                ins.then_inc(s["fold_w"], 1)
                dve.wait_ge(s["fold_w"], i)
                dve.wait_ge(s["r_stored"], 64 * i)
                dst = bigC3 if F == C3 else hA
                for t in range(NT):
                    dve.wait_ge(s["cv_done"], NT * (i - 1) + t + 1)
                    v.tensor_tensor(dst[:, t, :], ps[:, 4 + t % 4, 0:F], wreg[:, m * F:(m + 1) * F], ALU.add).then_inc(s["cv_evac"], 1)
                dve.wait_ge(s["cv_evac"], NT * i)

            feature_conv(1, R2, M2)
            fold(1, R2, M2, C3, col("g1", R2), col("be1", R2), "w2_in")
            split(bigC3, H3, dinv)
            step(v.memset(wreg[:, 720:720 + 432], 0.0))
            for gi in range(3):
                ins = v.tensor_copy(wreg[:, 720 + 192 * gi:720 + 192 * gi + C], comb[:, :])
            ins.then_inc(s["w1_ready"], 1)
            step(v.memset(Sflat[:, :], 0.0))
            feature_conv(2, R3, M3)
            out_degree(NT - 1)
            fold(2, R3, M3, C, col("g2", R3), col("be2", R3), "w3_in")
            split(hA, H1, dinv)
            step(v.memset(wreg[:, 288:416], 1.0))
            v.memset(Sflat[:, :], 0.0).then_inc(s["w1_ready"], 1)

            def node_quarters(i, fn):
                for q in range(4):
                    k = 4 * NODE_ORDER[i] + q
                    dve.wait_ge(s["nq_done"], k + 1)
                    n, t0 = QT[q], 6 * q
                    fn(ps[:, 4 + q % 2, 0:n * C].rearrange("p (t f) -> p t f", f=C), t0, n)
                    dve.sem_inc(s["nq_evac"], 1)

            def out_conv(p_, t0, n):
                step(v.tensor_tensor(hY[:, t0:t0 + n, :], p_, bc(dinv[:, t0:t0 + n].unsqueeze(2), [P, n, C]), ALU.mult))
                step(v.tensor_tensor(hY[:, t0:t0 + n, :], hY[:, t0:t0 + n, :], bc(wreg[:, C3:C3 + C].unsqueeze(1), [P, n, C]), ALU.add))

            node_quarters(3, out_conv)
            bn_nodes(1, hY, C, wreg[:, C3 + C:C3 + 2 * C], wreg[:, C3 + 2 * C:C3 + 3 * C])
            step(v.tensor_tensor(X[:, :, :], X[:, :, :], hY, ALU.add))
            dve.wait_ge(s["w4_in"], 144)
            step(diagonal(ALU.subtract))
            dve.sem_inc(s["adj_noi"], 1)
            step(v.tensor_scalar(wreg[0:C2P, C:2 * C], wreg[0:C2P, C:2 * C], half[0:C2P, 0:1], None, ALU.mult))
            step(v.tensor_scalar(wreg[0:C2P, 4 * C:5 * C], wreg[0:C2P, 4 * C:5 * C], half[0:C2P, 0:1], None, ALU.mult))
            step(v.tensor_copy(wreg[:, 288:416], ident16))
            dve.sem_inc(s["w1_ready"], 1)

            def self_term(layer, bB):
                for j in range(7):
                    k = 7 * layer + j
                    n = min(4, NT - 4 * j)
                    dve.wait_ge(s["tr_done"], k + 1)
                    v.tensor_copy(Sflat[0:C, (k % 2) * 512:(k % 2) * 512 + n * P], ps[0:C, 4 + k % 2, 0:n * P]).then_inc(s["tr_evac"], 1)
                    dve.wait_ge(s["self_done"], k + 1)
                    v.tensor_tensor(hY[:, 4 * j:4 * j + n, :], ps[:, 6 + k % 2, 0:n * C].rearrange("p (t f) -> p t f", f=C),
                                    bc(bB.unsqueeze(1), [P, n, C]), ALU.add).then_inc(s["self_evac"], 1)
                dve.wait_ge(s["self_evac"], 7 * layer + 7)

            def sage(dst, relu):
                def fn(p_, t0, n):
                    a = hT[:, t0:t0 + n, :]
                    step(v.tensor_tensor(a, p_, bc(rdeg[:, t0:t0 + n].unsqueeze(2), [P, n, C]), ALU.mult))
                    step(v.tensor_tensor(a, a, hY[:, t0:t0 + n, :], ALU.add))
                    if relu:
                        step(v.tensor_scalar(dst[:, t0:t0 + n, :], a, 0.0, None, ALU.max))
                    else:
                        step(v.tensor_tensor(dst[:, t0:t0 + n, :], dst[:, t0:t0 + n, :], a, ALU.add))
                return fn

            layernorm(hA, hT)
            dve.sem_inc(s["ln_x"], 1)
            self_term(0, wreg[:, 2 * C:3 * C])
            split(hA, H1)
            step(v.memset(Sflat[:, :], 0.0))
            dve.sem_inc(s["padz"], 1)
            node_quarters(4, sage(hA, True))
            dve.sem_inc(s["ln_x"], 1)
            self_term(1, wreg[:, 5 * C:6 * C])
            split(hA, H1)
            step(v.memset(Sflat[:, :], 0.0))
            dve.sem_inc(s["padz"], 1)
            node_quarters(5, sage(X, False))
            layernorm(hA, hT)
            for k, (x, ys) in enumerate(FLIPS):
                dve.wait_ge(s["flip_done"], k + 1)
                ys = [y for y in ys if y != x]
                if not ys:
                    continue
                n, wx = len(ys), min(P, NC - P * x)
                src_ = ps[:, 4 + k % 4, 0:n * 64].bitcast(F16).rearrange("p (j c) -> p j c", j=n)[:, :, 0:wx]
                v.tensor_copy(adj[:, ys[0]:ys[0] + n, P * x:P * x + wx], src_).then_inc(s["flip_cols"], 1)
            dve.wait_ge(s["flip_cols"], FLIP_COLS[-1])
            step(v.tensor_scalar(stat[:, 1, :], rtot[:, :], 1.0, None, ALU.max))
            sqrt_of(stat[:, 1, :], NT)
            step(v.reciprocal(dinv[:, :], sq[:, 0:NT]))
            diagonal(ALU.add).then_inc(s["adj_t"], 1)
            split(hA, H1, dinv)

            def light(dst, add):
                def fn(p_, t0, n):
                    a = hT[:, t0:t0 + n, :]
                    step(v.tensor_tensor(a, p_, bc(dinv[:, t0:t0 + n].unsqueeze(2), [P, n, C]), ALU.mult))
                    if add:
                        step(v.tensor_tensor(dst[:, t0:t0 + n, :], dst[:, t0:t0 + n, :], a, ALU.add))
                    else:
                        step(v.tensor_copy(dst[:, t0:t0 + n, :], a))
                return fn

            node_quarters(6, light(hA, False))
            split(hA, H1, dinv)
            node_quarters(7, light(X, True))
            layernorm(hA, hT)
            v.tensor_tensor(hT, hA, bc(nvec[:, :].unsqueeze(2), [P, NT, C]), ALU.mult).then_inc(s["hv_ready"], 1)
            dve.wait_ge(s["late_in"], 48)
            cutoff(lcw, cw_t[:, 0, :], cw_t[:, 1, :], cw_t[:, 2, :], 3)
            step(v.tensor_copy(lsrc, lsrc_i))
            step(v.tensor_scalar(lsrc, lsrc, float(-(NC // 2)), None, ALU.add))
            step(v.scalar_tensor_tensor(combA, wreg[0:2 * CA, 288 + CA:288 + 2 * CA], 1.0 / LOW, wreg[0:2 * CA, 288:288 + CA], ALU.mult, ALU.add))
            dve.wait_ge(s["consts"], 5)
            dve.sem_inc(s["l_msg"], 2)
            dve.sem_inc(s["l_res"], 2)

            base = step.n

            def message(b, par, first):
                dve.wait_ge(s[f"l_in{par}"], (b - par) * 16 + 32)
                dve.wait_ge(s[f"l_got{par}"], (b - par) * 32 + 64)
                n0 = b * 4 + base
                dve.wait_ge(s["l_mm"], b + 1)
                v.tensor_tensor(ldot[:, par, :, :], le[:, par, :, :], lh[:, par, :, C:C + GD], ALU.mult).then_inc(s["dve_step"], 1)
                for k in range(2):
                    v.tensor_scalar(ohn[:, par, k, :], iota_n, lsrc[:, bass.ds(b * 4 + k, 1)], None, ALU.is_equal)
                dve.wait_ge(s["dve_step"], n0 + 1)
                v.tensor_reduce(la[:, par, :], ldot[:, par, :, :], AX, ALU.add).then_inc(s["dve_step"], 1)
                dve.wait_ge(s["dve_step"], n0 + 2)
                v.tensor_tensor(la[:, par, :], la[:, par, :], lcw[:, bass.ds(b * 4, 4)], ALU.mult).then_inc(s["dve_step"], 1)
                dve.wait_ge(s["dve_step"], n0 + 3)
                v.tensor_tensor(lm[:, par, :, :], lg[:, par, :, :], bc(la[:, par, :].unsqueeze(2), [P, 4, C]), ALU.add).then_inc(s["dve_step"], 1)
                dve.wait_ge(s["dve_step"], n0 + 4)
                v.tensor_tensor(lm[:, par, :, :], lm[:, par, :, :], lh[:, par, :, 0:C], ALU.mult).then_inc(s["l_msg"], 1)
                for k in range(2, 4):
                    ins = v.tensor_scalar(ohn[:, par, k, :], iota_n, lsrc[:, bass.ds(b * 4 + k, 1)], None, ALU.is_equal)
                dve.wait_ge(s["l_hi"], b + 3)
                v.tensor_tensor(lm[:, par, :, :], lm[:, par, :, :], lmh[:, par, :, 0, 0:C], ALU.subtract).then_inc(s["l_res"], 1)

            with dve.Fori(0, NB // 2) as i:
                message(i * 2, 0, False)
                message(i * 2 + 1, 1, False)
            step.n = base + 4 * NB
            dve.wait_ge(s["agg_mm"], 4)
            for j in range(3):
                n = min(10, NT - 10 * j)
                agg = ps[:, j, 0:n * CA].rearrange("p (t f) -> p t f", f=CA)
                r_ = rtot[:, 10 * j:10 * j + n]
                step(v.tensor_scalar(r_, agg[:, :, C], 1e-8, None, ALU.max))
                step(v.reciprocal(r_, r_))
                step(v.tensor_tensor(hT[:, 10 * j:10 * j + n, :], agg[:, :, 0:C], bc(r_.unsqueeze(2), [P, n, C]), ALU.mult))
            step(v.tensor_tensor(hT, hT, hA, ALU.add))
            layernorm(hY, hA, positive=False, src=hT)
            dve.wait_ge(s["w6_in"], 32)
            step(v.tensor_tensor(hY, hY, bc(wreg[:, 512:512 + C].unsqueeze(1), [P, NT, C]), ALU.mult))
            step(v.tensor_tensor(hY, hY, bc(wreg[:, 512 + C:512 + 2 * C].unsqueeze(1), [P, NT, C]), ALU.add))
            v.tensor_tensor(X[:, :, :], X[:, :, :], hY, ALU.add).then_inc(s["out_ready"], 1)

        @block.scalar
        def _(act):
            a = nc.scalar
            act.sem_inc(s["silu_done"], 2)
            act.sem_inc(s["win_evac"], 2)
            act.wait_ge(s["t_r"], 1)
            a.activation(tw[:, 4:5], tw[:, 2:3], ACT.Sin).then_inc(s["t_emb"], 1)
            act.wait_ge(s["cw_ready"], 1)
            a.activation(Sflat[:, NCHUNK:2 * NCHUNK], Sflat[:, NCHUNK:2 * NCHUNK], ACT.Sin).then_inc(s["t_emb"], 1)
            act.wait_ge(s["padz"], 1)

            def evac_window(w, par):
                act.wait_ge(s["win_done"], w + 3)
                a.activation(adj[:, :, bass.ds(w * WIN, WIN)], ps[:, par, 0:NT * WIN].rearrange("p (s x) -> p s x", x=WIN),
                             ACT.Copy).then_inc(s["win_evac"], 1)

            def gate_silu(b, par):
                act.wait_ge(s["z_done"], b + 1)
                act.wait_ge(s["gate_done"], b + 1)
                a.activation(silu[0:C, par, :], ps[0:C, 2 + par, :], ACT.Silu, bias=b1c).then_inc(s["silu_done"], 1)

            def four_windows(i):
                gate_silu(i * 2, 0)
                evac_window(i * 4, 0)
                evac_window(i * 4 + 1, 1)
                gate_silu(i * 2 + 1, 1)
                evac_window(i * 4 + 2, 0)
                evac_window(i * 4 + 3, 1)

            act.sem_inc(s["deg_row"], 1)
            with act.Fori(0, SC) as i:
                four_windows(i)
            with act.Fori(1, SC) as c:
                for j in range(SC):
                    four_windows(c * SC + j)
                act.wait_ge(s["deg_mm"], c + 0)
                a.activation(degrow[:, bass.ds((c - 1) * SCW, SCW)], ps[0:1, 6, 0:SCW], ACT.Copy).then_inc(s["deg_row"], 1)
            gate_silu(NB - 6, 0)
            gate_silu(NB - 5, 1)
            act.wait_ge(s["deg_mm"], SC)
            a.activation(degrow_end, ps[0:1, 6, 0:SCW], ACT.Copy).then_inc(s["deg_row"], 1)
            nsq = [0]

            def sqrt_served(n, rows=P):
                nsq[0] += 1
                act.wait_ge(s["var_ready"], nsq[0])
                a.activation(sq[0:rows, 0:n], sq[0:rows, 0:n], ACT.Sqrt).then_inc(s["std_ready"], 1)

            sqrt_served(NT)
            for b in range(NB - 4, NB):
                gate_silu(b, b % 2)
            nsplit = [0]

            def split(val, hview):
                k = nsplit[0] = nsplit[0] + 1
                act.wait_ge(s["h_scaled"], k)
                gs = hview.shape[2]
                for gi in range(gs):
                    ins = a.activation(hview[:, :, gi, 0, :], val[:, :, C * gi:C * gi + C], ACT.Copy)
                ins.then_inc(s["h_hi"], 1)
                act.wait_ge(s["h_res"], k)
                for gi in range(gs):
                    ins = a.activation(hview[:, :, gi, 1, :], val[:, :, C * gi:C * gi + C], ACT.Copy, scale=LOW)
                ins.then_inc(s["h_ready"], 1)

            def evac_quarters(i):
                for q in range(4):
                    u = UNIT0[i] + q
                    act.wait_ge(s["spmm_done"], u + 1)
                    if q >= 2:
                        quarter_used(act, i, q - 2)
                    bank, hw = 2 * (u % 2), QW[q] // 2
                    a.activation(S[0:C2P, q % 2, 0:QW[q]].rearrange("p (c w) -> p c w", c=2), ps[0:C2P, bank:bank + 2, 0:hw],
                                 ACT.Copy).then_inc(s["spmm_evac"], 1)

            def bn_square(k, val, out_sq):
                act.wait_ge(s["bn_cent"], k + 1)
                a.activation(out_sq, val, ACT.Square).then_inc(s["bn_sq"], 1)
                sqrt_served(val.shape[2])

            def relu_blocks(i, rows, m, bias):
                for q in range(4):
                    hw = QW[q] // 2
                    if q or i > 1:
                        act.wait_ge(s["r_stored"], 16 * (4 * (i - 1) + q))
                        act.wait_ge(s["bn_read"], FE0[i] + 2 * m * q)
                    for c in range(2):
                        for mi in range(m):
                            k = FE0[i] + (2 * q + c) * m + mi
                            act.wait_ge(s["fe_done"], k + 1)
                            a.activation(rst[0:rows, mi, c * hw:(c + 1) * hw], ps[0:rows, 4 + k % 4, 0:hw], ACT.Relu,
                                         bias=bias[0:rows, mi:mi + 1]).then_inc(s["fe_evac"], 1)

            sqrt_served(NT)
            split(hA, H1)
            act.wait_ge(s["padz"], 1)
            evac_quarters(0)
            bn_square(0, bigC3, HfC3)
            split(bigC3, H3)
            act.wait_ge(s["bias_ready"], 1)
            relu_blocks(1, R2, M2, bias2)
            sqrt_served(M2, R2)
            split(bigC3, H3)
            relu_blocks(2, R3, M3, bias3)
            sqrt_served(M3, R3)
            split(hA, H1)
            act.wait_ge(s["w1_ready"], 4)
            evac_quarters(3)
            bn_square(1, hY, Hf1)
            sqrt_served(NT)
            split(hA, H1)
            act.wait_ge(s["padz"], 2)
            evac_quarters(4)
            split(hA, H1)
            act.wait_ge(s["padz"], 3)
            evac_quarters(5)
            sqrt_served(NT)
            for k, (x, ys) in enumerate(FLIPS):
                act.wait_ge(s["flip_done"], k + 1)
                wx = min(P, NC - P * x)
                w = min(P * len(ys), NC - P * ys[0])
                a.activation(adj[0:wx, x, P * ys[0]:P * ys[0] + w], ps[0:wx, k % 4, 0:256].bitcast(F16)[:, 0:w],
                             ACT.Copy).then_inc(s["flip_evac"], 1)
            sqrt_served(NT)
            split(hA, H1)
            evac_quarters(6)
            split(hA, H1)
            evac_quarters(7)
            sqrt_served(NT)
            act.wait_ge(s["cw_ready"], 2)
            a.activation(cw_t[:, 1, :], cw_t[:, 1, :], ACT.Sin).then_inc(s["t_emb"], 1)

            act.sem_inc(s["l_hi"], 2)

            def parts(b, par):
                act.wait_ge(s["l_msg"], b + 3)
                act.wait_ge(s["l_mm"], b + 1)
                a.activation(lmh[:, par, :, :, C], lh[:, par, :, C + GD:HROW], ACT.Copy)
                a.activation(lmh[:, par, :, 0, 0:C], lm[:, par, :, :], ACT.Copy).then_inc(s["l_hi"], 1)
                act.wait_ge(s["l_res"], b + 3)
                a.activation(lmh[:, par, :, 1, 0:C], lm[:, par, :, :], ACT.Copy, scale=LOW).then_inc(s["l_lo"], 1)

            with act.Fori(0, NB // 2) as i:
                parts(i * 2, 0)
                parts(i * 2 + 1, 1)
            act.wait_ge(s["l_mm"], NB + 2)
            for c in range(SC):
                ins = a.activation(aggS[0:2 * CA, c * SCW:(c + 1) * SCW], ps[0:2 * CA, c, 0:SCW], ACT.Copy)
            ins = a.activation(aggS[0:2 * CA, NC:NP], ps[0:2 * CA, 0, 0:NP - NC], ACT.Copy, scale=0.0).then_inc(s["agg_evac"], 1)
            sqrt_served(NT)

        @block.tensor
        def _(pe):
            mm = nc.tensor.matmul
            for nm, n in (("win_done", 2), ("gate_done", 2), ("l_mm", 2)):
                pe.sem_inc(s[nm], n)
            pe.wait_ge(s["in_small"], 16 * 22)
            pe.wait_ge(s["t_emb"], 1)
            mm(ps[:, 0, 0:1], wtm, tw[:, 4:5], start=True, stop=True).then_inc(s["t_mm1"], 1)
            pe.wait_ge(s["t_rel"], 1)
            for m in range(M2):
                mm(ps[0:R2, 1, m:m + 1], wt1[:, m * R2:(m + 1) * R2], tw[:, 5:6], start=True, stop=True)
            for m in range(M3):
                ins = mm(ps[0:R3, 1, M2 + m:M2 + m + 1], wt2[:, m * R3:(m + 1) * R3], tw[:, 5:6], start=True, stop=True)
            ins.then_inc(s["t_mm2"], 1)
            mm(ps[0:NEL, 2, 0:GD], embT, adaT, start=True, stop=True).then_inc(s["tables_T"], 1)
            pe.wait_ge(s["tables_tt"], 1)
            pe.wait_ge(s["t_onehot"], 1)
            for j in range(4):
                n = min(8, NT - 8 * j)
                for t in range(8 * j, 8 * j + n):
                    ins = mm(ps[:, 4 + j, 64 * (t % 8):64 * (t % 8) + 64], onehot_t[0:NEL, P * t:P * t + P], tt12, start=True, stop=True)
                ins.then_inc(s["t_mm"], 1)
            pe.wait_ge(s["c0_cmp"], 4)
            pe.wait_ge(s["ones_row"], 1)
            for k in range(4):
                ins = mm(ps[0:1, 3, 0:NWIN], ones1[0:104, :], cmp_w[:, k, :], start=(k == 0), stop=(k == 3))
            ins.then_inc(s["c0_sum"], 1)
            pe.wait_ge(s["c0_ready"], 1)
            pe.wait_ge(s["bias_ready"], 1)
            pe.wait_ge(s["t_evac"], 4)

            def window(w, par):
                pe.wait_ge(s["onehots_built"], w + 4)
                pe.wait_ge(s["win_evac"], w + 1)
                for k in range(WCH):
                    ins = mm(ps[:, par, 0:NT * WIN], sta[:, par, k, :], mov[:, par, k, :], start=(k == 0), stop=(k == WCH - 1))
                ins.then_inc(s["win_done"], 1)

            def gate_hidden(b, par):
                pe.wait_ge(s[f"attr_in{par}"], (b - par) * 8 + 16)
                pe.wait_ge(s["silu_done"], b + 1)
                mm(ps[:, 2 + par, :], w1t, attr[:, par, :], start=True, stop=True).then_inc(s["z_done"], 1)

            def gate_product(b, par):
                pe.wait_ge(s["silu_done"], b + 3)
                pe.wait_ge(s["g_evac"], b + 1)
                for k in range(4):
                    ins = mm(ps[:, 4 + par, C * k:C * k + C], silu[:, par, P * k:P * k + P], w2b, start=True, stop=True)
                ins.then_inc(s["gate_done"], 1)

            def four_windows(i):
                gate_hidden(i * 2, 0)
                window(i * 4, 0)
                window(i * 4 + 1, 1)
                gate_product(i * 2, 0)
                gate_hidden(i * 2 + 1, 1)
                window(i * 4 + 2, 0)
                window(i * 4 + 3, 1)
                gate_product(i * 2 + 1, 1)

            def sum_degrees(c, ks):
                if 0 in ks:
                    pe.wait_ge(s["win_evac"], (c + 1) * (4 * SC) + 2)
                    pe.wait_ge(s["deg_row"], c + 1)
                for k in ks:
                    ins = mm(ps[0:1, 6, 0:SCW], ones16[:, 0:1], adj[:, k, bass.ds(c * SCW, SCW)], start=(k == 0), stop=(k == NT - 1))
                if NT - 1 in ks:
                    ins.then_inc(s["deg_mm"], 1)

            pe.wait_ge(s["ones_ready"], 1)
            with pe.Fori(0, SC) as i:
                four_windows(i)
            with pe.Fori(1, SC) as c:
                for j in range(SC):
                    four_windows(c * SC + j)
                    sum_degrees(c - 1, range(j * NT // SC, (j + 1) * NT // SC))

            def gates(b):
                for fn in (gate_hidden, gate_product):
                    fn(b, 0)
                    fn(b + 1, 1)

            gates(NB - 6)
            sum_degrees(SC - 1, range(NT))
            pe.wait_ge(s["deg_row"], SC + 1)
            for t in range(NT):
                wd, at = min(P, NC - P * t), P * t - 6 * SCW
                row = degrow[:, P * t:P * t + wd] if at < 0 else degrow_end[:, at:at + wd]
                ins = mm(ps[0:wd, 7, t:t + 1], row, ones16[0:1, 0:1], start=True, stop=True)
            ins.then_inc(s["deg_tr"], 1)
            gates(NB - 4)
            pe.wait_ge(s["rows_summed"], 1)
            mm(ps[0:1, 6, 0:1], ones1, rowsum, start=True, stop=True).then_inc(s["total_mm"], 1)
            gates(NB - 2)
            pe.wait_ge(s["total_ready"], 1)
            missed = pe.value_load(flag_i, min_val=0, max_val=1)
            with pe.If(missed > 0):
                pe.sem_inc(s["all_used0"], 1)
                pe.sem_inc(s["all_used1"], 1)

                def all_groups(w, g, first=False, last=False):
                    for slot in range(2):
                        pe.wait_ge(s[f"all_onehots{slot}"], w * (NB // 2) + g + 1)
                        for k in range(WCH):
                            ins = mm(ps[:, 0, 0:NT * WIN], sta[:, slot, k, :], mov[:, slot, k, :], start=(first and slot + k == 0), stop=(last and slot == 1 and k == WCH - 1))
                        ins.then_inc(s[f"all_used{slot}"], 1)

                with pe.Fori(0, NWIN) as w:
                    pe.wait_ge(s["all_evac"], w + 1)
                    all_groups(w, 0, first=True)
                    with pe.Fori(1, NB // 2 - 1) as g:
                        all_groups(w, g)
                    all_groups(w, NB // 2 - 1, last=True)
                pe.wait_ge(s["all_evac"], NWIN + 1)

                def degrees(t, wd=P):
                    for k in range(NT):
                        ins = mm(ps[0:wd, 7, bass.ds(t, 1)], adj[:, k, bass.ds(t * P, wd)], ones16[:, 0:1], start=(k == 0), stop=(k == NT - 1))
                    return ins

                with pe.Fori(0, NT - 1) as t:
                    degrees(t)
                degrees(NT - 1, NC - P * (NT - 1)).then_inc(s["all_deg"], 1)
            pe.wait_ge(s["adj_i"], 1)
            pe.wait_ge(s["g_evac"], NB + 2)

            def spmm(i, q, gi, hview):
                u = UNIT0[i] + (3 * q + gi if GROUPS[i] == 3 else q)
                if q == 0 and gi == 0:
                    pe.wait_ge(s["h_ready"], i + 1)
                if u >= 2:
                    pe.wait_ge(s["spmm_evac"], u - 1)
                bank, hw = 2 * (u % 2), QW[q] // 2
                for t in range(NT):
                    for c in range(2):
                        ins = mm(ps[0:C2P, bank + c, 0:hw], hview[:, t, gi, :, :].rearrange("p h f -> p (h f)"),
                                 adj[:, t, QCOL[q] + c * hw:QCOL[q] + (c + 1) * hw], start=(t == 0), stop=(t == NT - 1))
                ins.then_inc(s["spmm_done"], 1)
                return u

            def conv1_tiles(q):
                pe.wait_ge(s["spmm_evac"], q + 1)
                for j in range(QT[q]):
                    t = 6 * q + j
                    if t == 0:
                        pe.wait_ge(s["w1_ready"], 1)
                    if t >= 4:
                        pe.wait_ge(s["n1_evac"], t - 3)
                    ins = mm(ps[:, 4 + t % 4, 0:C3], S[0:C2P, q % 2, P * j:P * j + P], wreg[0:C2P, 0:C3], start=True, stop=True)
                    ins.then_inc(s["n1_done"], 1)

            def bn_sums(k, val, sqv, F, evac_sem, evac_n):
                pe.wait_ge(evac_sem, evac_n)
                on = wreg[:, 576:704] if k == 0 else wreg[:, 288:416]
                for part, bank in ((0, 4), (1, 5)):
                    if part:
                        pe.wait_ge(s["bn_sq"], k + 1)
                    x_ = sqv if part else val
                    for t in range(NT):
                        r = P if t < NT - 1 else TAIL
                        ins = mm(ps[:, bank, 0:F], on[0:r, :], x_[0:r, t, :], start=(t == 0), stop=(t == NT - 1))
                    ins.then_inc(s["bn_mm"], 1)

            for q in range(4):
                spmm(0, q, 0, H1)
                if q:
                    conv1_tiles(q - 1)
            conv1_tiles(3)
            bn_sums(0, bigC3, HfC3, C3, s["n1_evac"], NT)

            def feature_blocks(i, q, rows, m, wv):
                pe.wait_ge(s["spmm_evac"], UNIT0[i] + 3 * q + 3)
                if q == 0:
                    pe.wait_ge(s["w1_ready"], i + 1)
                hw = QW[q] // 2
                for c in range(2):
                    for mi in range(m):
                        k = FE0[i] + (2 * q + c) * m + mi
                        if k >= 4:
                            pe.wait_ge(s["fe_evac"], k - 3)
                        for gi in range(3):
                            ins = mm(ps[0:rows, 4 + k % 4, 0:hw], wv[0:C2P, gi, mi * rows:(mi + 1) * rows], S[0:C2P, gi, c * hw:(c + 1) * hw],
                                     start=(gi == 0), stop=(gi == 2))
                        ins.then_inc(s["fe_done"], 1)

            def feature_conv(i, rows, m, wv):
                for q in range(4):
                    spmm(i, q, 0, H3)
                    if q:
                        feature_blocks(i, q - 1, rows, m, wv)
                    spmm(i, q, 1, H3)
                    spmm(i, q, 2, H3)
                feature_blocks(i, 3, rows, m, wv)

            def folded(i, rows, m, F):
                pe.wait_ge(s["fold_t"], i)
                pe.wait_ge(*((s["w2_in"], 16) if i == 1 else (s["w3_in"], 64)))
                pe.wait_ge(s["fe_evac"], FE0[i] + 8 * m)
                for mi in range(m):
                    ins = mm(ps[:, 4, 0:F], Hf[0:rows, mi * P:(mi + 1) * P], wreg[0:rows, mi * F:(mi + 1) * F], start=(mi == 0), stop=(mi == m - 1))
                ins.then_inc(s["fold_mm"], 1)
                pe.wait_ge(s["fold_w"], i)
                for t in range(NT):
                    k = NT * (i - 1) + t
                    uses = 16 * ((i - 1) * len(range(t % 4, NT, 4)) + t // 4 + 1)
                    pe.wait_ge(s[f"ring{t % 4}"], uses)
                    if t >= 4:
                        pe.wait_ge(s["cv_evac"], k - 3)
                    for mi in range(m):
                        lhs = Sflat[0:rows, (t % 4) * 512 + mi * P:(t % 4) * 512 + (mi + 1) * P]
                        ins = mm(ps[:, 4 + t % 4, 0:F], lhs, wreg[0:rows, mi * F:(mi + 1) * F], start=(mi == 0), stop=(mi == m - 1))
                    ins.then_inc(s["cv_done"], 1)

            feature_conv(1, R2, M2, wreg[:, :].rearrange("p (g f) -> p g f", g=3))
            folded(1, R2, M2, C3)
            feature_conv(2, R3, M3, wreg[:, 720:1152].rearrange("p (g f) -> p g f", g=3))
            folded(2, R3, M3, C)

            def node_tiles(i, q, wv):
                k = 4 * NODE_ORDER[i] + q
                pe.wait_ge(s["spmm_evac"], UNIT0[i] + q + 1)
                if k >= 2:
                    pe.wait_ge(s["nq_evac"], k - 1)
                for j in range(QT[q]):
                    ins = mm(ps[:, 4 + q % 2, C * j:C * j + C], S[0:C2P, q % 2, P * j:P * j + P], wv, start=True, stop=True)
                ins.then_inc(s["nq_done"], 1)

            def node_conv(i, wv):
                for q in range(4):
                    spmm(i, q, 0, H1)
                    if q:
                        node_tiles(i, q - 1, wv)
                node_tiles(i, 3, wv)

            node_conv(3, comb[0:C2P, :])
            bn_sums(1, hY, Hf1, C, s["nq_evac"], 4)

            def self_product(layer, wv):
                pe.wait_ge(s["ln_x"], layer + 1)
                if layer == 0:
                    pe.wait_ge(s["w1_ready"], 5)
                idf = wreg[:, 288:416]
                for j in range(7):
                    k = 7 * layer + j
                    n = min(4, NT - 4 * j)
                    if k >= 2:
                        pe.wait_ge(s["self_evac"], k - 1)
                    for t in range(n):
                        ins = nc.tensor.transpose(ps[0:C, 4 + k % 2, P * t:P * t + P], hA[:, 4 * j + t, :], idf)
                    ins.then_inc(s["tr_done"], 1)
                    pe.wait_ge(s["tr_evac"], k + 1)
                    for t in range(n):
                        ins = mm(ps[:, 6 + k % 2, C * t:C * t + C], Sflat[0:C, (k % 2) * 512 + t * P:(k % 2) * 512 + t * P + P], wv, start=True, stop=True)
                    ins.then_inc(s["self_done"], 1)

            pe.wait_ge(s["adj_noi"], 1)
            self_product(0, wreg[0:C, 0:C])
            node_conv(4, wreg[0:C2P, C:2 * C])
            self_product(1, wreg[0:C, 3 * C:4 * C])
            node_conv(5, wreg[0:C2P, 4 * C:5 * C])
            pe.wait_ge(s["nq_evac"], 12)
            id16 = ident16
            for k, (x, ys) in enumerate(FLIPS):
                if k >= 4:
                    pe.wait_ge(s["flip_evac"], k - 3)
                    if FLIP_COLS[k - 4]:
                        pe.wait_ge(s["flip_cols"], FLIP_COLS[k - 4])
                wx = min(P, NC - P * x)
                rows_ = ps[:, k % 4, 0:256].bitcast(F16)
                cols_ = ps[:, 4 + k % 4, 0:256].bitcast(F16)
                for j, y in enumerate(ys):
                    if y != x:
                        nc.tensor.transpose(cols_[:, P * j:P * j + P], adj[:, x, P * y:P * y + P], id16)
                    ins = nc.tensor.transpose(rows_[0:wx, P * j:P * j + P], adj[:, y, P * x:P * x + wx], id16)
                ins.then_inc(s["flip_done"], 1)
            pe.wait_ge(s["flip_evac"], len(FLIPS))
            pe.wait_ge(s["adj_t"], 1)
            node_conv(6, comb[0:C2P, :])
            node_conv(7, comb[0:C2P, :])

            def scatter(b, par, first, last):
                pe.wait_ge(s["l_res"], b + 3)
                pe.wait_ge(s["l_lo"], b + 1)
                for k in range(4):
                    for c in range(SC):
                        ins = mm(ps[0:2 * CA, c, 0:SCW], lmh[:, par, k, :, :].rearrange("p h f -> p (h f)"), ohn[:, par, k, c * SCW:(c + 1) * SCW],
                                 start=(first and k == 0), stop=(last and k == 3))
                ins.then_inc(s["l_mm"], 1)

            pe.wait_ge(s["nq_evac"], 20)
            scatter(0, 0, True, False)
            scatter(1, 1, False, False)
            with pe.Fori(1, NB // 2 - 1) as i:
                scatter(i * 2, 0, False, False)
                scatter(i * 2 + 1, 1, False, False)
            scatter(NB - 2, 0, False, False)
            scatter(NB - 1, 1, False, True)
            pe.wait_ge(s["agg_evac"], 1)
            for t in range(NT):
                ins = mm(ps[:, t // 10, CA * (t % 10):CA * (t % 10) + CA], aggS[0:2 * CA, P * t:P * t + P], combA, start=True, stop=True)
            ins.then_inc(s["agg_mm"], 4)


def kernel(**x):
    import concourse.bacc as _bacc
    from concourse.bass_utils import run_bass_kernel_spmd as _run

    def arr(name):
        return np.asarray(x[name])

    def by_chunk(a, fill):
        full = np.full(EP, fill, a.dtype)
        full[:E] = a
        return np.ascontiguousarray(full.reshape(NCHUNK, P).T)

    def by_tile(a):
        full = np.zeros(NP, a.dtype)
        full[:N] = a
        return np.ascontiguousarray(full.reshape(NT, P).T)

    def by_block(a, m):
        return np.ascontiguousarray(a.reshape(m, -1).T)

    xp = np.zeros((NP, C), np.float32)
    xp[:N] = arr("x")
    types = np.zeros(NP, np.int32)
    types[:N] = arr("node_type_119")
    attr = np.zeros((RBF, EP), np.float32)
    attr[:, :E] = arr("edge_attr_40").T
    freqs = np.exp(np.arange(64, dtype=np.float32) * np.float32(-np.log(10000.0) / 63)).astype(np.float32)
    L0, L1, L3 = "L0_gnn_", "L1_gnn_", "L3_gnn_"
    ins = {
        "x": xp, "src": by_chunk(arr("src"), NP - 1), "dst": by_chunk(arr("dst"), NP - 1),
        "edge_attr": attr, "edge_weight": by_chunk(arr("edge_weight"), 0.0),
        "node_type": types, "node_vec": by_tile(arr("node_vec")),
        "freq": np.concatenate([freqs, freqs]), "timestep": arr(L0 + "timestep"),
        "Wtm": arr(L0 + "Wtm"), "btm": arr(L0 + "btm"), "W_in": arr(L0 + "W_in"), "b_in": arr(L0 + "b_in"),
        "g_in": arr(L0 + "g_in"), "be_in": arr(L0 + "be_in"), "Wt1": arr(L0 + "Wt1"), "Wt2": arr(L0 + "Wt2"),
        "Wc1": arr(L0 + "Wc1"), "Wc2": arr(L0 + "Wc2"), "W_out": arr(L0 + "W_out"), "b_out": arr(L0 + "b_out"),
        "g_out": arr(L0 + "g_out"), "be_out": arr(L0 + "be_out"),
        "W_self1": arr(L1 + "W_self1"), "W_neigh1": arr(L1 + "W_neigh1"), "sb1": arr(L1 + "b1"),
        "W_self2": arr(L1 + "W_self2"), "W_neigh2": arr(L1 + "W_neigh2"), "sb2": arr(L1 + "b2"),
        "W1T": arr(L3 + "W1").T, "b1": arr(L3 + "b1"), "W2T": arr(L3 + "W2").T, "b2": arr(L3 + "b2"),
        "emb": arr(L3 + "emb"), "embT": arr(L3 + "emb").T, "adaT": arr(L3 + "adaptW").T,
        "gamma": arr(L3 + "gamma"), "beta": arr(L3 + "beta"),
    }
    for nm in ("bc1", "bt1", "g1", "be1"):
        ins[nm] = by_block(arr(L0 + nm), M2)
    for nm in ("bc2", "bt2", "g2", "be2"):
        ins[nm] = by_block(arr(L0 + nm), M3)

    nc = _bacc.Bacc("TRN2", target_bir_lowering=False, num_devices=1)
    arrays, aps = {}, {}
    for name, a in ins.items():
        a = np.ascontiguousarray(a)
        arrays["in_" + name] = a
        aps[name] = nc.dram_tensor("in_" + name, a.shape, mybir.dt.from_np(a.dtype), kind="ExternalInput").ap()
    out = nc.dram_tensor("out_0", [N, C], F32, kind="ExternalOutput").ap()
    build(nc, aps, out)
    r = _run(nc, [arrays], core_ids=[0])
    return r.results[0]["out_0"]
```

```python
from contextlib import ExitStack

import numpy as np

import concourse.bass as bass
from concourse import mybir

F32 = mybir.dt.float32
F16 = mybir.dt.float16
I32 = mybir.dt.int32
ALU = mybir.AluOpType
ACT = mybir.ActivationFunctionType
AX = mybir.AxisListType.X

N, E, C, RBF, NEL, GD = 3125, 53125, 48, 40, 119, 32
P = 128
NT = -(-N // P)
NP = NT * P
TAIL = N - (NT - 1) * P
C3, C9 = 3 * C, 9 * C
C2P = 2 * C
EPS = 1e-5
LOW = 4096.0

WIN = 16
NWIN = -(-N // WIN)
NC = NWIN * WIN
CODE = 64
WCH = 4
NCHUNK = 4 * (-(-E // 512))
EP = NCHUNK * P
NB = NCHUNK // 4

QT = [6, 6, 6, 7]
QCOL = [0, 768, 1536, 2304]
QW = [768, 768, 768, NC - 2304]
QMAX = max(QW)
SW = 7 * P
M2, M3 = 4, 2
R2, R3 = C9 // M2, C3 // M3
HALF = NC // 2
SC = 7
SCW = NC // SC
HROW = C + GD + 2
CA = C + 1


def two_pi_parts():
    a = 6.28125
    b = float(np.float32(2 * np.pi - a))
    return a, b, float(2 * np.pi - a - b)


def build(nc, d, out):
    with ExitStack() as ctx:
        def sb(name, shape, dt):
            return ctx.enter_context(nc.sbuf_tensor(name, shape, dt))

        def sem(name):
            return ctx.enter_context(nc.semaphore(name))

        adj = sb("adj", [P, NT, NC], F16)
        big = sb("big", [P, 3600], F32)
        H = sb("H", [P, 7200], F16)
        S = sb("S", [P, 3, SW], F32)
        X = sb("X", [P, NT, C], F32)
        dinv_q = sb("dinv_q", [P, QMAX], F32)
        wreg = sb("wreg", [P, 1296], F32)
        bnst = sb("bnst", [P, M2, 8, 6], F32)
        mv = sb("mv", [P, M2, 2], F32)
        dinv = sb("dinv", [P, NT], F32)
        rdeg = sb("rdeg", [P, NT], F32)
        nvec = sb("nvec", [P, NT], F32)
        rtot = sb("rtot", [P, NT], F32)
        stat = sb("stat", [P, 2, NT], F32)
        sq = sb("sq", [P, C3], F32)
        comb = sb("comb", [P, C], F32)
        pidx = sb("pidx", [P, 1], F32)
        half = sb("half", [P, 1], F32)
        cols = sb("cols", [P, 31], F32)
        bias2 = sb("bias2", [P, M2], F32)
        bias3 = sb("bias3", [P, M3], F32)
        e1st = sb("e1st", [P, 2, 2, GD], F32)
        e1ix = sb("e1ix", [P, 2, 4], I32)
        ps = ctx.enter_context(nc.psum_tensor("ps", [P, 8, 512], F32))

        G_d = nc.dram_tensor("gate_edges", [NB, P, 4 * C], F32, kind="Internal").ap()
        E1_d = nc.dram_tensor("emb_src_edges", [NB, P, 4 * GD], F32, kind="Internal").ap()
        TN1_d = nc.dram_tensor("emb_nodes", [NP, GD], F32, kind="Internal").ap()
        HV_d = nc.dram_tensor("hv_nodes", [NP, HROW], F32, kind="Internal").ap()
        DI_d = nc.dram_tensor("dinv_row", [NP], F32, kind="Internal").ap()
        R2_d = nc.dram_tensor("relu2", [R2, M2, NC], F32, kind="Internal").ap()
        R3_d = nc.dram_tensor("relu3", [R3, M3, NC], F32, kind="Internal").ap()

        ID_d = nc.dram_tensor("identity", [P, P], F16, kind="Internal").ap()

        bigC3 = big[:, :].rearrange("p (t f) -> p t f", f=C3)
        hA = big[:, 0:1200].rearrange("p (t f) -> p t f", f=C)
        hT = big[:, 1200:2400].rearrange("p (t f) -> p t f", f=C)
        hY = big[:, 2400:3600].rearrange("p (t f) -> p t f", f=C)
        H1 = H[:, 0:2400].rearrange("p (t g h f) -> p t g h f", g=1, h=2, f=C)
        H3 = H[:, :].rearrange("p (t g h f) -> p t g h f", g=3, h=2, f=C)
        Hf = H[:, :].bitcast(F32)
        HfC3 = Hf.rearrange("p (t f) -> p t f", f=C3)
        Hf1 = Hf[:, 0:1200].rearrange("p (t f) -> p t f", f=C)
        rst = big[:, 0:M2 * QMAX].rearrange("p (m w) -> p m w", w=QMAX)
        Sflat = S[:, :, :].rearrange("p a b -> p (a b)")
        early = adj[:, :, :].rearrange("p a b -> p (a b)").bitcast(F32)
        typ = early[:, 0:NP].bitcast(I32)
        onehot_t = early[:, NP:2 * NP]
        tn = early[:, 2 * NP:2 * NP + NT * 66].rearrange("p (t f) -> p t f", f=66)
        nv_hi = early[:, 2 * NP + NT * 66:2 * NP + NT * 67].bitcast(F16)[:, 0:NT]
        nv_lo = early[:, 2 * NP + NT * 67:2 * NP + NT * 68].bitcast(F16)[:, 0:NT]
        wtm = wreg[:, 0:128]
        wt1 = wreg[:, 128:560]
        wt2 = wreg[:, 560:704]
        embT = wreg[0:GD, 704:704 + NEL]
        adaT = wreg[0:GD, 824:824 + GD]
        tt12 = wreg[0:NEL, 856:856 + 64]
        w1t = wreg[0:RBF, 1168:1296]
        w2b = wreg[0:C + 1, 968:1016]
        b1c = wreg[0:C, 1016:1017]
        tw = wreg[:, 1020:1040]
        ident16 = wreg[:, 1040:1104].bitcast(F16)
        iota16 = wreg[:, 1104:1168].bitcast(F16)
        dst_i = big[:, 0:NCHUNK].bitcast(I32)
        src_i = big[:, NCHUNK:2 * NCHUNK].bitcast(I32)
        c0i = big[0:1, 2 * NCHUNK:2 * NCHUNK + NWIN].bitcast(I32)
        dst_f = big[:, 1200:1200 + NCHUNK]
        hi_f = big[:, 1200 + NCHUNK:1200 + 2 * NCHUNK]
        lo_f = big[:, 1200 + 2 * NCHUNK:1200 + 3 * NCHUNK]
        cw = big[:, 1200 + 3 * NCHUNK:1200 + 4 * NCHUNK]
        wtab = big[:, 2864:2864 + NWIN]
        key = big[:, 3060:3060 + 48].rearrange("p (b t w k) -> p b t w k", b=2, t=3, w=2)
        last_i = big[0:104, 3108:3112].bitcast(I32)
        last_f = big[0:104, 3112:3116]
        ones1 = big[:, 3116:3117]
        rowsum = big[:, 3117:3118]
        flag_f = big[0:1, 3118:3119]
        flag_i = big[0:1, 3119:3120].bitcast(I32)
        gst = big[:, 3216:3600].rearrange("p (b f) -> p b f", b=2)
        mov = H[:, 0:3200].rearrange("p (b k n) -> p b k n", b=2, k=WCH)
        sta = H[:, 3200:4224].rearrange("p (b k n) -> p b k n", b=2, k=WCH)
        iota_w = dinv_q[:, 0:200].bitcast(F16)
        c0f = Hf[0:1, 3200:3200 + NWIN]
        degrow = H[0:1, 4224:4224 + 6 * SCW]
        degrow_end = dinv_q[0:1, 400:400 + SCW // 2].bitcast(F16)
        all_keys = Hf[:, 2400:2400 + NCHUNK]
        cmp_w = Hf[0:104, 2320:2320 + NWIN * 4].rearrange("p (g w) -> p g w", g=4)
        attr = Sflat[0:RBF, 0:1024].rearrange("p (b e) -> p b e", b=2)
        silu = Sflat[0:C + 1, 1024:2048].rearrange("p (b e) -> p b e", b=2)
        ones16 = dinv_q[:, 200:201].bitcast(F16)
        af = adj[:, :, :].rearrange("p a b -> p (a b)").bitcast(F32)
        iota_n = adj[:, 0, :]
        ohn = adj[:, 1:9, :].rearrange("p (b k) n -> p b k n", b=2)
        o0 = 9 * NC // 2
        ldst = Hf[:, 1200:1200 + NCHUNK].bitcast(I32)
        lsrc_i = Hf[:, 1200 + NCHUNK:1200 + 2 * NCHUNK].bitcast(I32)
        lsrc = Hf[:, 1200 + 2 * NCHUNK:1200 + 3 * NCHUNK]
        lcw = Hf[:, 1200 + 3 * NCHUNK:1200 + 4 * NCHUNK]
        cw_t = (Hf[:, 1200 + 4 * NCHUNK:1200 + 5 * NCHUNK], big[:, 2400:2400 + NCHUNK], big[:, 2400 + NCHUNK:2400 + 2 * NCHUNK])
        o1 = o0

        def late(words):
            nonlocal o1
            o1 += words
            return af[:, o1 - words:o1]

        lg = late(8 * C).rearrange("p (b k f) -> p b k f", b=2, k=4)
        le = late(8 * GD).rearrange("p (b k f) -> p b k f", b=2, k=4)
        lh = late(8 * HROW).rearrange("p (b k f) -> p b k f", b=2, k=4)
        ldot = late(8 * GD).rearrange("p (b k f) -> p b k f", b=2, k=4)
        la = late(8).rearrange("p (b k) -> p b k", b=2)
        lm = late(8 * C).rearrange("p (b k f) -> p b k f", b=2, k=4)
        lmh = late(8 * CA).bitcast(F16).rearrange("p (b k h f) -> p b k h f", b=2, k=4, h=2)
        lix = late(8).bitcast(I32).rearrange("p (b k) -> p b k", b=2)
        aggS = late(NP)
        combA = wreg[0:2 * CA, 0:CA]

        CB = {}
        at = 0
        for nm, w in (("btm", 1), ("freq", 1), ("bc1", M2), ("bt1", M2), ("g1", M2), ("be1", M2),
                      ("bc2", M3), ("bt2", M3), ("g2", M3), ("be2", M3), ("tstep", 1)):
            CB[nm] = (at, w)
            at += w

        def col(nm, rows=P):
            a, w = CB[nm]
            return cols[0:rows, a:a + w]

        names = """in_small in_edges in_types in_x in_cw tables_tt tables_T t_onehot t_mm t_evac tn_stored
            consts ones_row c0_cmp c0_sum c0_ready keys_prep dve_step pool_step
            t_emb t_mm1 t_rel t_mm2 bias_ready t_r
            key_ready onehots_built win_done win_evac
            attr_in0 attr_in1 z_done silu_done gate_done g_evac gstored0 gstored1 cw_ready
            pool_passed ones_ready deg_mm deg_row deg_tr rows_summed total_mm total_ready all_keys_ready all_onehots0 all_onehots1 all_used0 all_used1 all_step all_step_passed
            all_evac all_deg deg_col dinv_stored dinv_in
            var_ready std_ready h_scaled h_hi h_res h_ready spmm_done spmm_evac
            n1_done n1_evac nq_done nq_evac fe_done fe_evac r_stored bn_read
            bn_mm bn_cent bn_sq bn_aff
            w0_in w1_in w1_ready w2_in w3_in w4_in w6_in fold_t fold_mm fold_w ring0 ring1 ring2 ring3
            cv_done cv_evac tr_done tr_evac self_done self_evac
            ident_ready ident_kept ident_in flip_done flip_evac flip_cols adj_i adj_noi adj_t e1_in0 e1_in1 e1_got0 e1_got1 e1_st0 e1_st1
            hv_ready hv_stored late_in l_in0 l_in1 l_got0 l_got1 l_msg l_hi l_res l_lo l_oh l_mm
            agg_evac agg_mm out_ready out_done padz""".split()
        s = {n: sem(n) for n in names}

        class Chain:

            def __init__(self, eng, semaphore):
                self.eng, self.sem, self.n = eng, semaphore, 0

            def __call__(self, instruction):
                self.n += 1
                instruction.then_inc(self.sem, 1)
                self.eng.wait_ge(self.sem, self.n)

        block = ctx.enter_context(nc.Block())
        GCN_FEATURE = (1, 2)

        def turned(k):
            return dinv_q[0:C, 0:512] if k % 2 else S[0:C, 2, 0:512]

        GROUPS = [1, 3, 3, 1, 1, 1, 1, 1]
        UNIT0 = [4 * sum(GROUPS[:i]) for i in range(9)]
        NODE_ORDER = {3: 0, 4: 1, 5: 2, 6: 3, 7: 4}
        FLIPS = [(x, list(range(y, min(y + 4, x + 1)))) for x in range(NT) for y in range(0, x + 1, 4)]
        FLIP_COLS = [sum(any(y != x for y in ys) for x, ys in FLIPS[:k + 1]) for k in range(len(FLIPS))]
        PARTS = [(t, min(t + 5, NT)) for t in range(0, NT, 5)]
        NPART = len(PARTS)
        ENDS = [(0, 10, 7), (10, 20, 0), (20, NT, 1)]
        FE0 = {1: 0, 2: 4 * 2 * M2}

        def quarter_used(eng, i, q):
            if i == 0:
                eng.wait_ge(s["n1_done"], sum(QT[:q + 1]))
            elif i in GCN_FEATURE:
                eng.wait_ge(s["fe_done"], FE0[i] + 2 * (M2 if i == 1 else M3) * (q + 1))
            else:
                eng.wait_ge(s["nq_done"], 4 * NODE_ORDER[i] + q + 1)

        def bc(ap, n):
            return ap.broadcast_to(n)

        def pb(name, n=P):
            return d[name][None, :].broadcast_to([n, d[name].shape[0]])

        small = [(wtm, d["Wtm"]), (wt1, d["Wt1"]), (wt2, d["Wt2"]), (embT, d["embT"]), (adaT, d["adaT"]),
                 (tt12[:, 0:GD], d["emb"]), (w1t[:, 0:C], d["W1T"]), (w2b[0:C, :], d["W2T"]),
                 (w2b[C:C + 1, :], d["b2"][None, :]), (b1c, d["b1"][:, None]),
                 (col("btm"), d["btm"][:, None]), (col("freq"), d["freq"][:, None]),
                 (col("tstep"), d["timestep"][None, :].broadcast_to([P, 1])), (nvec[:, :], d["node_vec"])]
        for nm, r in (("bc1", R2), ("bt1", R2), ("g1", R2), ("be1", R2),
                      ("bc2", R3), ("bt2", R3), ("g2", R3), ("be2", R3)):
            small.append((col(nm, r), d[nm]))

        @block.sync
        def _(sp):
            sp.dma_start(dst_i, d["dst"]).then_inc(s["in_edges"], 16)
            sp.dma_start(src_i, d["src"]).then_inc(s["in_edges"], 16)
            sp.dma_start(last_i, d["dst"][P - 1:P, :].rearrange("o (p g) -> (o p) g", g=4)).then_inc(s["in_edges"], 16)
            sp.dma_start(cw, d["edge_weight"]).then_inc(s["in_cw"], 16)
            for o, i in small[:11]:
                sp.dma_start(o, i).then_inc(s["in_small"], 16)
            sp.dma_start(typ[0:NEL, :], d["node_type"][None, :].broadcast_to([NEL, NP])).then_inc(s["in_types"], 16)
            sp.dma_start(X[:, :, :], d["x"].rearrange("(t p) f -> p t f", p=P)).then_inc(s["in_x"], 16)
            sp.wait_ge(s["ident_ready"], 1)
            sp.dma_start(ID_d, ident16).then_inc(s["ident_kept"], 16)
            sp.wait_ge(s["padz"], 1)

            def load_attr(b, par):
                sp.wait_ge(s["silu_done"], b + 1)
                sp.dma_start(attr[:, par, :], d["edge_attr"][:, bass.ds(b * 512, 512)]).then_inc(s[f"attr_in{par}"], 16)

            def store_gate(b, par):
                sp.wait_ge(s["g_evac"], b + 3)
                sp.dma_start(G_d[bass.ds(b, 1), :, :].rearrange("o p f -> (o p) f"), gst[:, par, :]).then_inc(s[f"gstored{par}"], 16)

            load_attr(0, 0)
            load_attr(1, 1)
            sp.wait_ge(s["t_evac"], 4)
            sp.dma_start(TN1_d.rearrange("(t p) f -> p t f", p=P), tn[:, :, 0:GD]).then_inc(s["tn_stored"], 16)
            sp.dma_start(HV_d[:, C:HROW].rearrange("(t p) f -> p t f", p=P), tn[:, :, GD:2 * GD + 2]).then_inc(s["tn_stored"], 16)
            w = wreg
            for o, i in ((w[0:C, 0:C3], d["W_in"]), (w[C:C2P, 0:C3], d["W_in"]), (w[:, C3:2 * C3], pb("b_in")),
                         (w[:, 2 * C3:3 * C3], pb("g_in")), (w[:, 3 * C3:4 * C3], pb("be_in"))):
                sp.dma_start(o, i).then_inc(s["w0_in"], 16)
            with sp.Fori(0, NB // 2 - 1) as i:
                load_attr(i * 2 + 2, 0)
                load_attr(i * 2 + 3, 1)
                store_gate(i * 2, 0)
                store_gate(i * 2 + 1, 1)
            store_gate(NB - 2, 0)
            store_gate(NB - 1, 1)
            sp.wait_ge(s["deg_col"], 1)
            sp.dma_start(DI_d.rearrange("(t p) -> p t", p=P), dinv[:, :], allow_slow_non_contiguous=True).then_inc(s["dinv_stored"], 16)
            sp.wait_ge(s["dinv_stored"], 16)

            def dinv_quarter(i, q):
                k = 4 * (i - 1) + q
                if k:
                    sp.wait_ge(s["spmm_evac"], UNIT0[i] + 3 * q)
                sp.dma_start(dinv_q[:, 0:QW[q]], DI_d[None, QCOL[q]:QCOL[q] + QW[q]].broadcast_to([P, QW[q]])).then_inc(s["dinv_in"], 16)

            def store_relu(i, q, dram, rows, m):
                k0 = FE0[i] + 2 * m * (q + 1)
                sp.wait_ge(s["fe_evac"], k0)
                sp.dma_start(dram[:, :, QCOL[q]:QCOL[q] + QW[q]], rst[0:rows, 0:m, 0:QW[q]]).then_inc(s["r_stored"], 16)

            def ring_tiles(i, dram, rows, m):
                for t in range(NT):
                    k = NT * (i - 1) + t
                    if t >= 4:
                        sp.wait_ge(s["cv_done"], NT * (i - 1) + t - 3)
                    wd = min(P, NC - P * t)
                    slot = Sflat[0:rows, (t % 4) * 512:(t % 4) * 512 + m * P].rearrange("p (m n) -> p m n", m=m)
                    sp.dma_start(slot[:, :, 0:wd], dram[:, :, P * t:P * t + wd]).then_inc(s[f"ring{t % 4}"], 16)

            sp.wait_ge(s["bn_aff"], 1)
            for o, i in ((w[0:C, :], 0), (w[C:C2P, :], 0)):
                sp.dma_start(o.rearrange("p (g f) -> p g f", g=3), d["Wc1"].rearrange("(g p) f -> p g f", g=3)).then_inc(s["w1_in"], 16)
            for q in range(4):
                dinv_quarter(1, q)
                if q:
                    store_relu(1, q - 1, R2_d, R2, M2)
            store_relu(1, 3, R2_d, R2, M2)
            quarter_used(sp, 1, 3)
            sp.dma_start(w[0:R2, 0:M2 * C3].rearrange("p (m f) -> p m f", m=M2), d["Wc2"].rearrange("(m p) f -> p m f", m=M2)).then_inc(s["w2_in"], 16)
            sp.wait_ge(s["r_stored"], 64)
            ring_tiles(1, R2_d, R2, M2)
            for q in range(4):
                dinv_quarter(2, q)
                if q:
                    store_relu(2, q - 1, R3_d, R3, M3)
            store_relu(2, 3, R3_d, R3, M3)
            quarter_used(sp, 2, 3)
            sp.wait_ge(s["ident_kept"], 16)
            sp.dma_start(ident16, ID_d).then_inc(s["ident_in"], 16)
            sp.dma_start(w[0:R3, 0:M3 * C].rearrange("p (m f) -> p m f", m=M3), d["W_out"].rearrange("(m p) f -> p m f", m=M3)).then_inc(s["w3_in"], 16)
            for k, nm in enumerate(("b_out", "g_out", "be_out")):
                sp.dma_start(w[:, C3 + C * k:C3 + C * k + C], pb(nm)).then_inc(s["w3_in"], 16)
            sp.wait_ge(s["r_stored"], 128)
            ring_tiles(2, R3_d, R3, M3)
            sp.wait_ge(s["bn_aff"], 2)
            for k, nm in enumerate(("W_self1", "W_neigh1", "sb1", "W_self2", "W_neigh2", "sb2")):
                if nm[0] == "s":
                    sp.dma_start(w[:, C * k:C * k + C], pb(nm)).then_inc(s["w4_in"], 16)
                else:
                    sp.dma_start(w[0:C, C * k:C * k + C], d[nm]).then_inc(s["w4_in"], 16)
                    if "neigh" in nm:
                        sp.dma_start(w[C:C2P, C * k:C * k + C], d[nm]).then_inc(s["w4_in"], 16)
            sp.wait_ge(s["adj_t"], 1)
            for k, nm in enumerate(("gamma", "beta")):
                sp.dma_start(w[:, 512 + C * k:512 + C * k + C], pb(nm)).then_inc(s["w6_in"], 16)
            sp.dma_start(ldst, d["dst"]).then_inc(s["late_in"], 16)
            sp.dma_start(lsrc_i, d["src"]).then_inc(s["late_in"], 16)
            sp.dma_start(lcw, d["edge_weight"]).then_inc(s["late_in"], 16)
            for q in range(4):
                sp.wait_ge(s["hv_ready"], q + 1)
                t0, t1 = 6 * q, 6 * q + QT[q]
                sp.dma_start(HV_d[P * t0:P * t1, 0:C].rearrange("(t p) f -> p t f", p=P), hT[:, t0:t1, :]).then_inc(s["hv_stored"], 16)
            sp.wait_ge(s["e1_st0"], 16 * NB)
            sp.wait_ge(s["e1_st1"], 16 * NB)

            def load_late(b, par):
                sp.wait_ge(s["l_msg"], b + 1)
                sp.dma_start(lg[:, par, :, :].rearrange("p k f -> p (k f)"), G_d[bass.ds(b, 1), :, :].rearrange("o p f -> (o p) f")).then_inc(s[f"l_in{par}"], 16)
                sp.dma_start(le[:, par, :, :].rearrange("p k f -> p (k f)"), E1_d[bass.ds(b, 1), :, :].rearrange("o p f -> (o p) f")).then_inc(s[f"l_in{par}"], 16)

            with sp.Fori(0, NB // 2) as i:
                load_late(i * 2, 0)
                load_late(i * 2 + 1, 1)
            for j, (t0, t1, _bank) in enumerate(ENDS):
                sp.wait_ge(s["out_ready"], j + 1)
                full = min(t1, NT - 1)
                sp.dma_start(out[P * t0:P * full, :].rearrange("(t p) f -> p t f", p=P), X[:, t0:full, :]).then_inc(s["out_done"], 16)
            sp.dma_start(out[P * (NT - 1):N, :], X[0:TAIL, NT - 1, :]).then_inc(s["out_done"], 16)
            sp.wait_ge(s["out_done"], 16 * (len(ENDS) + 1))

        @block.gpsimd
        def _(pool):
            g = nc.gpsimd
            step = Chain(pool, s["pool_step"])
            g.iota(pidx[:, :], [[0, 1]], base=0, channel_multiplier=1, allow_small_or_imprecise_dtypes=True).then_inc(s["consts"], 1)
            g.iota(iota16, [[1, P]], base=0, channel_multiplier=0, allow_small_or_imprecise_dtypes=True).then_inc(s["consts"], 1)
            g.iota(iota_w, [[CODE, NT], [1, WIN]], base=0, channel_multiplier=0, allow_small_or_imprecise_dtypes=True).then_inc(s["consts"], 1)
            g.memset(ones16, 1.0).then_inc(s["ones_ready"], 1)
            g.iota(wtab, [[WIN, NWIN]], base=0, channel_multiplier=0, allow_small_or_imprecise_dtypes=True).then_inc(s["consts"], 1)
            pool.wait_ge(s["consts"], 4)
            pool.wait_ge(s["keys_prep"], 1)
            pool.wait_ge(s["c0_ready"], 1)

            def pair_keys(pair, slot):
                w = pair * 2
                pool.wait_ge(s["onehots_built"], w + 1)
                c0 = [pool.value_load(c0i[0:1, bass.ds(w + j, 1)], min_val=0, max_val=NCHUNK - WCH) for j in range(2)]
                for j in range(2):
                    g.tensor_copy(key[:, slot, 2, j, :], lo_f[:, bass.ds(c0[j], WCH)])
                    ins = g.tensor_tensor(key[:, slot, 1, j, :], dst_f[:, bass.ds(c0[j], WCH)],
                                          bc(wtab[:, bass.ds(w + j, 1)], [P, WCH]), ALU.subtract)
                ins.then_inc(s["pool_step"], 1)
                pool.wait_ge(s["pool_step"], w + 1)
                pool.sem_inc(s["pool_passed"], 1)
                g.tensor_scalar(key[:, slot, 1, :, :], key[:, slot, 1, :, :], float(WIN), -1.0, ALU.min, ALU.max).then_inc(s["pool_step"], 1)
                pool.wait_ge(s["pool_step"], w + 2)
                for j in range(2):
                    ins = g.tensor_tensor(key[:, slot, 0, j, :], key[:, slot, 1, j, :], hi_f[:, bass.ds(c0[j], WCH)], ALU.add)
                ins.then_inc(s["key_ready"], 1)

            with pool.Fori(0, NWIN // 4) as i:
                pair_keys(i * 2, 0)
                pair_keys(i * 2 + 1, 1)

            def load_sources(b, par):
                pool.dma_start(e1ix[:, par, :], d["src"][:, bass.ds(b * 4, 4)]).then_inc(s[f"e1_in{par}"], 16)

            def gather_half(b, par, h, turn):
                if turn is not None:
                    pool.wait_ge(s[f"e1_st{h}"], turn)
                    pool.sem_inc(s["pool_passed"], 1)
                for k in range(2):
                    g.indirect_dma_start(out=e1st[:, h, k, :], out_offset=None, in_=TN1_d,
                                         in_offset=bass.IndirectOffsetOnAxis(ap=e1ix[:, par, 2 * h + k:2 * h + k + 1], axis=0)).then_inc(s[f"e1_got{h}"], 16)

            def store_half(b, h, turn):
                pool.wait_ge(s[f"e1_got{h}"], turn)
                pool.dma_start(E1_d[bass.ds(b, 1), :, 2 * GD * h:2 * GD * h + 2 * GD].rearrange("o p f -> (o p) f"),
                               e1st[:, h, :, :].rearrange("p k f -> p (k f)")).then_inc(s[f"e1_st{h}"], 16)

            def gather_batch(i, par, more=True):
                b = i * 2 + par
                pool.wait_ge(s[f"e1_in{par}"], i * 16 + 16)
                pool.sem_inc(s["pool_passed"], 1)
                first = isinstance(b, int) and b == 0
                gather_half(b, par, 0, None if first else b * 16)
                gather_half(b, par, 1, None if first else b * 16)
                store_half(b, 0, b * 32 + 32)
                store_half(b, 1, b * 32 + 32)
                if more:
                    load_sources(b + 2, par)

            pool.wait_ge(s["tn_stored"], 32)
            load_sources(0, 0)
            load_sources(1, 1)
            gather_batch(0, 0)
            gather_batch(0, 1)
            with pool.Fori(1, NB // 2 - 1) as i:
                gather_batch(i, 0)
                gather_batch(i, 1)
            gather_batch(NB // 2 - 1, 0, more=False)
            gather_batch(NB // 2 - 1, 1, more=False)
            pool.wait_ge(s["spmm_done"], UNIT0[8])
            g.iota(iota_n, [[1, NC]], base=-(NC // 2), channel_multiplier=0, allow_small_or_imprecise_dtypes=True).then_inc(s["consts"], 1)
            pool.wait_ge(s["hv_stored"], 64)
            pool.wait_ge(s["late_in"], 48)

            def gather_dst(b, par):
                pool.wait_ge(s["l_hi"], b + 1)
                g.tensor_copy(lix[:, par, :], ldst[:, bass.ds(b * 4, 4)]).then_inc(s["pool_step"], 1)
                pool.wait_ge(s["pool_step"], b + (NWIN + 1))
                pool.sem_inc(s["pool_passed"], 1)
                for k in range(4):
                    g.indirect_dma_start(out=lh[:, par, k, :], out_offset=None, in_=HV_d,
                                         in_offset=bass.IndirectOffsetOnAxis(ap=lix[:, par, k:k + 1], axis=0)).then_inc(s[f"l_got{par}"], 16)

            with pool.Fori(0, NB // 2) as i:
                gather_dst(i * 2, 0)
                gather_dst(i * 2 + 1, 1)

        @block.vector
        def _(dve):
            v = nc.vector
            step = Chain(dve, s["dve_step"])
            dve.sem_inc(s["onehots_built"], 3)
            dve.sem_inc(s["g_evac"], 2)
            step(v.memset(w1t[:, C:P], 0.0))
            dve.wait_ge(s["consts"], 2)
            step(v.tensor_scalar(half[:, :], pidx[:, :], float(C), 1.0 / LOW - 1.0, ALU.is_ge, ALU.mult))
            step(v.tensor_scalar(half[:, :], half[:, :], 1.0, None, ALU.add))
            step(v.tensor_scalar(sq[:, 0:C], iota16[:, 0:C], pidx[:, 0:1], None, ALU.is_equal))
            step(v.tensor_scalar(sq[:, C:C + 1], pidx[:, :], -float(C), None, ALU.add))
            step(v.tensor_scalar(comb[:, :], iota16[:, 0:C], sq[:, C:C + 1], None, ALU.is_equal))
            step(v.tensor_tensor(comb[:, :], comb[:, :], sq[:, 0:C], ALU.add))
            step(v.tensor_scalar(comb[:, :], comb[:, :], half[:, 0:1], None, ALU.mult))
            v.tensor_scalar(ident16, iota16, pidx[:, 0:1], None, ALU.is_equal).then_inc(s["ident_ready"], 1)
            dve.wait_ge(s["in_edges"], 48)
            step(v.tensor_copy(last_f, last_i))
            v.memset(ones1, 1.0).then_inc(s["ones_row"], 1)
            dve.wait_ge(s["consts"], 4)
            for k in range(4):
                v.tensor_scalar(cmp_w[:, k, :], wtab[0:104, :], last_f[:, k:k + 1], None, ALU.is_gt).then_inc(s["c0_cmp"], 1)
            step(v.tensor_copy(dst_f, dst_i))
            step(v.tensor_scalar(dst_i, src_i, 7, 6, ALU.arith_shift_right, ALU.logical_shift_left))
            step(v.tensor_copy(hi_f, dst_i))
            step(v.tensor_scalar(dst_i, src_i, P - 1, None, ALU.bitwise_and))
            v.tensor_copy(lo_f, dst_i).then_inc(s["keys_prep"], 1)
            dve.wait_ge(s["c0_sum"], 1)
            step(v.tensor_scalar(c0f, ps[0:1, 3, 0:NWIN], float(NCHUNK - WCH), None, ALU.min))
            v.tensor_copy(c0i, c0f).then_inc(s["c0_ready"], 1)
            dve.wait_ge(s["in_small"], 16 * 22)
            A, B, D = two_pi_parts()
            ang, kk, r, ph = tw[:, 0:1], tw[:, 1:2], tw[:, 2:3], tw[:, 3:4]
            step(v.tensor_tensor(ang, col("tstep"), col("freq"), ALU.mult))
            step(v.tensor_scalar(ph, pidx[:, :], 64.0, float(np.pi / 2), ALU.is_ge, ALU.mult))
            step(v.tensor_tensor(kk, ang, ph, ALU.add))
            step(v.tensor_scalar(kk, kk, float(1 / (2 * np.pi)), 12582912.0, ALU.mult, ALU.add))
            step(v.tensor_scalar(kk, kk, -12582912.0, None, ALU.add))
            step(v.scalar_tensor_tensor(r, kk, -A, ang, ALU.mult, ALU.add))
            step(v.scalar_tensor_tensor(r, kk, -B, r, ALU.mult, ALU.add))
            step(v.tensor_tensor(r, r, ph, ALU.add))
            step(v.scalar_tensor_tensor(r, kk, -D, r, ALU.mult, ALU.add))
            v.tensor_scalar(r, r, 3.1415925, -3.1415925, ALU.min, ALU.max).then_inc(s["t_r"], 1)
            dve.wait_ge(s["t_mm1"], 1)
            step(v.tensor_tensor(tw[:, 5:6], ps[:, 0, 0:1], col("btm"), ALU.add))
            v.tensor_scalar(tw[:, 5:6], tw[:, 5:6], 0.0, None, ALU.max).then_inc(s["t_rel"], 1)
            dve.wait_ge(s["t_mm2"], 1)
            step(v.tensor_tensor(bias2[0:R2, :], ps[0:R2, 1, 0:M2], col("bt1", R2), ALU.add))
            step(v.tensor_scalar(bias2[0:R2, :], bias2[0:R2, :], 0.0, None, ALU.max))
            step(v.tensor_tensor(bias2[0:R2, :], bias2[0:R2, :], col("bc1", R2), ALU.add))
            step(v.tensor_tensor(bias3[0:R3, :], ps[0:R3, 1, M2:M2 + M3], col("bt2", R3), ALU.add))
            step(v.tensor_scalar(bias3[0:R3, :], bias3[0:R3, :], 0.0, None, ALU.max))
            v.tensor_tensor(bias3[0:R3, :], bias3[0:R3, :], col("bc2", R3), ALU.add).then_inc(s["bias_ready"], 1)
            dve.wait_ge(s["tables_T"], 1)
            v.tensor_copy(tt12[:, GD:2 * GD], ps[0:NEL, 2, 0:GD]).then_inc(s["tables_tt"], 1)
            dve.wait_ge(s["in_types"], 16)
            v.tensor_scalar(onehot_t[0:NEL, :], typ[0:NEL, :], pidx[0:NEL, 0:1], None, ALU.is_equal).then_inc(s["t_onehot"], 1)
            dve.wait_ge(s["in_cw"], 16)

            def cutoff(wd, k, r, m, act_at):
                step(v.tensor_scalar(k, wd, 1.0 / 12.0, 12582912.0, ALU.mult, ALU.add))
                step(v.tensor_scalar(k, k, -12582912.0, None, ALU.add))
                step(v.scalar_tensor_tensor(r, k, -12.0, wd, ALU.mult, ALU.add))
                step(v.tensor_scalar(k, r, -1.0, None, ALU.mult))
                step(v.tensor_tensor(r, r, k, ALU.max))
                step(v.tensor_scalar(r, r, float(-np.pi / 6), float(np.pi / 2), ALU.mult, ALU.add))
                v.tensor_scalar(m, wd, 6.0, 0.5, ALU.is_lt, ALU.mult).then_inc(s["cw_ready"], 1)
                dve.wait_ge(s["t_emb"], act_at)
                dve.wait_ge(s["cw_ready"], 1 if act_at == 2 else 2)
                step(v.tensor_scalar(r, r, 1.0, None, ALU.add))
                step(v.tensor_tensor(wd, r, m, ALU.mult))

            cutoff(cw, Sflat[:, 0:NCHUNK], Sflat[:, NCHUNK:2 * NCHUNK], Sflat[:, 2 * NCHUNK:3 * NCHUNK], 2)
            v.memset(silu[:, :, :], 1.0).then_inc(s["padz"], 1)

            step(v.tensor_copy(nv_hi, nvec[:, :]))
            step(v.tensor_tensor(tn[:, :, 2 * GD + 1], nvec[:, :], nv_hi, ALU.subtract))
            step(v.tensor_scalar(tn[:, :, 2 * GD + 1], tn[:, :, 2 * GD + 1], LOW, None, ALU.mult))
            v.tensor_copy(nv_lo, tn[:, :, 2 * GD + 1])
            step(v.tensor_copy(tn[:, :, 2 * GD], nv_hi))
            step(v.tensor_copy(tn[:, :, 2 * GD + 1], nv_lo))
            for j in range(4):
                n = min(8, NT - 8 * j)
                dve.wait_ge(s["t_mm"], j + 1)
                v.tensor_copy(tn[:, 8 * j:8 * j + n, 0:2 * GD], ps[:, 4 + j, 0:64 * n].rearrange("p (t f) -> p t f", f=64)).then_inc(s["t_evac"], 1)

            def window_onehots(pair, slot, half_):
                w, par = pair * 2 + half_, half_
                if half_ == 0:
                    dve.wait_ge(s["key_ready"], pair + 1)
                dve.wait_ge(s["win_done"], w + 1)
                for k in range(WCH):
                    v.tensor_scalar(mov[:, par, k, :], iota_w, key[:, slot, 0, half_, k:k + 1], None, ALU.is_equal)
                    last = v.tensor_scalar(sta[:, par, k, :], iota16, key[:, slot, 2, half_, k:k + 1], None, ALU.is_equal)
                last.then_inc(s["onehots_built"], 1)

            def gate_out(b, par, turn):
                dve.wait_ge(s["gate_done"], b + 3)
                if not (isinstance(turn, int) and turn == 0):
                    dve.wait_ge(s[f"gstored{par}"], turn * 16)
                v.tensor_tensor(gst[:, par, :].rearrange("p (k f) -> p k f", k=4), ps[:, 4 + par, 0:4 * C].rearrange("p (k f) -> p k f", k=4),
                                bc(cw[:, bass.ds(b * 4, 4)].unsqueeze(2), [P, 4, C]), ALU.mult).then_inc(s["g_evac"], 1)

            def windows_and_gates(i):
                window_onehots(i * 2, 0, 0)
                window_onehots(i * 2, 0, 1)
                if not isinstance(i, int):
                    gate_out(i * 2 - 1, 1, i - 1)
                window_onehots(i * 2 + 1, 1, 0)
                window_onehots(i * 2 + 1, 1, 1)
                gate_out(i * 2, 0, i)

            windows_and_gates(0)
            with dve.Fori(1, NWIN // 4) as i:
                windows_and_gates(i)
            gate_out(2 * (NWIN // 4) - 1, 1, NWIN // 4 - 1)
            nsq = [0]

            def sqrt_of(a, n, rows=P, meanwhile=()):
                nsq[0] += 1
                v.tensor_copy(sq[0:rows, 0:n], a).then_inc(s["var_ready"], 1)
                for b in meanwhile:
                    gate_out(b, b % 2, b // 2)
                dve.wait_ge(s["std_ready"], nsq[0])

            def layernorm(out_h, tmp, positive=True, src=None, meanwhile=(), tiles=(0, NT)):
                t0, t1 = tiles
                n = t1 - t0
                src = (X[:, :, :] if src is None else src)[:, t0:t1, :]
                out_h, tmp = out_h[:, t0:t1, :], tmp[:, t0:t1, :]
                mean, var = stat[:, 0, t0:t1], stat[:, 1, t0:t1]
                step(v.tensor_reduce(mean, src, AX, ALU.add))
                step(v.tensor_scalar(mean, mean, 1.0 / C, None, ALU.mult))
                step(v.tensor_tensor(out_h, src, bc(mean.unsqueeze(2), [P, n, C]), ALU.subtract))
                step(v.tensor_tensor(tmp, out_h, out_h, ALU.mult))
                step(v.tensor_reduce(var, tmp, AX, ALU.add))
                step(v.tensor_scalar(var, var, 1.0 / C, EPS, ALU.mult, ALU.add))
                sqrt_of(var, n, meanwhile=meanwhile)
                step(v.reciprocal(var, sq[:, 0:n]))
                scale = bc(var.unsqueeze(2), [P, n, C])
                if positive:
                    step(v.scalar_tensor_tensor(out_h, out_h, 0.0, scale, ALU.max, ALU.mult))
                else:
                    step(v.tensor_tensor(out_h, out_h, scale, ALU.mult))

            dve.wait_ge(s["in_x"], 16)
            dve.wait_ge(s["win_done"], NWIN + 2)
            layernorm(hA, Hf1, meanwhile=(NB - 6, NB - 5))

            def read_degrees(step):
                step(v.memset(stat[:, 0, :], 0.0))
                step(v.tensor_copy(stat[:, 0, 0:NT - 1], ps[:, 7, 0:NT - 1]))
                step(v.tensor_copy(stat[0:NC - P * (NT - 1), 0, NT - 1:NT], ps[0:NC - P * (NT - 1), 7, NT - 1:NT]))

            dve.wait_ge(s["deg_tr"], 1)
            read_degrees(step)
            v.tensor_reduce(rowsum, stat[:, 0, :], AX, ALU.add).then_inc(s["rows_summed"], 1)
            for b in (NB - 4, NB - 3):
                gate_out(b, b % 2, b // 2)
            dve.wait_ge(s["total_mm"], 1)
            step(v.tensor_scalar(flag_f, ps[0:1, 6, 0:1], float(E), None, ALU.not_equal))
            step(v.tensor_copy(flag_i, flag_f))
            dve.sem_inc(s["total_ready"], 1)
            missed = dve.value_load(flag_i, min_val=0, max_val=1)
            with dve.If(missed > 0):
                dve.sem_inc(s["all_evac"], 1)
                with dve.Fori(0, NWIN) as w:
                    v.tensor_tensor(all_keys, dst_f, bc(wtab[:, bass.ds(w, 1)], [P, NCHUNK]), ALU.subtract).then_inc(s["all_keys_ready"], 1)
                    dve.wait_ge(s["all_keys_ready"], w * 3 + 1)
                    v.tensor_scalar(all_keys, all_keys, float(WIN), -1.0, ALU.min, ALU.max).then_inc(s["all_keys_ready"], 1)
                    dve.wait_ge(s["all_keys_ready"], w * 3 + 2)
                    v.tensor_tensor(all_keys, all_keys, hi_f, ALU.add).then_inc(s["all_keys_ready"], 1)
                    dve.wait_ge(s["all_keys_ready"], w * 3 + 3)
                    dve.sem_inc(s["all_step_passed"], 1)
                    with dve.Fori(0, NB // 2) as g:
                        for slot in range(2):
                            dve.wait_ge(s[f"all_used{slot}"], w * (NB // 2) + g + 1)
                            for k in range(WCH):
                                c = g * (2 * WCH) + (WCH * slot + k)
                                v.tensor_scalar(mov[:, slot, k, :], iota_w, all_keys[:, bass.ds(c, 1)], None, ALU.is_equal)
                                ins = v.tensor_scalar(sta[:, slot, k, :], iota16, lo_f[:, bass.ds(c, 1)], None, ALU.is_equal)
                            ins.then_inc(s[f"all_onehots{slot}"], 1)
                    dve.wait_ge(s["all_used1"], w * (NB // 2) + (NB // 2 + 1))
                    v.tensor_copy(adj[:, :, bass.ds(w * WIN, WIN)], ps[:, 0, 0:NT * WIN].rearrange("p (s x) -> p s x", x=WIN)).then_inc(s["all_evac"], 1)
                dve.wait_ge(s["all_deg"], 1)
                read_degrees(Chain(dve, s["all_step"]))

            def diagonal(op):
                for t in range(NT):
                    wd = min(P, NC - P * t)
                    i = v.tensor_tensor(adj[0:wd, t, P * t:P * t + wd], adj[0:wd, t, P * t:P * t + wd], ident16[0:wd, 0:wd], op)
                return i

            diagonal(ALU.add).then_inc(s["adj_i"], 1)
            step(v.tensor_scalar(stat[:, 1, :], stat[:, 0, :], 1.0, None, ALU.add))
            step(v.tensor_scalar(rdeg[:, :], stat[:, 0, :], 1.0, None, ALU.max))
            step(v.reciprocal(rdeg[:, :], rdeg[:, :]))
            sqrt_of(stat[:, 1, :], NT, meanwhile=(NB - 2, NB - 1))
            v.reciprocal(dinv[:, :], sq[:, 0:NT]).then_inc(s["deg_col"], 1)
            dve.wait_ge(s["deg_col"], 1)
            step(v.memset(Sflat[:, :], 0.0))

            nsplit = [0]

            def split(val, hview, scale=None, rest=None, relu=False):
                k = nsplit[0] = nsplit[0] + NPART
                k -= NPART
                rest = val if rest is None else rest

                def scaled(n):
                    if n == NPART:
                        return
                    a_, b_ = PARTS[n]
                    x_ = val[:, a_:b_, :]
                    if scale is None:
                        dve.sem_inc(s["h_scaled"], 1)
                    elif relu:
                        v.scalar_tensor_tensor(x_, x_, 0.0, bc(scale[:, a_:b_].unsqueeze(2), list(x_.shape)), ALU.max, ALU.mult).then_inc(s["h_scaled"], 1)
                    else:
                        v.tensor_tensor(x_, x_, bc(scale[:, a_:b_].unsqueeze(2), list(x_.shape)), ALU.mult).then_inc(s["h_scaled"], 1)

                scaled(0)
                for n, (a_, b_) in enumerate(PARTS):
                    scaled(n + 1)
                    if scale is not None:
                        dve.wait_ge(s["h_scaled"], k + n + 1)
                    dve.wait_ge(s["h_hi"], k + n + 1)
                    grouped = "p t (g f) -> p t g f"
                    v.tensor_tensor(rest[:, a_:b_, :].rearrange(grouped, f=C), val[:, a_:b_, :].rearrange(grouped, f=C), hview[:, a_:b_, :, 0, :],
                                    ALU.subtract).then_inc(s["h_res"], 1)

            def bn_nodes(k, val, F, gB, bB):
                dve.wait_ge(s["bn_mm"], 2 * k + 1)
                step(v.tensor_scalar(sq[:, 0:F], ps[:, 4, 0:F], 1.0 / N, None, ALU.mult))
                for a_, b_ in PARTS:
                    v.tensor_tensor(val[:, a_:b_, :], val[:, a_:b_, :], bc(sq[:, 0:F].unsqueeze(1), [P, b_ - a_, F]), ALU.subtract).then_inc(s["bn_cent"], 1)
                dve.wait_ge(s["bn_cent"], NPART * (k + 1))
                dve.wait_ge(s["bn_mm"], 2 * k + 2)
                step(v.tensor_scalar(sq[:, 0:F], ps[:, 5, 0:F], 1.0 / N, EPS, ALU.mult, ALU.add))
                nsq[0] += 1
                dve.sem_inc(s["var_ready"], 1)
                dve.wait_ge(s["std_ready"], nsq[0])
                step(v.reciprocal(sq[:, 0:F], sq[:, 0:F]))
                step(v.tensor_tensor(sq[:, 0:F], sq[:, 0:F], gB, ALU.mult))
                step(v.tensor_tensor(val, val, bc(sq[:, 0:F].unsqueeze(1), [P, NT, F]), ALU.mult))
                step(v.tensor_tensor(val, val, bc(bB.unsqueeze(1), [P, NT, F]), ALU.add))
                dve.sem_inc(s["bn_aff"], 1)

            split(hA, H1, dinv)
            dve.wait_ge(s["w0_in"], 80)
            step(v.memset(wreg[:, 576:704], 1.0))
            v.tensor_scalar(wreg[0:C2P, 0:C3], wreg[0:C2P, 0:C3], half[0:C2P, 0:1], None, ALU.mult).then_inc(s["w1_ready"], 1)
            for par in range(2):
                dve.wait_ge(s[f"gstored{par}"], 16 * (NB // 2))
            for t in range(NT):
                dve.wait_ge(s["n1_done"], t + 1)
                i = v.scalar_tensor_tensor(bigC3[:, t, :], ps[:, 4 + t % 4, 0:C3], dinv[:, t:t + 1], wreg[:, C3:2 * C3],
                                           ALU.mult, ALU.add).then_inc(s["n1_evac"], 1)
            dve.wait_ge(s["n1_evac"], NT)
            bn_nodes(0, bigC3, C3, wreg[:, 2 * C3:3 * C3], wreg[:, 3 * C3:4 * C3])
            split(bigC3, H3, dinv, relu=True)
            dve.wait_ge(s["w1_in"], 32)
            v.tensor_scalar(wreg[0:C2P, :], wreg[0:C2P, :], half[0:C2P, 0:1], None, ALU.mult).then_inc(s["w1_ready"], 1)

            def out_degree(t):
                v.tensor_reduce(rtot[:, t:t + 1], adj[:, t, :], AX, ALU.add)

            def feature_conv(i, rows, m):
                for q in range(4):
                    for gi in range(3):
                        u = UNIT0[i] + 3 * q + gi
                        dve.wait_ge(s["spmm_done"], u + 1)
                        if gi == 0:
                            dve.wait_ge(s["dinv_in"], 16 * (4 * (i - 1) + q + 1))
                            if q:
                                quarter_used(dve, i, q - 1)
                        bank = 2 * (u % 2)
                        hw = QW[q] // 2
                        v.tensor_tensor(S[0:C2P, gi, 0:QW[q]].rearrange("p (c w) -> p c w", c=2), ps[0:C2P, bank:bank + 2, 0:hw],
                                        dinv_q[0:C2P, 0:QW[q]].rearrange("p (c w) -> p c w", c=2), ALU.mult).then_inc(s["spmm_evac"], 1)
                        out_degree(12 * (i - 1) + 3 * q + gi)
                    if q:
                        stats_of(i, q - 1, rows, m)
                stats_of(i, 3, rows, m)

            def stats_of(i, q, rows, m):
                hw = QW[q] // 2
                for c in range(2):
                    for mi in range(m):
                        k = FE0[i] + (2 * q + c) * m + mi
                        dve.wait_ge(s["fe_evac"], k + 1)
                        n = min(hw, N - QCOL[q] - c * hw)
                        v.bn_stats(bnst[0:rows, mi, 2 * q + c, :], rst[0:rows, mi, c * hw:c * hw + n]).then_inc(s["bn_read"], 1)

            def fold(i, rows, m, F, gc, bc_, win):
                dve.wait_ge(s["bn_read"], FE0[i] + 8 * m)
                for mi in range(m):
                    ins = v.bn_aggr(mv[0:rows, mi, :], bnst[0:rows, mi, :, :].rearrange("p a b -> p (a b)"))
                step(ins)
                step(v.tensor_scalar(mv[0:rows, 0:m, 1], mv[0:rows, 0:m, 1], EPS, None, ALU.add))
                sqrt_of(mv[0:rows, 0:m, 1], m, rows)
                step(v.reciprocal(sq[0:rows, 0:m], sq[0:rows, 0:m]))
                step(v.tensor_tensor(sq[0:rows, 0:m], sq[0:rows, 0:m], gc, ALU.mult))
                step(v.tensor_tensor(sq[0:rows, m:2 * m], sq[0:rows, 0:m], mv[0:rows, 0:m, 0], ALU.mult))
                step(v.tensor_tensor(sq[0:rows, 2 * m:3 * m], bc_, sq[0:rows, m:2 * m], ALU.subtract))
                step(v.memset(Hf[0:rows, 0:m * P], 1.0))
                for mi in range(m):
                    ins = v.tensor_scalar(Hf[0:rows, mi * P:(mi + 1) * P], Hf[0:rows, mi * P:(mi + 1) * P], sq[0:rows, 2 * m + mi:2 * m + mi + 1], None, ALU.mult)
                dve.wait_ge(s[win], 16 if i == 1 else 64)
                ins.then_inc(s["fold_t"], 1)
                dve.wait_ge(s["fold_mm"], i)
                v.tensor_copy(wreg[:, m * F:(m + 1) * F], ps[:, 4, 0:F])
                for mi in range(m):
                    ins = v.tensor_scalar(wreg[0:rows, mi * F:(mi + 1) * F], wreg[0:rows, mi * F:(mi + 1) * F], sq[0:rows, mi:mi + 1], None, ALU.mult)
                ins.then_inc(s["fold_w"], 1)
                dve.wait_ge(s["fold_w"], i)
                dve.wait_ge(s["r_stored"], 64 * i)
                dst = bigC3 if F == C3 else hA
                for t in range(NT):
                    dve.wait_ge(s["cv_done"], NT * (i - 1) + t + 1)
                    v.tensor_tensor(dst[:, t, :], ps[:, 4 + t % 4, 0:F], wreg[:, m * F:(m + 1) * F], ALU.add).then_inc(s["cv_evac"], 1)
                dve.wait_ge(s["cv_evac"], NT * i)

            feature_conv(1, R2, M2)
            fold(1, R2, M2, C3, col("g1", R2), col("be1", R2), "w2_in")
            split(bigC3, H3, dinv)
            step(v.memset(wreg[:, 720:720 + 432], 0.0))
            for gi in range(3):
                ins = v.tensor_copy(wreg[:, 720 + 192 * gi:720 + 192 * gi + C], comb[:, :])
            ins.then_inc(s["w1_ready"], 1)
            step(v.memset(Sflat[:, :], 0.0))
            feature_conv(2, R3, M3)
            out_degree(NT - 1)
            fold(2, R3, M3, C, col("g2", R3), col("be2", R3), "w3_in")
            split(hA, H1, dinv)
            step(v.memset(wreg[:, 288:416], 1.0))
            v.memset(Sflat[:, :], 0.0).then_inc(s["w1_ready"], 1)

            def node_quarters(i, fn):
                for q in range(4):
                    k = 4 * NODE_ORDER[i] + q
                    dve.wait_ge(s["nq_done"], k + 1)
                    n, t0 = QT[q], 6 * q
                    fn(ps[:, 4 + q % 2, 0:n * C].rearrange("p (t f) -> p t f", f=C), t0, n)
                    dve.sem_inc(s["nq_evac"], 1)

            def out_conv(p_, t0, n):
                step(v.tensor_tensor(hY[:, t0:t0 + n, :], p_, bc(dinv[:, t0:t0 + n].unsqueeze(2), [P, n, C]), ALU.mult))
                step(v.tensor_tensor(hY[:, t0:t0 + n, :], hY[:, t0:t0 + n, :], bc(wreg[:, C3:C3 + C].unsqueeze(1), [P, n, C]), ALU.add))

            node_quarters(3, out_conv)
            dve.wait_ge(s["ident_in"], 16)
            diagonal(ALU.subtract).then_inc(s["adj_noi"], 1)
            bn_nodes(1, hY, C, wreg[:, C3 + C:C3 + 2 * C], wreg[:, C3 + 2 * C:C3 + 3 * C])
            step(v.scalar_tensor_tensor(X[:, :, :], hY, 0.0, X[:, :, :], ALU.max, ALU.add))
            layernorm(hA, hT)
            split(hA, H1, rest=hT)
            dve.wait_ge(s["w4_in"], 128)
            step(v.tensor_scalar(wreg[0:C2P, C:2 * C], wreg[0:C2P, C:2 * C], half[0:C2P, 0:1], None, ALU.mult))
            step(v.tensor_scalar(wreg[0:C2P, 4 * C:5 * C], wreg[0:C2P, 4 * C:5 * C], half[0:C2P, 0:1], None, ALU.mult))
            step(v.tensor_copy(wreg[:, 288:416], ident16))
            dve.sem_inc(s["w1_ready"], 1)

            def self_term(layer, bB):
                for j in range(7):
                    k = 7 * layer + j
                    n = min(4, NT - 4 * j)
                    dve.wait_ge(s["tr_done"], k + 1)
                    v.tensor_copy(turned(k)[:, 0:n * P], ps[0:C, 4 + k % 2, 0:n * P]).then_inc(s["tr_evac"], 1)
                    dve.wait_ge(s["self_done"], k + 1)
                    v.tensor_tensor(hY[:, 4 * j:4 * j + n, :], ps[:, 6 + k % 2, 0:n * C].rearrange("p (t f) -> p t f", f=C),
                                    bc(bB.unsqueeze(1), [P, n, C]), ALU.add).then_inc(s["self_evac"], 1)
                dve.wait_ge(s["self_evac"], 7 * layer + 7)

            def sage(dst, relu):
                def fn(p_, t0, n):
                    a = hT[:, t0:t0 + n, :]
                    step(v.tensor_tensor(a, p_, bc(rdeg[:, t0:t0 + n].unsqueeze(2), [P, n, C]), ALU.mult))
                    step(v.tensor_tensor(a, a, hY[:, t0:t0 + n, :], ALU.add))
                    if relu:
                        step(v.tensor_scalar(dst[:, t0:t0 + n, :], a, 0.0, None, ALU.max))
                    else:
                        step(v.tensor_tensor(dst[:, t0:t0 + n, :], dst[:, t0:t0 + n, :], a, ALU.add))
                return fn

            self_term(0, wreg[:, 2 * C:3 * C])
            node_quarters(4, sage(hA, True))
            split(hA, H1, rest=hT)
            step(v.tensor_scalar(stat[:, 1, :], rtot[:, :], 1.0, None, ALU.max))
            sqrt_of(stat[:, 1, :], NT)
            step(v.reciprocal(dinv[:, :], sq[:, 0:NT]))
            self_term(1, wreg[:, 5 * C:6 * C])

            def sage_end(p_, t0, n):
                sage(X, False)(p_, t0, n)
                layernorm(hA, hT, tiles=(t0, t0 + n))

            node_quarters(5, sage_end)
            split(hA, H1, dinv)
            for k, (x, ys) in enumerate(FLIPS):
                dve.wait_ge(s["flip_done"], k + 1)
                ys = [y for y in ys if y != x]
                if not ys:
                    continue
                n, wx = len(ys), min(P, NC - P * x)
                src_ = ps[:, 4 + k % 4, 0:n * 64].bitcast(F16).rearrange("p (j c) -> p j c", j=n)[:, :, 0:wx]
                v.tensor_copy(adj[:, ys[0]:ys[0] + n, P * x:P * x + wx], src_).then_inc(s["flip_cols"], 1)
            dve.wait_ge(s["flip_cols"], FLIP_COLS[-1])
            dve.wait_ge(s["flip_evac"], len(FLIPS))
            diagonal(ALU.add).then_inc(s["adj_t"], 1)

            def light(dst, add):
                def fn(p_, t0, n):
                    a = hT[:, t0:t0 + n, :]
                    step(v.tensor_tensor(a, p_, bc(dinv[:, t0:t0 + n].unsqueeze(2), [P, n, C]), ALU.mult))
                    if add:
                        step(v.tensor_tensor(dst[:, t0:t0 + n, :], dst[:, t0:t0 + n, :], a, ALU.add))
                    else:
                        step(v.tensor_copy(dst[:, t0:t0 + n, :], a))
                return fn

            node_quarters(6, light(hA, False))
            split(hA, H1, dinv)
            dve.wait_ge(s["late_in"], 48)
            cutoff(lcw, *cw_t, 3)
            step(v.tensor_copy(lsrc, lsrc_i))
            step(v.tensor_scalar(lsrc, lsrc, float(-(NC // 2)), None, ALU.add))
            step(v.scalar_tensor_tensor(combA, wreg[0:2 * CA, 288 + CA:288 + 2 * CA], 1.0 / LOW, wreg[0:2 * CA, 288:288 + CA], ALU.mult, ALU.add))

            def light_end(p_, t0, n):
                light(X, True)(p_, t0, n)
                layernorm(hA, hT, tiles=(t0, t0 + n))
                v.tensor_tensor(hT[:, t0:t0 + n, :], hA[:, t0:t0 + n, :], bc(nvec[:, t0:t0 + n].unsqueeze(2), [P, n, C]), ALU.mult).then_inc(s["hv_ready"], 1)

            node_quarters(7, light_end)
            dve.wait_ge(s["consts"], 5)
            v.memset(aggS[0:2 * CA, NC:NP], 0.0)
            dve.sem_inc(s["l_msg"], 2)
            dve.sem_inc(s["l_res"], 2)

            base = step.n

            def message(b, par):
                dve.wait_ge(s[f"l_in{par}"], (b - par) * 16 + 32)
                dve.wait_ge(s[f"l_got{par}"], (b - par) * 32 + 64)
                n0 = b * 4 + base
                v.tensor_tensor(ldot[:, par, :, :], le[:, par, :, :], lh[:, par, :, C:C + GD], ALU.mult).then_inc(s["dve_step"], 1)
                dve.wait_ge(s["l_mm"], b + 1)
                v.tensor_scalar(ohn[:, par, 0, :], iota_n, lsrc[:, bass.ds(b * 4, 1)], None, ALU.is_equal)
                dve.wait_ge(s["dve_step"], n0 + 1)
                v.tensor_reduce(la[:, par, :], ldot[:, par, :, :], AX, ALU.add).then_inc(s["dve_step"], 1)
                v.tensor_scalar(ohn[:, par, 1, :], iota_n, lsrc[:, bass.ds(b * 4 + 1, 1)], None, ALU.is_equal)
                dve.wait_ge(s["dve_step"], n0 + 2)
                v.tensor_tensor(la[:, par, :], la[:, par, :], lcw[:, bass.ds(b * 4, 4)], ALU.mult).then_inc(s["dve_step"], 1)
                dve.wait_ge(s["dve_step"], n0 + 3)
                v.tensor_tensor(lm[:, par, :, :], lg[:, par, :, :], bc(la[:, par, :].unsqueeze(2), [P, 4, C]), ALU.add).then_inc(s["dve_step"], 1)
                dve.wait_ge(s["dve_step"], n0 + 4)
                v.tensor_tensor(lm[:, par, :, :], lm[:, par, :, :], lh[:, par, :, 0:C], ALU.mult).then_inc(s["l_msg"], 1)
                v.tensor_scalar(ohn[:, par, 2, :], iota_n, lsrc[:, bass.ds(b * 4 + 2, 1)], None, ALU.is_equal)
                dve.wait_ge(s["l_hi"], b + 3)
                v.tensor_tensor(lm[:, par, :, :], lm[:, par, :, :], lmh[:, par, :, 0, 0:C], ALU.subtract).then_inc(s["l_res"], 1)
                v.tensor_scalar(ohn[:, par, 3, :], iota_n, lsrc[:, bass.ds(b * 4 + 3, 1)], None, ALU.is_equal).then_inc(s["l_oh"], 1)

            with dve.Fori(0, NB // 2) as i:
                message(i * 2, 0)
                message(i * 2 + 1, 1)
            step.n = base + 4 * NB
            dve.wait_ge(s["w6_in"], 32)
            for j, (t0, t1, bank) in enumerate(ENDS):
                n = t1 - t0
                dve.wait_ge(s["agg_mm"], j + 1)
                agg = ps[:, bank, 0:n * CA].rearrange("p (t f) -> p t f", f=CA)
                tot, x_, y_ = rtot[:, t0:t1], hT[:, t0:t1, :], hY[:, t0:t1, :]
                step(v.tensor_scalar(tot, agg[:, :, C], 1e-8, None, ALU.max))
                step(v.reciprocal(tot, tot))
                step(v.tensor_tensor(x_, agg[:, :, 0:C], bc(tot.unsqueeze(2), [P, n, C]), ALU.mult))
                step(v.tensor_tensor(x_, x_, hA[:, t0:t1, :], ALU.add))
                layernorm(hY, hA, positive=False, src=hT, tiles=(t0, t1))
                step(v.tensor_tensor(y_, y_, bc(wreg[:, 512:512 + C].unsqueeze(1), [P, n, C]), ALU.mult))
                step(v.tensor_tensor(y_, y_, bc(wreg[:, 512 + C:512 + 2 * C].unsqueeze(1), [P, n, C]), ALU.add))
                v.tensor_tensor(X[:, t0:t1, :], X[:, t0:t1, :], y_, ALU.add).then_inc(s["out_ready"], 1)

        @block.scalar
        def _(act):
            a = nc.scalar
            act.sem_inc(s["silu_done"], 2)
            act.sem_inc(s["win_evac"], 2)
            for o, i in small[11:]:
                act.dma_start(o, i).then_inc(s["in_small"], 16)
            act.wait_ge(s["t_r"], 1)
            a.activation(tw[:, 4:5], tw[:, 2:3], ACT.Sin).then_inc(s["t_emb"], 1)
            act.wait_ge(s["cw_ready"], 1)
            a.activation(Sflat[:, NCHUNK:2 * NCHUNK], Sflat[:, NCHUNK:2 * NCHUNK], ACT.Sin).then_inc(s["t_emb"], 1)
            act.wait_ge(s["padz"], 1)
            act.wait_ge(s["tn_stored"], 32)

            def evac_window(w, par):
                act.wait_ge(s["win_done"], w + 3)
                a.activation(adj[:, :, bass.ds(w * WIN, WIN)], ps[:, par, 0:NT * WIN].rearrange("p (s x) -> p s x", x=WIN),
                             ACT.Copy).then_inc(s["win_evac"], 1)

            def gate_silu(b, par):
                act.wait_ge(s["z_done"], b + 1)
                act.wait_ge(s["gate_done"], b + 1)
                a.activation(silu[0:C, par, :], ps[0:C, 2 + par, :], ACT.Silu, bias=b1c).then_inc(s["silu_done"], 1)

            def four_windows(i):
                gate_silu(i * 2, 0)
                evac_window(i * 4, 0)
                evac_window(i * 4 + 1, 1)
                gate_silu(i * 2 + 1, 1)
                evac_window(i * 4 + 2, 0)
                evac_window(i * 4 + 3, 1)

            act.sem_inc(s["deg_row"], 1)
            with act.Fori(0, SC) as i:
                four_windows(i)
            with act.Fori(1, SC) as c:
                for j in range(SC):
                    four_windows(c * SC + j)
                act.wait_ge(s["deg_mm"], c + 0)
                a.activation(degrow[:, bass.ds((c - 1) * SCW, SCW)], ps[0:1, 6, 0:SCW], ACT.Copy).then_inc(s["deg_row"], 1)
            gate_silu(NB - 6, 0)
            gate_silu(NB - 5, 1)
            act.wait_ge(s["deg_mm"], SC)
            a.activation(degrow_end, ps[0:1, 6, 0:SCW], ACT.Copy).then_inc(s["deg_row"], 1)
            nsq = [0]

            def sqrt_served(n, rows=P):
                nsq[0] += 1
                act.wait_ge(s["var_ready"], nsq[0])
                a.activation(sq[0:rows, 0:n], sq[0:rows, 0:n], ACT.Sqrt).then_inc(s["std_ready"], 1)

            sqrt_served(NT)
            for b in range(NB - 4, NB):
                gate_silu(b, b % 2)
            nsplit = [0]

            def split(val, hview, rest=None):
                k = nsplit[0]
                nsplit[0] += NPART
                rest = val if rest is None else rest

                def high(n):
                    if n == NPART:
                        return
                    a_, b_ = PARTS[n]
                    act.wait_ge(s["h_scaled"], k + n + 1)
                    a.activation(hview[:, a_:b_, :, 0, :], val[:, a_:b_, :].rearrange("p t (g f) -> p t g f", f=C), ACT.Copy).then_inc(s["h_hi"], 1)

                high(0)
                for n, (a_, b_) in enumerate(PARTS):
                    high(n + 1)
                    act.wait_ge(s["h_res"], k + n + 1)
                    a.activation(hview[:, a_:b_, :, 1, :], rest[:, a_:b_, :].rearrange("p t (g f) -> p t g f", f=C), ACT.Copy, scale=LOW).then_inc(s["h_ready"], 1)

            def evac_quarters(i, serve=None):
                for q in range(4):
                    u = UNIT0[i] + q
                    act.wait_ge(s["spmm_done"], u + 1)
                    if q >= 2:
                        quarter_used(act, i, q - 2)
                    bank, hw = 2 * (u % 2), QW[q] // 2
                    a.activation(S[0:C2P, q % 2, 0:QW[q]].rearrange("p (c w) -> p c w", c=2), ps[0:C2P, bank:bank + 2, 0:hw],
                                 ACT.Copy).then_inc(s["spmm_evac"], 1)
                    if serve and q:
                        serve(QT[q - 1])

            def bn_square(k, val, out_sq):
                for n, (a_, b_) in enumerate(PARTS):
                    act.wait_ge(s["bn_cent"], NPART * k + n + 1)
                    a.activation(out_sq[:, a_:b_, :], val[:, a_:b_, :], ACT.Square).then_inc(s["bn_sq"], 1)
                sqrt_served(val.shape[2])

            def relu_blocks(i, rows, m, bias):
                for q in range(4):
                    hw = QW[q] // 2
                    if q or i > 1:
                        act.wait_ge(s["r_stored"], 16 * (4 * (i - 1) + q))
                        act.wait_ge(s["bn_read"], FE0[i] + 2 * m * q)
                    for c in range(2):
                        for mi in range(m):
                            k = FE0[i] + (2 * q + c) * m + mi
                            act.wait_ge(s["fe_done"], k + 1)
                            a.activation(rst[0:rows, mi, c * hw:(c + 1) * hw], ps[0:rows, 4 + k % 4, 0:hw], ACT.Relu,
                                         bias=bias[0:rows, mi:mi + 1]).then_inc(s["fe_evac"], 1)

            sqrt_served(NT)
            split(hA, H1)
            act.wait_ge(s["padz"], 1)
            evac_quarters(0)
            bn_square(0, bigC3, HfC3)
            split(bigC3, H3)
            act.wait_ge(s["bias_ready"], 1)
            relu_blocks(1, R2, M2, bias2)
            sqrt_served(M2, R2)
            split(bigC3, H3)
            relu_blocks(2, R3, M3, bias3)
            sqrt_served(M3, R3)
            split(hA, H1)
            act.wait_ge(s["w1_ready"], 4)
            evac_quarters(3)
            bn_square(1, hY, Hf1)
            sqrt_served(NT)
            split(hA, H1, hT)
            evac_quarters(4)
            split(hA, H1, hT)
            sqrt_served(NT)
            evac_quarters(5, sqrt_served)
            sqrt_served(QT[3])
            split(hA, H1)
            for k, (x, ys) in enumerate(FLIPS):
                act.wait_ge(s["flip_done"], k + 1)
                wx = min(P, NC - P * x)
                w = min(P * len(ys), NC - P * ys[0])
                a.activation(adj[0:wx, x, P * ys[0]:P * ys[0] + w], ps[0:wx, k % 4, 0:256].bitcast(F16)[:, 0:w],
                             ACT.Copy).then_inc(s["flip_evac"], 1)
            evac_quarters(6)
            split(hA, H1)
            act.wait_ge(s["cw_ready"], 2)
            a.activation(cw_t[1], cw_t[1], ACT.Sin).then_inc(s["t_emb"], 1)
            evac_quarters(7, sqrt_served)
            sqrt_served(QT[3])

            act.sem_inc(s["l_hi"], 2)

            def parts(b, par):
                act.wait_ge(s["l_msg"], b + 3)
                act.wait_ge(s["l_mm"], b + 1)
                a.activation(lmh[:, par, :, :, C], lh[:, par, :, C + GD:HROW], ACT.Copy)
                a.activation(lmh[:, par, :, 0, 0:C], lm[:, par, :, :], ACT.Copy).then_inc(s["l_hi"], 1)
                act.wait_ge(s["l_res"], b + 3)
                a.activation(lmh[:, par, :, 1, 0:C], lm[:, par, :, :], ACT.Copy, scale=LOW).then_inc(s["l_lo"], 1)

            with act.Fori(0, NB // 2) as i:
                parts(i * 2, 0)
                parts(i * 2 + 1, 1)
            act.wait_ge(s["l_mm"], NB + 2)
            for c in range(SC):
                a.activation(aggS[0:2 * CA, c * SCW:(c + 1) * SCW], ps[0:2 * CA, c, 0:SCW], ACT.Copy).then_inc(s["agg_evac"], 1)
            for t0, t1, _bank in ENDS:
                sqrt_served(t1 - t0)

        @block.tensor
        def _(pe):
            mm = nc.tensor.matmul
            for nm, n in (("win_done", 2), ("gate_done", 2), ("l_mm", 2)):
                pe.sem_inc(s[nm], n)
            pe.wait_ge(s["c0_cmp"], 4)
            pe.wait_ge(s["ones_row"], 1)
            for k in range(4):
                ins = mm(ps[0:1, 3, 0:NWIN], ones1[0:104, :], cmp_w[:, k, :], start=(k == 0), stop=(k == 3))
            ins.then_inc(s["c0_sum"], 1)
            pe.wait_ge(s["in_small"], 16 * 22)
            pe.wait_ge(s["t_emb"], 1)
            mm(ps[:, 0, 0:1], wtm, tw[:, 4:5], start=True, stop=True).then_inc(s["t_mm1"], 1)
            pe.wait_ge(s["t_rel"], 1)
            for m in range(M2):
                mm(ps[0:R2, 1, m:m + 1], wt1[:, m * R2:(m + 1) * R2], tw[:, 5:6], start=True, stop=True)
            for m in range(M3):
                ins = mm(ps[0:R3, 1, M2 + m:M2 + m + 1], wt2[:, m * R3:(m + 1) * R3], tw[:, 5:6], start=True, stop=True)
            ins.then_inc(s["t_mm2"], 1)
            mm(ps[0:NEL, 2, 0:GD], embT, adaT, start=True, stop=True).then_inc(s["tables_T"], 1)
            pe.wait_ge(s["tables_tt"], 1)
            pe.wait_ge(s["t_onehot"], 1)
            for j in range(4):
                n = min(8, NT - 8 * j)
                for t in range(8 * j, 8 * j + n):
                    ins = mm(ps[:, 4 + j, 64 * (t % 8):64 * (t % 8) + 64], onehot_t[0:NEL, P * t:P * t + P], tt12, start=True, stop=True)
                ins.then_inc(s["t_mm"], 1)
            pe.wait_ge(s["c0_ready"], 1)
            pe.wait_ge(s["bias_ready"], 1)
            pe.wait_ge(s["t_evac"], 4)

            def window(w, par):
                pe.wait_ge(s["onehots_built"], w + 4)
                pe.wait_ge(s["win_evac"], w + 1)
                for k in range(WCH):
                    ins = mm(ps[:, par, 0:NT * WIN], sta[:, par, k, :], mov[:, par, k, :], start=(k == 0), stop=(k == WCH - 1))
                ins.then_inc(s["win_done"], 1)

            def gate_hidden(b, par):
                pe.wait_ge(s[f"attr_in{par}"], (b - par) * 8 + 16)
                pe.wait_ge(s["silu_done"], b + 1)
                mm(ps[:, 2 + par, :], w1t, attr[:, par, :], start=True, stop=True).then_inc(s["z_done"], 1)

            def gate_product(b, par):
                pe.wait_ge(s["silu_done"], b + 3)
                pe.wait_ge(s["g_evac"], b + 1)
                for k in range(4):
                    ins = mm(ps[:, 4 + par, C * k:C * k + C], silu[:, par, P * k:P * k + P], w2b, start=True, stop=True)
                ins.then_inc(s["gate_done"], 1)

            def four_windows(i):
                gate_hidden(i * 2, 0)
                window(i * 4, 0)
                window(i * 4 + 1, 1)
                gate_product(i * 2, 0)
                gate_hidden(i * 2 + 1, 1)
                window(i * 4 + 2, 0)
                window(i * 4 + 3, 1)
                gate_product(i * 2 + 1, 1)

            def sum_degrees(c, ks):
                if 0 in ks:
                    pe.wait_ge(s["win_evac"], (c + 1) * (4 * SC) + 2)
                    pe.wait_ge(s["deg_row"], c + 1)
                for k in ks:
                    ins = mm(ps[0:1, 6, 0:SCW], ones16[:, 0:1], adj[:, k, bass.ds(c * SCW, SCW)], start=(k == 0), stop=(k == NT - 1))
                if NT - 1 in ks:
                    ins.then_inc(s["deg_mm"], 1)

            pe.wait_ge(s["ones_ready"], 1)
            with pe.Fori(0, SC) as i:
                four_windows(i)
            with pe.Fori(1, SC) as c:
                for j in range(SC):
                    four_windows(c * SC + j)
                    sum_degrees(c - 1, range(j * NT // SC, (j + 1) * NT // SC))

            def gates(b):
                for fn in (gate_hidden, gate_product):
                    fn(b, 0)
                    fn(b + 1, 1)

            gates(NB - 6)
            sum_degrees(SC - 1, range(NT))
            pe.wait_ge(s["deg_row"], SC + 1)
            for t in range(NT):
                wd, at = min(P, NC - P * t), P * t - 6 * SCW
                row = degrow[:, P * t:P * t + wd] if at < 0 else degrow_end[:, at:at + wd]
                ins = mm(ps[0:wd, 7, t:t + 1], row, ones16[0:1, 0:1], start=True, stop=True)
            ins.then_inc(s["deg_tr"], 1)
            gates(NB - 4)
            pe.wait_ge(s["rows_summed"], 1)
            mm(ps[0:1, 6, 0:1], ones1, rowsum, start=True, stop=True).then_inc(s["total_mm"], 1)
            gates(NB - 2)
            pe.wait_ge(s["total_ready"], 1)
            missed = pe.value_load(flag_i, min_val=0, max_val=1)
            with pe.If(missed > 0):
                pe.sem_inc(s["all_used0"], 1)
                pe.sem_inc(s["all_used1"], 1)

                def all_groups(w, g, first=False, last=False):
                    for slot in range(2):
                        pe.wait_ge(s[f"all_onehots{slot}"], w * (NB // 2) + g + 1)
                        for k in range(WCH):
                            ins = mm(ps[:, 0, 0:NT * WIN], sta[:, slot, k, :], mov[:, slot, k, :], start=(first and slot + k == 0), stop=(last and slot == 1 and k == WCH - 1))
                        ins.then_inc(s[f"all_used{slot}"], 1)

                with pe.Fori(0, NWIN) as w:
                    pe.wait_ge(s["all_evac"], w + 1)
                    all_groups(w, 0, first=True)
                    with pe.Fori(1, NB // 2 - 1) as g:
                        all_groups(w, g)
                    all_groups(w, NB // 2 - 1, last=True)
                pe.wait_ge(s["all_evac"], NWIN + 1)

                def degrees(t, wd=P):
                    for k in range(NT):
                        ins = mm(ps[0:wd, 7, bass.ds(t, 1)], adj[:, k, bass.ds(t * P, wd)], ones16[:, 0:1], start=(k == 0), stop=(k == NT - 1))
                    return ins

                with pe.Fori(0, NT - 1) as t:
                    degrees(t)
                degrees(NT - 1, NC - P * (NT - 1)).then_inc(s["all_deg"], 1)
            pe.wait_ge(s["adj_i"], 1)
            pe.wait_ge(s["g_evac"], NB + 2)

            def spmm(i, q, gi, hview, midway=None):
                u = UNIT0[i] + (3 * q + gi if GROUPS[i] == 3 else q)
                if u >= 2:
                    pe.wait_ge(s["spmm_evac"], u - 1)
                bank, hw = 2 * (u % 2), QW[q] // 2
                for t in range(NT):
                    if q == 0 and gi == 0 and t % 5 == 0:
                        pe.wait_ge(s["h_ready"], NPART * i + t // 5 + 1)
                    if t == 10 and midway is not None:
                        midway()
                    for c in range(2):
                        ins = mm(ps[0:C2P, bank + c, 0:hw], hview[:, t, gi, :, :].rearrange("p h f -> p (h f)"),
                                 adj[:, t, QCOL[q] + c * hw:QCOL[q] + (c + 1) * hw], start=(t == 0), stop=(t == NT - 1))
                ins.then_inc(s["spmm_done"], 1)
                return u

            def conv1_tiles(q):
                pe.wait_ge(s["spmm_evac"], q + 1)
                for j in range(QT[q]):
                    t = 6 * q + j
                    if t == 0:
                        pe.wait_ge(s["w1_ready"], 1)
                    if t >= 4:
                        pe.wait_ge(s["n1_evac"], t - 3)
                    ins = mm(ps[:, 4 + t % 4, 0:C3], S[0:C2P, q % 2, P * j:P * j + P], wreg[0:C2P, 0:C3], start=True, stop=True)
                    ins.then_inc(s["n1_done"], 1)

            def bn_sums(k, val, sqv, F, evac_sem, evac_n):
                pe.wait_ge(evac_sem, evac_n)
                on = wreg[:, 576:704] if k == 0 else wreg[:, 288:416]
                for part, bank in ((0, 4), (1, 5)):
                    x_ = sqv if part else val
                    for t in range(NT):
                        if part and t % 5 == 0:
                            pe.wait_ge(s["bn_sq"], NPART * k + t // 5 + 1)
                        r = P if t < NT - 1 else TAIL
                        ins = mm(ps[:, bank, 0:F], on[0:r, :], x_[0:r, t, :], start=(t == 0), stop=(t == NT - 1))
                    ins.then_inc(s["bn_mm"], 1)

            for q in range(4):
                spmm(0, q, 0, H1, (lambda: conv1_tiles(q - 1)) if q else None)
            conv1_tiles(3)
            bn_sums(0, bigC3, HfC3, C3, s["n1_evac"], NT)

            def feature_blocks(i, q, rows, m, wv):
                pe.wait_ge(s["spmm_evac"], UNIT0[i] + 3 * q + 3)
                if q == 0:
                    pe.wait_ge(s["w1_ready"], i + 1)
                hw = QW[q] // 2
                for c in range(2):
                    for mi in range(m):
                        k = FE0[i] + (2 * q + c) * m + mi
                        if k >= 4:
                            pe.wait_ge(s["fe_evac"], k - 3)
                        for gi in range(3):
                            ins = mm(ps[0:rows, 4 + k % 4, 0:hw], wv[0:C2P, gi, mi * rows:(mi + 1) * rows], S[0:C2P, gi, c * hw:(c + 1) * hw],
                                     start=(gi == 0), stop=(gi == 2))
                        ins.then_inc(s["fe_done"], 1)

            def feature_conv(i, rows, m, wv):
                for q in range(4):
                    spmm(i, q, 0, H3)
                    if q:
                        feature_blocks(i, q - 1, rows, m, wv)
                    spmm(i, q, 1, H3)
                    spmm(i, q, 2, H3)
                feature_blocks(i, 3, rows, m, wv)

            def folded(i, rows, m, F):
                pe.wait_ge(s["fold_t"], i)
                pe.wait_ge(*((s["w2_in"], 16) if i == 1 else (s["w3_in"], 64)))
                pe.wait_ge(s["fe_evac"], FE0[i] + 8 * m)
                for mi in range(m):
                    ins = mm(ps[:, 4, 0:F], Hf[0:rows, mi * P:(mi + 1) * P], wreg[0:rows, mi * F:(mi + 1) * F], start=(mi == 0), stop=(mi == m - 1))
                ins.then_inc(s["fold_mm"], 1)
                pe.wait_ge(s["fold_w"], i)
                for t in range(NT):
                    k = NT * (i - 1) + t
                    uses = 16 * ((i - 1) * len(range(t % 4, NT, 4)) + t // 4 + 1)
                    pe.wait_ge(s[f"ring{t % 4}"], uses)
                    if t >= 4:
                        pe.wait_ge(s["cv_evac"], k - 3)
                    for mi in range(m):
                        lhs = Sflat[0:rows, (t % 4) * 512 + mi * P:(t % 4) * 512 + (mi + 1) * P]
                        ins = mm(ps[:, 4 + t % 4, 0:F], lhs, wreg[0:rows, mi * F:(mi + 1) * F], start=(mi == 0), stop=(mi == m - 1))
                    ins.then_inc(s["cv_done"], 1)

            feature_conv(1, R2, M2, wreg[:, :].rearrange("p (g f) -> p g f", g=3))
            folded(1, R2, M2, C3)
            feature_conv(2, R3, M3, wreg[:, 720:1152].rearrange("p (g f) -> p g f", g=3))
            folded(2, R3, M3, C)

            def node_tiles(i, q, wv):
                k = 4 * NODE_ORDER[i] + q
                pe.wait_ge(s["spmm_evac"], UNIT0[i] + q + 1)
                if k >= 2:
                    pe.wait_ge(s["nq_evac"], k - 1)
                for j in range(QT[q]):
                    ins = mm(ps[:, 4 + q % 2, C * j:C * j + C], S[0:C2P, q % 2, P * j:P * j + P], wv, start=True, stop=True)
                ins.then_inc(s["nq_done"], 1)

            def node_conv(i, wv, meanwhile=None):
                for q in range(4):
                    spmm(i, q, 0, H1, (lambda: node_tiles(i, q - 1, wv)) if q else None)
                    if q == 0 and meanwhile is not None:
                        meanwhile()
                node_tiles(i, 3, wv)

            node_conv(3, comb[0:C2P, :])
            bn_sums(1, hY, Hf1, C, s["nq_evac"], 4)

            def self_product(layer, wv):
                if layer == 0:
                    pe.wait_ge(s["w1_ready"], 5)
                idf = wreg[:, 288:416]

                def transposes(j):
                    k = 7 * layer + j
                    if k >= 2:
                        pe.wait_ge(s["self_evac"], k - 1)
                    for t in range(4 * j, min(4 * j + 4, NT)):
                        ins = nc.tensor.transpose(ps[0:C, 4 + k % 2, P * (t % 4):P * (t % 4) + P], hA[:, t, :], idf)
                    ins.then_inc(s["tr_done"], 1)

                transposes(0)
                for j in range(7):
                    k = 7 * layer + j
                    if j < 6:
                        transposes(j + 1)
                    pe.wait_ge(s["tr_evac"], k + 1)
                    for t in range(min(4, NT - 4 * j)):
                        ins = mm(ps[:, 6 + k % 2, C * t:C * t + C], turned(k)[:, t * P:t * P + P], wv, start=True, stop=True)
                    ins.then_inc(s["self_done"], 1)

            pe.wait_ge(s["adj_noi"], 1)
            node_conv(4, wreg[0:C2P, C:2 * C], lambda: self_product(0, wreg[0:C, 0:C]))
            node_conv(5, wreg[0:C2P, 4 * C:5 * C], lambda: self_product(1, wreg[0:C, 3 * C:4 * C]))
            pe.wait_ge(s["nq_evac"], 12)
            id16 = ident16
            for k, (x, ys) in enumerate(FLIPS):
                if k >= 4:
                    pe.wait_ge(s["flip_evac"], k - 3)
                    if FLIP_COLS[k - 4]:
                        pe.wait_ge(s["flip_cols"], FLIP_COLS[k - 4])
                wx = min(P, NC - P * x)
                rows_ = ps[:, k % 4, 0:256].bitcast(F16)
                cols_ = ps[:, 4 + k % 4, 0:256].bitcast(F16)
                for j, y in enumerate(ys):
                    if y != x:
                        nc.tensor.transpose(cols_[:, P * j:P * j + P], adj[:, x, P * y:P * y + P], id16)
                    ins = nc.tensor.transpose(rows_[0:wx, P * j:P * j + P], adj[:, y, P * x:P * x + wx], id16)
                ins.then_inc(s["flip_done"], 1)
            pe.wait_ge(s["flip_evac"], len(FLIPS))
            pe.wait_ge(s["adj_t"], 1)
            node_conv(6, comb[0:C2P, :])
            node_conv(7, comb[0:C2P, :])

            def scatter(b, par, first, last):
                pe.wait_ge(s["l_oh"], b + 1)
                pe.wait_ge(s["l_lo"], b + 1)
                for k in range(4):
                    for c in range(SC):
                        ins = mm(ps[0:2 * CA, c, 0:SCW], lmh[:, par, k, :, :].rearrange("p h f -> p (h f)"), ohn[:, par, k, c * SCW:(c + 1) * SCW],
                                 start=(first and k == 0), stop=(last and k == 3))
                ins.then_inc(s["l_mm"], 1)

            pe.wait_ge(s["nq_evac"], 20)
            scatter(0, 0, True, False)
            scatter(1, 1, False, False)
            with pe.Fori(1, NB // 2 - 1) as i:
                scatter(i * 2, 0, False, False)
                scatter(i * 2 + 1, 1, False, False)
            scatter(NB - 2, 0, False, False)
            scatter(NB - 1, 1, False, True)
            for t0, t1, bank in ENDS:
                for t in range(t0, t1):
                    pe.wait_ge(s["agg_evac"], -(-min(P * (t + 1), NC) // SCW))
                    ins = mm(ps[:, bank, CA * (t - t0):CA * (t - t0) + CA], aggS[0:2 * CA, P * t:P * t + P], combA, start=True, stop=True)
                ins.then_inc(s["agg_mm"], 1)


def kernel(**x):
    import concourse.bacc as _bacc
    from concourse.bass_utils import run_bass_kernel_spmd as _run

    def arr(name):
        return np.asarray(x[name])

    def by_chunk(a, fill):
        full = np.full(EP, fill, a.dtype)
        full[:E] = a
        return np.ascontiguousarray(full.reshape(NCHUNK, P).T)

    def by_tile(a):
        full = np.zeros(NP, a.dtype)
        full[:N] = a
        return np.ascontiguousarray(full.reshape(NT, P).T)

    def by_block(a, m):
        return np.ascontiguousarray(a.reshape(m, -1).T)

    xp = np.zeros((NP, C), np.float32)
    xp[:N] = arr("x")
    types = np.zeros(NP, np.int32)
    types[:N] = arr("node_type_119")
    attr = np.zeros((RBF, EP), np.float32)
    attr[:, :E] = arr("edge_attr_40").T
    freqs = np.exp(np.arange(64, dtype=np.float32) * np.float32(-np.log(10000.0) / 63)).astype(np.float32)
    L0, L1, L3 = "L0_gnn_", "L1_gnn_", "L3_gnn_"
    ins = {
        "x": xp, "src": by_chunk(arr("src"), NP - 1), "dst": by_chunk(arr("dst"), NP - 1),
        "edge_attr": attr, "edge_weight": by_chunk(arr("edge_weight"), 0.0),
        "node_type": types, "node_vec": by_tile(arr("node_vec")),
        "freq": np.concatenate([freqs, freqs]), "timestep": arr(L0 + "timestep"),
        "Wtm": arr(L0 + "Wtm"), "btm": arr(L0 + "btm"), "W_in": arr(L0 + "W_in"), "b_in": arr(L0 + "b_in"),
        "g_in": arr(L0 + "g_in"), "be_in": arr(L0 + "be_in"), "Wt1": arr(L0 + "Wt1"), "Wt2": arr(L0 + "Wt2"),
        "Wc1": arr(L0 + "Wc1"), "Wc2": arr(L0 + "Wc2"), "W_out": arr(L0 + "W_out"), "b_out": arr(L0 + "b_out"),
        "g_out": arr(L0 + "g_out"), "be_out": arr(L0 + "be_out"),
        "W_self1": arr(L1 + "W_self1"), "W_neigh1": arr(L1 + "W_neigh1"), "sb1": arr(L1 + "b1"),
        "W_self2": arr(L1 + "W_self2"), "W_neigh2": arr(L1 + "W_neigh2"), "sb2": arr(L1 + "b2"),
        "W1T": arr(L3 + "W1").T, "b1": arr(L3 + "b1"), "W2T": arr(L3 + "W2").T, "b2": arr(L3 + "b2"),
        "emb": arr(L3 + "emb"), "embT": arr(L3 + "emb").T, "adaT": arr(L3 + "adaptW").T,
        "gamma": arr(L3 + "gamma"), "beta": arr(L3 + "beta"),
    }
    for nm in ("bc1", "bt1", "g1", "be1"):
        ins[nm] = by_block(arr(L0 + nm), M2)
    for nm in ("bc2", "bt2", "g2", "be2"):
        ins[nm] = by_block(arr(L0 + nm), M3)

    nc = _bacc.Bacc("TRN2", target_bir_lowering=False, num_devices=1)
    arrays, aps = {}, {}
    for name, a in ins.items():
        a = np.ascontiguousarray(a)
        arrays["in_" + name] = a
        aps[name] = nc.dram_tensor("in_" + name, a.shape, mybir.dt.from_np(a.dtype), kind="ExternalInput").ap()
    out = nc.dram_tensor("out_0", [N, C], F32, kind="ExternalOutput").ap()
    build(nc, aps, out)
    r = _run(nc, [arrays], core_ids=[0])
    return r.results[0]["out_0"]
```
